# Optimizing a Trainium2 kernel written in Bass

```python
import numpy as np
import jax
import jax.numpy as jnp

def _softmax(x, axis=-1):
    return jax.nn.softmax(x, axis=axis)

def _gelu(x):
    return jax.nn.gelu(x, approximate=True)

def _silu(x):
    return jax.nn.silu(x)

def _sigmoid(x):
    return jax.nn.sigmoid(x)

def _layernorm(x, axis=-1, eps=1e-05):
    m = jnp.mean(x, axis=axis, keepdims=True)
    v = jnp.var(x, axis=axis, keepdims=True)
    return (x - m) / jnp.sqrt(v + eps)

def _scatter_add(tgt, idx, src, axis=0):
    return tgt.at[idx].add(src)

def _segment_sum(src, seg, n):
    return jax.ops.segment_sum(src, seg, n)
kernel_name = 'mk_flamingo_gated_d2_seqx_r4_50079e'

def setup_inputs(seed: int=0):
    np.random.seed(seed)
    _w = jnp.asarray

    def _rec_inputs():
        import jax
        import jax.numpy as jnp
        _rk = jax.random.key(seed)
        x = -0.0002928 + 1 * jax.random.normal(jax.random.fold_in(_rk, 1), (16, 128, 256), jnp.float32)
        _lenS = 128 - jax.random.randint(jax.random.fold_in(_rk, 7), (16,), 0, max(1, 128 // 4) + 1, jnp.int32)
        _lenS2 = 128 - jax.random.randint(jax.random.fold_in(_rk, 8), (16,), 0, max(1, 128 // 4) + 1, jnp.int32)
        _ctx_1024P = jax.random.normal(jax.random.fold_in(_rk, 11), (16, 16, 256), jnp.float32)
        _ctx_1024c = jax.random.dirichlet(jax.random.fold_in(_rk, 511), 0.3 * jnp.ones((16,), jnp.float32), (16, 128))
        _ctx_1024t = jnp.einsum('bsk,bkd->bsd', _ctx_1024c, _ctx_1024P)
        _ctx_1024t = _ctx_1024t * jax.lax.rsqrt(jnp.mean(jnp.square(_ctx_1024t)) + 1e-12) * 0.953939
        ctx_1024 = -1.39393e-06 + 0.999914 * (_ctx_1024t + 0.3 * jax.random.normal(jax.random.fold_in(_rk, 611), (16, 128, 256), jnp.float32))
        fside_BxSx4_0 = jax.random.uniform(jax.random.fold_in(_rk, 12), (16, 128, 4), jnp.float32, 0.0, 0.999884)
        _g = jax.random.normal(jax.random.fold_in(_rk, 9001), (2, 2), jnp.float32)
        _g = jnp.sign(_g) * jnp.maximum(jnp.abs(_g), 1.0) + (_g == 0) * 1.0
        g_xattn = _g[0]
        g_ffn = _g[1]
        return (x, ctx_1024, fside_BxSx4_0, g_xattn, g_ffn)
    x, ctx_1024, fside_BxSx4_0, g_xattn, g_ffn = _rec_inputs()

    def _L0_xattn_setup():
        import jax, jax.numpy as jnp
        import numpy as np
        D_MODEL = 256
        H = 16
        D_K = 64
        D_V = 64
        D_G = D_MODEL // H
        WAVE_LEN = 1000.0
        B = 8
        N = 128

        def box_relational_embedding(boxes, dim_g=D_G):
            x_min, y_min, x_max, y_max = jnp.split(boxes, 4, axis=-1)
            cx = (x_min + x_max) * 0.5
            cy = (y_min + y_max) * 0.5
            w = x_max - x_min + 1.0
            h = y_max - y_min + 1.0
            delta_x = jnp.log(jnp.clip(jnp.abs((cx - jnp.swapaxes(cx, 1, 2)) / w), 0.001, None))
            delta_y = jnp.log(jnp.clip(jnp.abs((cy - jnp.swapaxes(cy, 1, 2)) / h), 0.001, None))
            delta_w = jnp.log(w / jnp.swapaxes(w, 1, 2))
            delta_h = jnp.log(h / jnp.swapaxes(h, 1, 2))
            pos = jnp.stack([delta_x, delta_y, delta_w, delta_h], axis=-1)
            n_freq = dim_g // 8
            feat_range = jnp.arange(n_freq, dtype=jnp.float32)
            dim_mat = 1.0 / WAVE_LEN ** (feat_range / n_freq)
            mul = (100.0 * pos)[..., None] * dim_mat
            b, n = (pos.shape[0], pos.shape[1])
            mul = mul.reshape(b, n, n, 4 * n_freq)
            return jnp.concatenate([jnp.sin(mul), jnp.cos(mul)], axis=-1)
        key = jax.random.key(seed)
        ks = jax.random.split(key, 12)
        s = 0.02
        inp = {'queries': jax.random.normal(ks[0], (B, N, D_MODEL), jnp.float32), 'keys': jax.random.normal(ks[1], (B, N, D_MODEL), jnp.float32), 'values': jax.random.normal(ks[2], (B, N, D_MODEL), jnp.float32), 'boxes': jax.random.uniform(ks[3], (B, N, 4), jnp.float32), 'Wq': jax.random.normal(ks[4], (H * D_K, D_MODEL), jnp.float32) * s, 'bq': jnp.zeros((H * D_K,), jnp.float32), 'Wk': jax.random.normal(ks[5], (H * D_K, D_MODEL), jnp.float32) * s, 'bk': jnp.zeros((H * D_K,), jnp.float32), 'Wv': jax.random.normal(ks[6], (H * D_V, D_MODEL), jnp.float32) * s, 'bv': jnp.zeros((H * D_V,), jnp.float32), 'Wo': jax.random.normal(ks[7], (D_MODEL, H * D_V), jnp.float32) * s, 'bo': jnp.zeros((D_MODEL,), jnp.float32), 'Wg': jax.random.normal(ks[8], (H, D_G), jnp.float32) * s, 'bg': jnp.zeros((H,), jnp.float32)}
        return inp
    _L0_xattn_all = _L0_xattn_setup()
    _L0_xattn_in = {k: v for k, v in _L0_xattn_all.items() if k in ('Wq', 'bq', 'Wk', 'bk', 'Wv', 'bv', 'Wo', 'bo', 'Wg', 'bg')}
    del _L0_xattn_all

    def _L0_ffn_setup():
        import jax, jax.numpy as jnp
        import numpy as np

        def _bitlinear(x, w_latent):
            scale = jax.lax.stop_gradient(jnp.clip(jnp.mean(jnp.abs(w_latent), axis=1, keepdims=True), 1e-05, None))
            tern = jnp.clip(jnp.round(w_latent / scale), -1.0, 1.0)
            w = w_latent + jax.lax.stop_gradient(tern - w_latent)
            return x @ (w * scale).T
        key = jax.random.key(seed)
        ks = jax.random.split(key, 6)
        dim, hidden, rank = (256, 1024, 16)
        B, S = (4, 1024)
        x = jax.random.normal(ks[0], (B, S, dim), dtype=jnp.float32)
        w_fc = 0.02 * jax.random.normal(ks[1], (hidden, dim), dtype=jnp.float32)
        w_proj = 0.02 * jax.random.normal(ks[2], (dim, hidden), dtype=jnp.float32)
        u = 0.02 * jax.random.normal(ks[3], (hidden, rank), dtype=jnp.float32)
        v = 0.02 * jax.random.normal(ks[4], (rank, dim), dtype=jnp.float32)
        fast_b = jax.random.normal(ks[5], (rank, rank), dtype=jnp.float32)
        gate = jnp.float32(0.05)
        return {'x': x, 'fast_b': fast_b, 'w_fc': w_fc, 'w_proj': w_proj, 'u': u, 'v': v, 'gate': gate}
    _L0_ffn_all = _L0_ffn_setup()
    _L0_ffn_in = {k: v for k, v in _L0_ffn_all.items() if k in ('fast_b', 'w_fc', 'w_proj', 'u', 'v', 'gate')}
    del _L0_ffn_all

    def _L1_xattn_setup():
        import jax, jax.numpy as jnp
        import numpy as np
        HEADS = 16
        EPS = 1e-06

        def _rmsnorm(x, gamma):
            inv = jax.lax.rsqrt(jnp.mean(x * x, axis=-1, keepdims=True) + EPS)
            return x * inv * gamma
        key = jax.random.key(seed)
        ks = jax.random.split(key, 7)
        B, L, Lc, D, CTX = (4, 1024, 256, 256, 256)
        hd = D // HEADS
        s = 1.0 / np.sqrt(D)
        return {'x': jax.random.normal(ks[0], (B, L, D), jnp.float32), 'ctx': jax.random.normal(ks[1], (B, Lc, CTX), jnp.float32), 'Wq': jax.random.normal(ks[2], (D, D), jnp.float32) * s, 'Wkv': jax.random.normal(ks[3], (CTX, 2 * D), jnp.float32) * s, 'Wproj': jax.random.normal(ks[4], (D, D), jnp.float32) * s, 'q_gamma': jnp.ones((hd,), jnp.float32), 'k_gamma': jnp.ones((hd,), jnp.float32)}
    _L1_xattn_all = _L1_xattn_setup()
    _L1_xattn_in = {k: v for k, v in _L1_xattn_all.items() if k in ('Wq', 'Wkv', 'Wproj', 'q_gamma', 'k_gamma')}
    del _L1_xattn_all

    def _L1_ffn_setup():
        import jax, jax.numpy as jnp
        import numpy as np
        B, S, D, F, E, K = (4, 512, 256, 1024, 8, 2)
        key = jax.random.key(seed)
        ks = jax.random.split(key, 8)
        x = jax.random.normal(ks[0], (B, S, D), dtype=jnp.float32)
        router_w = jax.random.normal(ks[1], (E, D), dtype=jnp.float32) * 0.02
        w1_w = jax.random.normal(ks[2], (E, F, D), dtype=jnp.float32) * 0.02
        w1_b = jax.random.normal(ks[3], (E, F), dtype=jnp.float32) * 0.02
        w2_w = jax.random.normal(ks[4], (E, D, F), dtype=jnp.float32) * 0.02
        w2_b = jax.random.normal(ks[5], (E, D), dtype=jnp.float32) * 0.02
        wg_w = jax.random.normal(ks[6], (E, F, D), dtype=jnp.float32) * 0.02
        wg_b = jax.random.normal(ks[7], (E, F), dtype=jnp.float32) * 0.02
        return {'x': x, 'router_w': router_w, 'w1_w': w1_w, 'w1_b': w1_b, 'w2_w': w2_w, 'w2_b': w2_b, 'wg_w': wg_w, 'wg_b': wg_b}
    _L1_ffn_all = _L1_ffn_setup()
    _L1_ffn_in = {k: v for k, v in _L1_ffn_all.items() if k in ('router_w', 'w1_w', 'w1_b', 'w2_w', 'w2_b', 'wg_w', 'wg_b')}
    del _L1_ffn_all
    return {'x': x, 'ctx_1024': ctx_1024, 'fside_BxSx4_0': fside_BxSx4_0, 'g_xattn': g_xattn, 'g_ffn': g_ffn, 'L0_xattn_Wq': _L0_xattn_in['Wq'], 'L0_xattn_bq': _L0_xattn_in['bq'], 'L0_xattn_Wk': _L0_xattn_in['Wk'], 'L0_xattn_bk': _L0_xattn_in['bk'], 'L0_xattn_Wv': _L0_xattn_in['Wv'], 'L0_xattn_bv': _L0_xattn_in['bv'], 'L0_xattn_Wo': _L0_xattn_in['Wo'], 'L0_xattn_bo': _L0_xattn_in['bo'], 'L0_xattn_Wg': _L0_xattn_in['Wg'], 'L0_xattn_bg': _L0_xattn_in['bg'], 'L0_ffn_fast_b': _L0_ffn_in['fast_b'], 'L0_ffn_w_fc': _L0_ffn_in['w_fc'], 'L0_ffn_w_proj': _L0_ffn_in['w_proj'], 'L0_ffn_u': _L0_ffn_in['u'], 'L0_ffn_v': _L0_ffn_in['v'], 'L0_ffn_gate': _L0_ffn_in['gate'], 'L1_xattn_Wq': _L1_xattn_in['Wq'], 'L1_xattn_Wkv': _L1_xattn_in['Wkv'], 'L1_xattn_Wproj': _L1_xattn_in['Wproj'], 'L1_xattn_q_gamma': _L1_xattn_in['q_gamma'], 'L1_xattn_k_gamma': _L1_xattn_in['k_gamma'], 'L1_ffn_router_w': _L1_ffn_in['router_w'], 'L1_ffn_w1_w': _L1_ffn_in['w1_w'], 'L1_ffn_w1_b': _L1_ffn_in['w1_b'], 'L1_ffn_w2_w': _L1_ffn_in['w2_w'], 'L1_ffn_w2_b': _L1_ffn_in['w2_b'], 'L1_ffn_wg_w': _L1_ffn_in['wg_w'], 'L1_ffn_wg_b': _L1_ffn_in['wg_b']}

def reference(x, ctx_1024, fside_BxSx4_0, g_xattn, g_ffn, L0_xattn_Wq, L0_xattn_bq, L0_xattn_Wk, L0_xattn_bk, L0_xattn_Wv, L0_xattn_bv, L0_xattn_Wo, L0_xattn_bo, L0_xattn_Wg, L0_xattn_bg, L0_ffn_fast_b, L0_ffn_w_fc, L0_ffn_w_proj, L0_ffn_u, L0_ffn_v, L0_ffn_gate, L1_xattn_Wq, L1_xattn_Wkv, L1_xattn_Wproj, L1_xattn_q_gamma, L1_xattn_k_gamma, L1_ffn_router_w, L1_ffn_w1_w, L1_ffn_w1_b, L1_ffn_w2_w, L1_ffn_w2_b, L1_ffn_wg_w, L1_ffn_wg_b):
    import jax
    import jax.numpy as jnp

    def _L0_xattn_ref(queries, keys, values, boxes, Wq, bq, Wk, bk, Wv, bv, Wo, bo, Wg, bg):
        import jax, jax.numpy as jnp
        import numpy as np
        D_MODEL = 256
        H = 16
        D_K = 64
        D_V = 64
        D_G = D_MODEL // H
        WAVE_LEN = 1000.0
        B = 8
        N = 128

        def box_relational_embedding(boxes, dim_g=D_G):
            x_min, y_min, x_max, y_max = jnp.split(boxes, 4, axis=-1)
            cx = (x_min + x_max) * 0.5
            cy = (y_min + y_max) * 0.5
            w = x_max - x_min + 1.0
            h = y_max - y_min + 1.0
            delta_x = jnp.log(jnp.clip(jnp.abs((cx - jnp.swapaxes(cx, 1, 2)) / w), 0.001, None))
            delta_y = jnp.log(jnp.clip(jnp.abs((cy - jnp.swapaxes(cy, 1, 2)) / h), 0.001, None))
            delta_w = jnp.log(w / jnp.swapaxes(w, 1, 2))
            delta_h = jnp.log(h / jnp.swapaxes(h, 1, 2))
            pos = jnp.stack([delta_x, delta_y, delta_w, delta_h], axis=-1)
            n_freq = dim_g // 8
            feat_range = jnp.arange(n_freq, dtype=jnp.float32)
            dim_mat = 1.0 / WAVE_LEN ** (feat_range / n_freq)
            mul = (100.0 * pos)[..., None] * dim_mat
            b, n = (pos.shape[0], pos.shape[1])
            mul = mul.reshape(b, n, n, 4 * n_freq)
            return jnp.concatenate([jnp.sin(mul), jnp.cos(mul)], axis=-1)
        b, nq, _ = queries.shape
        nk = keys.shape[1]
        emb = box_relational_embedding(boxes)
        g = jax.nn.relu(jnp.einsum('bnmd,hd->bhnm', emb, Wg) + bg[None, :, None, None])
        q = (queries @ Wq.T + bq).reshape(b, nq, H, D_K).transpose(0, 2, 1, 3)
        k = (keys @ Wk.T + bk).reshape(b, nk, H, D_K).transpose(0, 2, 1, 3)
        v = (values @ Wv.T + bv).reshape(b, nk, H, D_V).transpose(0, 2, 1, 3)
        a = jnp.einsum('bhqd,bhkd->bhqk', q, k) / jnp.sqrt(jnp.float32(D_K))
        mn = jax.nn.softmax(jnp.log(jnp.clip(g, 1e-06, None)) + a, axis=-1)
        out = jnp.einsum('bhqk,bhkd->bqhd', mn, v).reshape(b, nq, H * D_V)
        return out @ Wo.T + bo

    def _L0_ffn_ref(x, fast_b, w_fc, w_proj, u, v, gate):
        import jax, jax.numpy as jnp
        import numpy as np

        def _bitlinear(x, w_latent):
            scale = jax.lax.stop_gradient(jnp.clip(jnp.mean(jnp.abs(w_latent), axis=1, keepdims=True), 1e-05, None))
            tern = jnp.clip(jnp.round(w_latent / scale), -1.0, 1.0)
            w = w_latent + jax.lax.stop_gradient(tern - w_latent)
            return x @ (w * scale).T
        h = _bitlinear(x, w_fc) + gate * (x @ v.T @ fast_b.T @ u.T)
        r = jnp.maximum(h, 0.0)
        return _bitlinear(r * r, w_proj)

    def _L1_xattn_ref(x, ctx, Wq, Wkv, Wproj, q_gamma, k_gamma):
        import jax, jax.numpy as jnp
        import numpy as np
        HEADS = 16
        EPS = 1e-06

        def _rmsnorm(x, gamma):
            inv = jax.lax.rsqrt(jnp.mean(x * x, axis=-1, keepdims=True) + EPS)
            return x * inv * gamma
        B, L, D = x.shape
        Lc = ctx.shape[1]
        H = HEADS
        hd = D // H
        q = (x @ Wq).reshape(B, L, H, hd).transpose(0, 2, 1, 3)
        kv = (ctx @ Wkv).reshape(B, Lc, 2, H, hd).transpose(2, 0, 3, 1, 4)
        k, v = (kv[0], kv[1])
        q = _rmsnorm(q, q_gamma)
        k = _rmsnorm(k, k_gamma)
        scale = 1.0 / np.sqrt(hd)
        attn = jnp.einsum('bhld,bhmd->bhlm', q, k) * scale
        attn = jax.nn.softmax(attn, axis=-1)
        out = jnp.einsum('bhlm,bhmd->bhld', attn, v)
        out = out.transpose(0, 2, 1, 3).reshape(B, L, D)
        return out @ Wproj

    def _L1_ffn_ref(x, router_w, w1_w, w1_b, w2_w, w2_b, wg_w, wg_b):
        import jax, jax.numpy as jnp
        import numpy as np
        B, S, D, F, E, K = (4, 512, 256, 1024, 8, 2)
        probs = jax.nn.softmax(jnp.einsum('bsd,ed->bse', x, router_w), axis=-1)
        token_probs, probs_idx = jax.lax.top_k(probs, K)
        gates = jnp.sum(token_probs[..., None] * jax.nn.one_hot(probs_idx, E, dtype=x.dtype), axis=-2)
        gates_e = jnp.moveaxis(gates, -1, 0)

        def body(acc, params):
            w1w, w1b, w2w, w2b, wgw, wgb, g = params
            y = jax.nn.gelu(jnp.einsum('bsd,fd->bsf', x, wgw) + wgb, approximate=False)
            h = y * (jnp.einsum('bsd,fd->bsf', x, w1w) + w1b)
            out = jnp.einsum('bsf,df->bsd', h, w2w) + w2b
            return (acc + out * g[..., None], None)
        acc0 = jnp.zeros_like(x)
        out, _ = jax.lax.scan(body, acc0, (w1_w, w1_b, w2_w, w2_b, wg_w, wg_b, gates_e))
        return out
    x = x + jnp.tanh(g_xattn[0]) * _L0_xattn_ref(_layernorm(x, axis=-1), ctx_1024, ctx_1024, fside_BxSx4_0, L0_xattn_Wq, L0_xattn_bq, L0_xattn_Wk, L0_xattn_bk, L0_xattn_Wv, L0_xattn_bv, L0_xattn_Wo, L0_xattn_bo, L0_xattn_Wg, L0_xattn_bg)
    x = x + jnp.tanh(g_ffn[0]) * _L0_ffn_ref(_layernorm(x, axis=-1), L0_ffn_fast_b, L0_ffn_w_fc, L0_ffn_w_proj, L0_ffn_u, L0_ffn_v, L0_ffn_gate)
    x = x + jnp.tanh(g_xattn[1]) * _L1_xattn_ref(_layernorm(x, axis=-1), ctx_1024, L1_xattn_Wq, L1_xattn_Wkv, L1_xattn_Wproj, L1_xattn_q_gamma, L1_xattn_k_gamma)
    x = x + jnp.tanh(g_ffn[1]) * _L1_ffn_ref(_layernorm(x, axis=-1), L1_ffn_router_w, L1_ffn_w1_w, L1_ffn_w1_b, L1_ffn_w2_w, L1_ffn_w2_b, L1_ffn_wg_w, L1_ffn_wg_b)
    return x

_drawn_inputs = setup_inputs


def setup_inputs(seed=0):
    import zlib

    import numpy as np

    out = dict(_drawn_inputs(seed))
    spreads = {'g_ffn': (-1.0, 0.6),
     'L0_xattn_bq': (0.0, 0.8),
     'L0_xattn_bk': (0.0, 2.0),
     'L0_xattn_bv': (0.0, 0.1),
     'L0_xattn_bo': (0.0, 0.1),
     'L0_xattn_bg': (0.0, 0.1),
     'L1_xattn_q_gamma': (1.0, 0.2),
     'L1_xattn_k_gamma': (1.0, 0.538)}
    factors = {'L0_xattn_Wq': 8.0,
     'L0_xattn_Wk': 8.0,
     'L0_ffn_fast_b': 8.0,
     'L0_ffn_u': 8.0,
     'L0_ffn_v': 8.0,
     'L1_ffn_router_w': 8.0,
     'L1_ffn_w1_w': 8.0,
     'L1_ffn_w1_b': 8.0,
     'L1_ffn_w2_w': 8.0,
     'L1_ffn_w2_b': 64.0,
     'L1_ffn_wg_w': 8.0,
     'L1_ffn_wg_b': 8.0}
    for name, (base, spread) in spreads.items():
        noise = np.random.default_rng([zlib.crc32(name.encode()), seed]).standard_normal(out[name].shape)
        drawn = base * np.exp(spread * noise) if base else spread * noise
        out[name] = jnp.asarray(drawn.astype(out[name].dtype))
    for name, factor in factors.items():
        out[name] = (out[name] * factor).astype(out[name].dtype)
    return out
```

```python
from contextlib import ExitStack

import numpy as np
import concourse.bass as bass
from concourse import mybir

ALU = mybir.AluOpType
ACT = mybir.ActivationFunctionType
AX = mybir.AxisListType
F32 = mybir.dt.float32
F16 = mybir.dt.float16
I32 = mybir.dt.int32
U32 = mybir.dt.uint32

P = 128
B = 16
N = 128
D = 256
T = B * N
KD = D // P
H = 16
DK = 64
HD = D // H
CH = H * DK // P
NN = 16
NJ = N // NN
HS = 4
NHG = H // HS
SLOTS = 16
WSC = 64.0
FF = 1024
FC = FF // P
E = 8
MT = 256
NT = (2 * T + E * (MT - 1)) // MT
WM = 2 * KD * FF + FC * D
WB = WM + 2 * FC
GT = 4
NG = B // GT
RANK = 16
EPS_G = 1e-6
ROUND = 12582912.0
TWO_PI = 6.2831845
SHIFT_SCALE = 1.0

HEAD_OF = [8 * (g // 2) + 2 * i + g % 2 for g in range(NHG) for i in range(HS)]


class Count:

    def __init__(self, sem):
        self.sem, self.n = sem, 0

    def up(self, ins):
        ins.then_inc(self.sem, 1)
        self.n += 1
        return self.n


def build(nc, a, dbg=None):
    stages = {"x1": 1, "x2": 2, "x3": 3}.get(dbg, 4)
    with ExitStack() as ctx:
        def sem(name):
            return ctx.enter_context(nc.semaphore(name))

        def sb(name, shape, dt=F32, scope=None):
            return (scope or ctx).enter_context(nc.sbuf_tensor(name, shape, dt))

        bank = [ctx.enter_context(nc.psum_tensor(f"bank{i}", [P, 512], F32)) for i in range(8)]

        X = sb("X", [P, B, D])
        mv = sb("mv", [P, B, 2])
        bst = sb("bst", [P, B, 6])
        rstd = sb("rstd", [P, B])
        rstd_t = sb("rstd_t", [P, 3, B])
        ident = sb("ident", [P, P])
        ident16 = sb("ident16", [P, P], F16)
        gates = sb("gates", [P, 4])
        tg = sb("tg", [P, 4])
        xn = sb("xn", [P, D])

        zero = sb("zero", [P, 2 * D], F16)

        l0 = ExitStack()
        F = sb("F", [P, B, NJ * N], F32, l0)
        Lw16 = sb("Lw16", [P, 2, 2, NJ, H * NN], F16, l0)
        Rm16 = sb("Rm16", [P, B, 2, N], F16, l0)
        We = sb("We", [P, H * NN], F32, l0)
        We16 = sb("We16", [P, 2, H * NN], F16, l0)
        wqkv16 = sb("wqkv16", [P, 3, 2, KD, H * DK], F16, l0)
        WoT = sb("WoT", [P, CH, D], F32, l0)
        bqk = sb("bqk", [P, 2, CH], F32, l0)
        bv = sb("bv", [P, H * DK], F32, l0)
        bo = sb("bo", [P, D], F32, l0)
        pre = ExitStack()
        rows = sb("rows", [P, 2, T], F32, pre)
        cm = sb("cm", [P, T], F32, pre)
        boxn = sb("boxn", [P, B * NJ, 2], F32, pre)
        cn = sb("cn", [P, B * NJ], F32, pre)
        rw = sb("rw", [P, B * NJ], F32, pre)
        cst = sb("cst", [P, 8], F32, pre)
        whc = sb("whc", [P, 2, 2, N], F32, pre)
        wha = sb("wha", [P, 2, N], F32, pre)
        wht = sb("wht", [P, 3, 2, N], F32, pre)
        whk = sb("whk", [P, 3, 2, N], F32, pre)
        AB = sb("AB", [P, 2, H], F32, pre)
        mask = sb("mask", [P, 8], F32, pre)
        Lt = sb("Lt", [P, 2, NJ, H * NN], F32, pre)
        kr = sb("kr", [P, 2, NJ * N], F32, pre)
        wst = Lt[:, 0, :, :].rearrange("p j c -> p (j c)").rearrange("p (k f) -> p k f", k=KD)
        pre.close()
        att = ExitStack()
        q16 = sb("q16", [P, 2, 2, 2, CH, N], F16, att)
        vv = sb("vv", [P, 2, H, DK + 1], F32, att)
        EX = sb("EX", [P, H, N], F32, att)
        PT = sb("PT", [P, H, N], F32, att)
        O = sb("O", [P, H * DK], F32, att)
        OT = sb("OT", [P, CH, N], F32, att)
        qt = sb("qt", [P, 2, HS, N], F32, att)
        ctxf = sb("ctxf", [P, 2, KD, N], F32, att)
        ctx16 = sb("ctx16", [P, 2, 2, KD, N], F16, att)
        xn16 = sb("xn16", [P, 2, 2, KD, N], F16, att)
        nmx = sb("nmx", [P, H], F16, att)
        rden = sb("rden", [P, 2, HS], F32, att)
        otmp = sb("otmp", [P, D], F32, att)
        att.close()
        l0.close()

        l1w = ExitStack()
        wst1 = sb("wst1", [P, KD, 3 * D], F32, l1w)
        w1_16 = sb("w1_16", [P, 2, KD, 3 * D], F16, l1w)
        wpr = sb("wpr", [P, KD, D], F32, l1w)
        gam = sb("gam", [P, 2, D], F32, l1w)

        l0f = ExitStack()
        W1T16 = sb("W1T16", [P, 2, KD, FF], F16, l0f)
        W2T16 = sb("W2T16", [P, FC, D], F16, l0f)
        w2row = sb("w2row", [P, D], F32, l0f)
        xg16 = sb("xg16", [P, 2, 2, KD, GT * N], F16, l0f)
        hr = sb("hr", [P, 2, GT * N], F32, l0f)
        h2 = sb("h2", [P, 2, GT * N], F32, l0f)
        h216 = sb("h216", [P, 2, 2, FC, GT * N], F16, l0f)
        xng = sb("xng", [P, 2, GT, D], F32, l0f)
        ftmp = sb("ftmp", [P, 2, D], F32, l0f)
        fpre = ExitStack()
        wfc = sb("wfc", [P, FC, D], F32, fpre)
        wfa = sb("wfa", [P, FC, D], F32, fpre)
        wfb = sb("wfb", [P, FC, D], F32, fpre)
        wpj = sb("wpj", [P, KD, FF], F32, fpre)
        wpa = sb("wpa", [P, KD, FF], F32, fpre)
        thr = sb("thr", [P, 4, FC + KD], F32, fpre)
        lowr = sb("lowr", [RANK, FF + RANK + D], F32, fpre)
        lowm = sb("lowm", [RANK, D], F32, fpre)
        fgate = sb("fgate", [P, 1], F32, fpre)
        fpre.close()
        l0f.close()

        l1 = ExitStack()
        raw = sb("raw", [P, B, 2, D], F32, l1)
        v1 = sb("v1", [P, B, H, HD + 1], F32, l1)
        ms = sb("ms", [P, 4, B, 2 * H], F32, l1)
        sq = sb("sq", [P, 2, 2, D], F32, l1)
        xn1 = sb("xn1", [P, 2, D], F32, l1)
        x116 = sb("x116", [P, 2, 2, KD, N], F16, l1)
        c1f = sb("c1f", [P, 2, KD, N], F32, l1)
        c116 = sb("c116", [P, 2, 2, KD, N], F16, l1)
        qn = sb("qn", [P, 2, 2, D], F32, l1)
        seg = sb("seg", [P, 2, 2, H, 4, HD], F16, l1)
        qT1 = sb("qT1", [P, 2, 2, CH, N], F16, l1)
        P1 = sb("P1", [P, H, N], F32, l1)
        O1 = sb("O1", [P, D], F32, l1)
        OT1 = sb("OT1", [P, KD, N], F32, l1)
        rden1 = sb("rden1", [P, H], F32, l1)
        nmx1 = sb("nmx1", [P, H], F16, l1)
        l1.close()
        l1w.close()

        mo = ExitStack()
        rwt = sb("rwt", [P, KD, E], F32, mo)
        xnm = sb("xnm", [P, 2, D], F32, mo)
        xm16 = sb("xm16", [P, B, 2, D], F16, mo)
        xTm = sb("xTm", [P, 2, KD, N], F32, mo)
        lg = sb("lg", [P, B, E], F32, mo)
        top = sb("top", [P, B, 8], F32, mo)
        topi = sb("topi", [P, B, 8], U32, mo)
        ex = sb("ex", [P, B, E + 1], F32, mo)
        den = sb("den", [P, 2, B], F32, mo)
        wk = sb("wk", [P, 2, B], F32, mo)
        idf = sb("idf", [P, B, 2], F32, mo)
        oh = sb("oh", [P, E, B * 2], F32, mo)
        oh16 = sb("oh16", [P, E * B * 2], F16, mo)
        tot = sb("tot", [P, E * B * 2], F32, mo)
        cum = sb("cum", [P, E * B * 2], F32, mo)
        pos = sb("pos", [P, E, B * 2], F32, mo)
        one = sb("one", [P, E * B * 2], F32, mo)
        cnt = sb("cnt", [P, 6, E], F32, mo)
        slotf = sb("slotf", [P, B * 2], F32, mo)
        slot = sb("slot", [P, B * 2], U32, mo)
        tri = sb("tri", [P, P], F16, mo)
        one16 = sb("one16", [P, P], F16, mo)
        ioe = sb("ioe", [P, E], F32, mo)
        iot = sb("iot", [P, NT], F32, mo)
        cmp = sb("cmp", [P, NT, E], F32, mo)
        etf = sb("etf", [P, NT], F32, mo)
        eti = sb("eti", [P, NT], I32, mo)
        wsm = sb("wsm", [P, 2, WB], F32, mo)
        wm16 = sb("wm16", [P, 2, 2, WM], F16, mo)
        bms = sb("bms", [P, 2, 2 * FC], F32, mo)
        b2r = sb("b2r", [P, 2, D], F32, mo)
        xin = sb("xin", [P, 2, MT // P, 2 * D], F16, mo)
        xT16 = sb("xT16", [P, 2, 2 * KD, MT], F16, mo)
        yg = sb("yg", [P, 4, MT], F32, mo)
        hf = sb("hf", [P, 2, 2, MT], F32, mo)
        hm16 = sb("hm16", [P, 2, 2, FC, MT], F16, mo)
        ys = sb("ys", [P, 2, MT // P, D], F32, mo)
        yk = sb("yk", [P, 4, D], F32, mo)
        mo.close()
        xs_dram = nc.dram_tensor("expert_tokens", [NT * MT, 2 * D], F16)
        ys_dram = nc.dram_tensor("expert_outputs", [NT * MT, D], F32)

        s_var, s_sqrt = sem("var_ready"), sem("sqrt_ready")
        s_whw, s_whl, s_wht, s_whs = sem("sizes_ready"), sem("sizes_log"), sem("sizes_turns"), sem("sizes_sine")
        s_tg, s_small = sem("tanh_ready"), sem("gate_small_ready")
        s_x, s_c, s_cw = sem("x_loaded"), sem("consts_loaded"), sem("gate_inputs_loaded")
        s_w, s_wfree = sem("weight_staged"), sem("weight_split")
        s_wlo = sem("weight_split_lo")
        s_o = sem("out_weights_loaded")
        s_pv, s_pp = sem("prefix_vector"), sem("prefix_pool")
        s_u, s_abs, s_max, s_ln, s_tt, s_r, s_sin, s_fhi, s_flo = (sem("gate_" + n) for n in (
            "difference", "absolute", "floored", "log", "turns", "reduced", "sine", "high", "low"))
        s_xn, s_xt, s_xh, s_xl = sem("xn_ready"), sem("xn_turned"), sem("xn_high"), sem("xn_low")
        s_cf, s_ch, s_cl = [sem("ctx_loaded_even"), sem("ctx_loaded_odd")], sem("ctx_high"), sem("ctx_low")
        s_qf, s_qe, s_qh, s_ql = sem("qkv_full"), sem("qkv_taken"), sem("qk_high"), sem("qk_low")
        s_sm, s_red = sem("row_scores"), sem("row_max")
        s_st, s_exp = sem("scores_full"), sem("exp_done")
        s_gf, s_pm = sem("gate_full"), sem("probs_ready")
        s_of, s_rd, s_oe = sem("pv_full"), sem("den_inverse"), sem("pv_taken")
        s_ot, s_oc = sem("o_turned"), sem("o_turned_taken")
        s_op, s_opt, s_xu, s_bs, s_bn = sem("proj_full"), sem("proj_taken"), sem("x_updated"), sem("bn_stats_done"), sem("stats_ready")
        s_out = sem("stored")
        f_ld, f_w, f_m, f_lp, f_low, f_tp, f_hi, f_lo, f_sc = (sem("ffn_" + n) for n in (
            "weights_loaded", "ternary_ready", "product_ready", "low_rank_full", "low_rank_added", "weights_turned",
            "weights_high", "weights_low", "row_scale_ready"))
        f_mp = sem("ffn_product_full")
        f_w2 = sem("ffn_w2_ready")
        f_xn, f_xt, f_xh, f_xl = (sem("ffn_" + n) for n in ("xn_ready", "xn_turned", "xn_high", "xn_low"))
        f_h, f_r, f_sq, f_h2, f_l = (sem("ffn_" + n) for n in ("hidden_full", "relu_done", "square_high", "square_done", "square_low"))
        m_ld, m_z, m_zf = sem("router_loaded"), sem("zero_ready"), sem("slots_zeroed")
        m_xn, m_xt, m_xc, m_xh, m_xl = (sem("router_" + n) for n in ("xn_ready", "xn_turned", "xn_copied", "xn_high", "xn_low"))
        m_lg, m_ex, m_er, m_oh, m_pr, m_sl, m_c = (sem("route_" + n) for n in (
            "logits_full", "exponents_ready", "exp_done", "onehot_ready", "counts_full", "slots_ready", "constants_ready"))
        m_v = sem("route_vector")
        m_sc = sem("tokens_scattered")
        m_w = [sem("expert_weights_even"), sem("expert_weights_odd")]
        m_x = [sem("expert_tokens_even"), sem("expert_tokens_odd")]
        m_wh, m_wl, m_bs = sem("expert_weights_high"), sem("expert_weights_low"), sem("expert_bias_scaled")
        m_tt, m_tc = sem("expert_tokens_turned"), sem("expert_tokens_copied")
        m_h, m_g, m_u, m_hh, m_hl = (sem("expert_" + n) for n in ("hidden_full", "gelu_done", "product_done", "hidden_high", "hidden_low"))
        m_o, m_y = sem("expert_out_full"), sem("expert_out_taken")
        m_ys = [sem("expert_stored_even"), sem("expert_stored_odd")]
        m_gk = [sem(f"gathered_{i}") for i in range(4)]
        m_f = sem("x_final")
        a_ld, a_ldk, a_w, a_wl, a_g = (sem("l1_" + n) for n in ("weights_loaded", "late_loaded", "weights_high", "weights_low", "gamma_ready"))
        a_xn, a_xt, a_xh, a_xl = (sem("l1_" + n) for n in ("xn_ready", "xn_turned", "xn_high", "xn_low"))
        a_cf = [sem("l1_ctx_loaded_even"), sem("l1_ctx_loaded_odd")]
        a_ch, a_cl = sem("l1_ctx_high"), sem("l1_ctx_low")
        a_qf, a_kf, a_raw, a_red, a_v = (sem("l1_" + n) for n in ("q_full", "kv_full", "raw_copied", "squares_summed", "v_copied"))
        a_ms, a_sq = sem("l1_mean_ready"), sem("l1_root_ready")
        a_qn, a_gn, a_sh, a_sl = (sem("l1_" + n) for n in ("qk_scaled", "k_gamma_done", "segments_high", "segments_low"))
        a_tq, a_tk, a_cq, a_ck = (sem("l1_" + n) for n in ("q_turned", "k_turned", "q_copied", "k_copied"))
        a_sm, a_mx, a_st, a_ex = (sem("l1_" + n) for n in ("row_scores", "row_max", "scores_full", "exp_done"))
        a_pv, a_rd, a_o, a_ot, a_oc, a_op, a_xu = (sem("l1_" + n) for n in (
            "pv_full", "den_inverse", "pv_taken", "o_turned", "o_turned_taken", "proj_full", "x_updated"))
        f_o, f_ot, f_xu = sem("ffn_out_full"), sem("ffn_out_taken"), sem("ffn_x_updated")

        block = ctx.enter_context(nc.Block())

        @block.sync
        def _(sp):
            sp.dma_start(boxn[:, :, :], a["boxn"]).then_inc(s_cw, 16)
            for xy in range(2):
                for e in range(2):
                    sp.dma_start(rows[64 * xy:64 * xy + 64, e, :], a["boxm"][xy, e, :].partition_broadcast(64)).then_inc(s_cw, 16)
            sp.dma_start(cst[:, :], a["cst"]).then_inc(s_cw, 16)
            sp.dma_start(whc[:, :, :, :], a["whc"]).then_inc(s_cw, 16)
            sp.dma_start(AB[:, :, :], a["AB"]).then_inc(s_cw, 16)
            sp.dma_start(mask[:, :], a["mask"]).then_inc(s_cw, 16)
            sp.dma_start(We[:, :], a["We"]).then_inc(s_cw, 16)
            for j in range(3):
                if j:
                    sp.wait_ge(s_wfree, j)
                    sp.wait_ge(s_wlo, j)
                sp.dma_start(wst[:, :, :], a["wqkv"][j].rearrange("(k p) f -> p k f", p=P)).then_inc(s_w, 16)
            sp.dma_start(WoT[:, :, :], a["woT"].rearrange("(c p) f -> p c f", p=P)).then_inc(s_o, 16)
            sp.dma_start(bqk[:, :, :], a["bqk"]).then_inc(s_o, 16)
            sp.dma_start(bv[:, :], a["bv"].partition_broadcast(P)).then_inc(s_o, 16)
            sp.dma_start(bo[:, :], a["bo"].partition_broadcast(P)).then_inc(s_o, 16)
            sp.wait_ge(s_fhi, B)
            sp.wait_ge(s_flo, B)

            def load_ctx(b, par):
                sp.dma_start(ctxf[:, par, :, :], a["ctxT"][:, bass.ds(b * N, N)].rearrange("(k p) n -> p k n", p=P)).then_inc(s_cf[par], 16)

            load_ctx(0, 0)
            load_ctx(1, 1)
            with sp.Fori(0, B // 2 - 1) as i:
                for par in range(2):
                    b = i * 2 + par
                    sp.wait_ge(s_ch, b + 1)
                    sp.wait_ge(s_cl, b + 1)
                    load_ctx(b + 2, par)
            if stages > 1:
                sp.wait_ge(s_op, B)
                sp.wait_ge(s_xu, B)
                sp.wait_ge(s_oc, 2 * B)
                sp.wait_ge(s_ql, 4 * B)
                sp.wait_ge(s_cl, B)
                sp.dma_start(wfc[:, :, :], a["w_fc"].rearrange("(c p) d -> p c d", p=P)).then_inc(f_ld, 16)
                sp.dma_start(wpj[:, :, :], a["w_proj"].rearrange("(c p) f -> p c f", p=P)).then_inc(f_ld, 16)
                sp.dma_start(lowr[:, :], a["low"]).then_inc(f_ld, 16)
                sp.dma_start(fgate[:, :], a["fgate"].partition_broadcast(P)).then_inc(f_ld, 16)
            if stages > 2:
                sp.dma_start(wst1[:, :, 0:D], a["wq1"].rearrange("(k p) f -> p k f", p=P)).then_inc(a_ld, 16)
                sp.dma_start(wst1[:, :, D:], a["wkv1"].rearrange("(k p) f -> p k f", p=P)).then_inc(a_ld, 16)
                sp.dma_start(wpr[:, :, :], a["wpr1"].rearrange("(k p) f -> p k f", p=P)).then_inc(a_ld, 16)
                sp.dma_start(gam[:, 0, :], a["gq"].partition_broadcast(P)).then_inc(a_ld, 16)
                sp.dma_start(gam[:, 1, :], a["gk"].partition_broadcast(P)).then_inc(a_ld, 16)
                sp.wait_ge(f_xu, B)

                def load_ctx1(b, par):
                    sp.dma_start(c1f[:, par, :, :], a["ctxT"][:, bass.ds(b * N, N)].rearrange("(k p) n -> p k n", p=P)).then_inc(a_cf[par], 16)

                load_ctx1(0, 0)
                load_ctx1(1, 1)
                with sp.Fori(0, B // 2 - 1) as i:
                    for par in range(2):
                        b = i * 2 + par
                        sp.wait_ge(a_ch, b + 1)
                        sp.wait_ge(a_cl, b + 1)
                        load_ctx1(b + 2, par)
            if stages > 3:
                sp.wait_ge(a_xu, B)
                sp.wait_ge(a_op, B)
                sp.dma_start(rwt[:, :, :], a["rwt"].rearrange("(k p) e -> p k e", p=P)).then_inc(m_ld, 16)
                sp.wait_ge(m_sl, 2)

                def load_expert(t, par, first):
                    e = sp.value_load(eti[0:1, bass.ds(t, 1)], min_val=0, max_val=E - 1)
                    if not first:
                        sp.wait_ge(m_wh, 3 * (t - 2) + 3)
                        sp.wait_ge(m_wl, 3 * (t - 2) + 3)
                        sp.wait_ge(m_bs, t - 1)
                    sp.dma_start(wsm[:, par, :], a["wcat"][bass.ds(e, 1), :, :].rearrange("o p c -> (o p) c")).then_inc(m_w[par], 16)
                    if not first:
                        sp.wait_ge(m_y, t - 1)
                    sp.dma_start(b2r[:, par, :], a["b2"][bass.ds(e, 1), :].rearrange("o c -> (o c)").partition_broadcast(P)).then_inc(m_w[par], 16)

                def load_tokens(t, par, first):
                    if not first:
                        sp.wait_ge(m_tt, t - 1)
                    sp.dma_start(xin[:, par, :, :], xs_dram.ap()[bass.ds(t * MT, MT), :].rearrange("(h p) c -> p h c", p=P)).then_inc(m_x[par], 16)

                def store(t, par):
                    sp.wait_ge(m_y, t + 1)
                    sp.dma_start(ys_dram.ap()[bass.ds(t * MT, MT), :].rearrange("(h p) c -> p h c", p=P), ys[:, par, :, :]).then_inc(m_ys[par], 16)

                load_expert(0, 0, True)
                load_expert(1, 1, True)
                sp.wait_ge(m_sc, 16 * 2 * B)
                load_tokens(0, 0, True)
                load_tokens(1, 1, True)
                load_tokens(2, 0, False)
                load_expert(2, 0, False)
                with sp.Fori(0, (NT - 3) // 2) as i:
                    for par in (1, 0):
                        t = i * 2 + 2 - par
                        load_tokens(t + 2, par, False)
                        store(t - 1, 1 - par)
                        load_expert(t + 2, par, False)
                store(NT - 3, 0)
                store(NT - 2, 1)
                store(NT - 1, 0)
                sp.wait_ge(m_f, B)
                sp.dma_start(a["out"].rearrange("b n d -> n b d"), X[:, :, :]).then_inc(s_out, 16)
                sp.wait_ge(s_out, 16)
            if dbg == "x3":
                sp.wait_ge(a_xu, B)
                sp.dma_start(a["out"].rearrange("b n d -> n b d"), X[:, :, :]).then_inc(s_out, 16)
                sp.wait_ge(s_out, 16)
            if dbg == "x2":
                sp.wait_ge(f_xu, B)
                sp.dma_start(a["out"].rearrange("b n d -> n b d"), X[:, :, :]).then_inc(s_out, 16)
                sp.wait_ge(s_out, 16)
            if dbg == "x1":
                sp.wait_ge(s_xu, B)
                sp.dma_start(a["out"].rearrange("b n d -> n b d"), X[:, :, :]).then_inc(s_out, 16)
                sp.wait_ge(s_out, 16)

        @block.gpsimd
        def _(gp):
            pc = Count(s_pp)
            pc.up(nc.gpsimd.memset(ident[:, :], 0.0))
            gp.wait_ge(s_pp, 1)
            n = pc.up(nc.gpsimd.affine_select(out=ident[:, :], in_=ident[:, :], compare_op=ALU.not_equal, fill=1.0,
                                              base=0, pattern=[[-1, P]], channel_multiplier=1))
            gp.wait_ge(s_pp, n)
            pc.up(nc.gpsimd.tensor_copy(ident16[:, :], ident[:, :]))
            nc.gpsimd.memset(zero[:, :], 0.0).then_inc(m_z, 1)
            gp.wait_ge(m_z, 1)
            gp.dma_start(xs_dram.ap().rearrange("(a p) c -> p a c", p=P), zero[:, :].unsqueeze(1).to_broadcast([P, NT * MT // P, 2 * D])).then_inc(m_zf, 16)
            with gp.Fori(0, B // 2) as i:
                for par in range(2):
                    b = i * 2 + par
                    gp.wait_ge(s_sin, b + 1)
                    nc.gpsimd.tensor_copy(F[:, bass.ds(b, 1), 0:NJ * N // 2].bitcast(F16), kr[:, par:par + 1, :]).then_inc(s_fhi, 1)

            def split_ctx(b, par):
                gp.wait_ge(s_ch, b + 1)
                nc.gpsimd.tensor_tensor(ctx16[:, par, 1, :, :], ctxf[:, par, :, :], ctx16[:, par, 0, :, :], ALU.subtract).then_inc(s_cl, 1)

            def split_qk(b, par):
                for r in range(4):
                    w, g = r // 2, r % 2
                    hi = q16[:, par, w, 0, HS * g:HS * g + HS, :]
                    gp.wait_ge(s_qh, 4 * b + r + 1)
                    nc.gpsimd.tensor_tensor(q16[:, par, w, 1, HS * g:HS * g + HS, :], qt[:, r % 2, :, :], hi, ALU.subtract).then_inc(s_ql, 1)

            gp.wait_ge(s_flo, B)
            split_ctx(0, 0)
            split_ctx(1, 1)
            split_qk(0, 0)
            with gp.Fori(0, B // 2 - 1) as i:
                for par in range(2):
                    b = i * 2 + par
                    split_ctx(b + 2, par)
                    split_qk(b + 1, 1 - par)
            split_qk(B - 1, 1)

            if stages > 1:
                for g in range(NG):
                    for c in range(FC):
                        n = g * FC + c
                        gp.wait_ge(f_sq, n + 1)
                        gp.wait_ge(f_h2, n + 1)
                        if g > 1:
                            gp.wait_ge(f_o, GT * (g - 1))
                        nc.gpsimd.tensor_tensor(h216[:, g % 2, 1, c, :], h2[:, n % 2, :], h216[:, g % 2, 0, c, :], ALU.subtract).then_inc(f_l, 1)

            if stages > 2:
                def split_ctx1(b, par):
                    gp.wait_ge(a_ch, b + 1)
                    nc.gpsimd.tensor_tensor(c116[:, par, 1, :, :], c1f[:, par, :, :], c116[:, par, 0, :, :], ALU.subtract).then_inc(a_cl, 1)

                split_ctx1(0, 0)
                split_ctx1(1, 1)
                with gp.Fori(1, B // 2) as i:
                    for par in range(2):
                        split_ctx1(i * 2 + par, par)

            if stages > 3:
                gp.wait_ge(a_xu, B)
                gp.wait_ge(a_op, B)
                nc.gpsimd.memset(one16[:, :], 1.0).then_inc(m_c, 1)
                nc.gpsimd.memset(one[:, :], 1.0).then_inc(m_c, 1)
                gp.wait_ge(m_c, 2)
                nc.gpsimd.affine_select(out=tri[:, :], in_=one16[:, :], compare_op=ALU.is_gt, fill=0.0, base=0,
                                        pattern=[[1, P]], channel_multiplier=-1).then_inc(m_c, 1)
                nc.gpsimd.iota(ioe[:, :], pattern=[[1, E]], base=0, channel_multiplier=0, allow_small_or_imprecise_dtypes=True).then_inc(m_c, 1)
                nc.gpsimd.iota(iot[:, :], pattern=[[1, NT]], base=0, channel_multiplier=0, allow_small_or_imprecise_dtypes=True).then_inc(m_c, 1)

                with gp.Fori(0, B // 2) as i:
                    for par in range(2):
                        b = i * 2 + par
                        gp.wait_ge(m_xh, b + 1)
                        nc.gpsimd.tensor_tensor(xm16[:, bass.ds(b, 1), 1, :], xnm[:, par:par + 1, :], xm16[:, bass.ds(b, 1), 0, :], ALU.subtract).then_inc(m_xl, 1)
                gp.wait_ge(m_xl, B)
                gp.wait_ge(m_zf, 16)
                gp.wait_ge(m_sl, 1)
                for b in range(B):
                    for k in range(2):
                        nc.gpsimd.indirect_dma_start(out=xs_dram.ap(), out_offset=bass.IndirectOffsetOnAxis(ap=slot[:, 2 * b + k:2 * b + k + 1], axis=0),
                                                     in_=xm16[:, b, :, :].rearrange("p h d -> p (h d)"), in_offset=None).then_inc(m_sc, 16)

                def split_low(t, par, q):
                    gp.wait_ge(m_wh, 3 * t + q + 1)
                    cut = WM // 3
                    nc.gpsimd.tensor_tensor(wm16[:, par, 1, q * cut:(q + 1) * cut], wsm[:, par, q * cut:(q + 1) * cut],
                                            wm16[:, par, 0, q * cut:(q + 1) * cut], ALU.subtract).then_inc(m_wl, 1)

                with gp.Fori(0, (NT - 1) // 2) as i:
                    for par in range(2):
                        for q in range(3):
                            split_low(i * 2 + par, par, q)
                for q in range(3):
                    split_low(NT - 1, 0, q)
                gp.wait_ge(m_ys[0], 16 * ((NT + 1) // 2))
                gp.wait_ge(m_ys[1], 16 * (NT // 2))
                for b in range(B):
                    for k in range(2):
                        n = 2 * b + k
                        if n > 3:
                            gp.wait_ge(m_f, (n - 4) // 2 + 1)
                        nc.gpsimd.indirect_dma_start(out=yk[:, n % 4, :], out_offset=None, in_=ys_dram.ap(),
                                                     in_offset=bass.IndirectOffsetOnAxis(ap=slot[:, n:n + 1], axis=0)).then_inc(m_gk[n % 4], 16)

        @block.vector
        def _(dv):
            v = nc.vector
            vc = Count(s_pv)

            def step(ins):
                dv.wait_ge(s_pv, vc.up(ins))

            dv.wait_ge(s_x, 16)
            stats = [1]

            def tile_stats():
                for b in range(B):
                    ins = v.bn_stats(bst[:, b, :], X[:, b, :])
                ins.then_inc(s_bs, 1)
                aggregate()

            def aggregate():
                k = stats[0]
                dv.wait_ge(s_bs, k)
                for b in range(B):
                    ins = v.bn_aggr(mv[:, b, :], bst[:, b, :])
                ins.then_inc(s_bn, 1)

            tile_stats()

            def make_rstd():
                k = stats[0]
                dv.wait_ge(s_bn, k)
                v.tensor_scalar(rstd_t[:, 0, :], mv[:, :, 1], 1e-5, None, ALU.add).then_inc(s_var, 1)
                dv.wait_ge(s_sqrt, k)
                step(v.reciprocal(rstd_t[:, 2, :], rstd_t[:, 1, :]))
                step(v.tensor_tensor(rstd_t[:, 1, :], rstd_t[:, 2, :], rstd_t[:, 2, :], ALU.mult))
                step(v.tensor_tensor(rstd_t[:, 1, :], rstd_t[:, 1, :], rstd_t[:, 0, :], ALU.mult))
                step(v.tensor_scalar(rstd_t[:, 1, :], rstd_t[:, 1, :], -0.5, 1.5, ALU.mult, ALU.add))
                step(v.tensor_tensor(rstd[:, :], rstd_t[:, 1, :], rstd_t[:, 2, :], ALU.mult))
                stats[0] += 1

            make_rstd()
            dv.wait_ge(s_cw, 16 * 10)
            step(v.tensor_tensor(cn[:, :], boxn[:, :, 0], boxn[:, :, 1], ALU.add))
            step(v.tensor_scalar(cn[:, :], cn[:, :], 0.5, None, ALU.mult))
            step(v.tensor_tensor(rw[:, :], boxn[:, :, 1], boxn[:, :, 0], ALU.subtract))
            step(v.tensor_scalar(rw[:, :], rw[:, :], 1.0, None, ALU.add))
            step(v.reciprocal(rw[:, :], rw[:, :]))
            step(v.tensor_tensor(cm[:, :], rows[:, 0, :], rows[:, 1, :], ALU.add))
            step(v.tensor_scalar(cm[:, :], cm[:, :], 0.5, None, ALU.mult))
            step(v.tensor_tensor(wha[:, :, :], whc[:, :, 1, :], whc[:, :, 0, :], ALU.subtract))
            v.tensor_scalar(wha[:, :, :], wha[:, :, :], 1.0, None, ALU.add).then_inc(s_whw, 1)
            for j in range(3):
                dv.wait_ge(s_wfree, j + 1)
                v.scalar_tensor_tensor(wqkv16[:, j, 1, :, :], wst[:, :, :], WSC, wqkv16[:, j, 0, :, :], ALU.mult, ALU.subtract).then_inc(s_wlo, 1)
            with dv.Fori(0, B) as b:
                for j in range(NJ):
                    ins = v.tensor_scalar(F[:, bass.ds(b, 1), j * N:(j + 1) * N], cm[:, bass.ds(b * N, N)],
                                          cn[:, bass.ds(b * NJ + j, 1)], rw[:, bass.ds(b * NJ + j, 1)],
                                          ALU.subtract, ALU.mult)
                ins.then_inc(s_u, 1)
            with dv.Fori(0, B) as b:
                dv.wait_ge(s_abs, b + 1)
                v.tensor_scalar(F[:, bass.ds(b, 1), :], F[:, bass.ds(b, 1), :], 1e-3, None, ALU.max).then_inc(s_max, 1)
            step(v.tensor_copy(We16[:, 0, :], We[:, :]))
            step(v.tensor_tensor(We16[:, 1, :], We[:, :], We16[:, 0, :], ALU.subtract))
            dv.wait_ge(s_whl, 1)
            for r in range(3):
                ins = v.tensor_scalar(wht[:, r, :, :], wha[:, :, :], cst[:, 2:3], cst[:, 3 + r:4 + r], ALU.mult, ALU.add)
            step(ins)
            step(v.tensor_scalar(whk[:, :, :, :], wht[:, :, :, :], ROUND, ROUND, ALU.add, ALU.subtract))
            v.tensor_tensor(wht[:, :, :, :], wht[:, :, :, :], whk[:, :, :, :], ALU.subtract).then_inc(s_wht, 1)
            with dv.Fori(0, B) as b:
                dv.wait_ge(s_ln, b + 1)
                fb = F[:, bass.ds(b, 1), :]
                v.tensor_scalar(fb, fb, cst[:, 0:1], cst[:, 1:2], ALU.mult, ALU.add).then_inc(s_tt, 1)
                dv.wait_ge(s_tt, b * 2 + 1)
                v.tensor_scalar(kr[:, 0:1, :], fb, ROUND, ROUND, ALU.add, ALU.subtract).then_inc(s_tt, 1)
                dv.wait_ge(s_tt, b * 2 + 2)
                v.tensor_tensor(fb, fb, kr[:, 0:1, :], ALU.subtract).then_inc(s_r, 1)
                dv.wait_ge(s_r, b + 1)
            dv.wait_ge(s_whs, 1)
            for g in range(2):
                def bc_n(t):
                    return t.rearrange("p (j n) -> p j n", j=NJ).unsqueeze(2).to_broadcast([P, NJ, H, NN])

                def bc_h(t):
                    return t.unsqueeze(1).unsqueeze(3).to_broadcast([P, NJ, H, NN])

                for r in range(2):
                    o = Lt[:, r, :, :].rearrange("p j (h n) -> p j h n", h=H)
                    for j in range(NJ):
                        ins = v.tensor_tensor(o[:, j], AB[:, r, :].unsqueeze(2).to_broadcast([P, H, NN]),
                                              wht[:, r, g, j * NN:(j + 1) * NN].unsqueeze(1).to_broadcast([P, H, NN]), ALU.mult)
                    step(ins)
                step(v.tensor_tensor(Lt[:, 0, :, :], Lt[:, 0, :, :], Lt[:, 1, :, :], ALU.add))
                step(v.tensor_copy(Lw16[:, g, 0, :, :], Lt[:, 0, :, :]))
                step(v.tensor_tensor(Lw16[:, g, 1, :, :], Lt[:, 0, :, :], Lw16[:, g, 0, :, :], ALU.subtract))
            for b in range(B):
                ins = v.tensor_scalar(Rm16[:, b, 0, :], wht[:, 2, b // 8, :], mask[:, b % 8:b % 8 + 1], None, ALU.mult)
            step(ins)
            for b in range(B):
                ins = v.scalar_tensor_tensor(Rm16[:, b, 1, :], wht[:, 2, b // 8, :], mask[:, b % 8:b % 8 + 1],
                                             Rm16[:, b, 0, :], ALU.mult, ALU.subtract)
            ins.then_inc(s_small, 1)
            with dv.Fori(0, B // 2) as i:
                for par in range(2):
                    b = i * 2 + par
                    dv.wait_ge(s_fhi, b + 1)
                    v.tensor_tensor(F[:, bass.ds(b, 1), NJ * N // 2:].bitcast(F16), kr[:, par:par + 1, :],
                                    F[:, bass.ds(b, 1), 0:NJ * N // 2].bitcast(F16), ALU.subtract).then_inc(s_flo, 1)
            dv.wait_ge(s_flo, B)
            step(v.memset(vv[:, :, :, DK:DK + 1], 1.0))

            def norm(b, wait):
                if wait is not None:
                    dv.wait_ge(s_xt, wait)
                v.tensor_scalar(xn[:, :], X[:, bass.ds(b, 1), :], mv[:, bass.ds(b, 1), 0:1], rstd[:, bass.ds(b, 1)],
                                ALU.subtract, ALU.mult).then_inc(s_xn, 1)

            def xn_low(b, par):
                dv.wait_ge(s_xh, b + 1)
                v.tensor_tensor(xn16[:, par, 1, :, :], bank[6][:, 0:KD * N].rearrange("p (k n) -> p k n", k=KD),
                                xn16[:, par, 0, :, :], ALU.subtract).then_inc(s_xl, 1)

            def row_max(b):
                for g in range(NHG):
                    dv.wait_ge(s_sm, 4 * b + g + 1)
                    v.tensor_reduce(nmx[:, HS * g:HS * g + HS], bank[g % 2][:, :].rearrange("p (h n) -> p h n", h=HS),
                                    AX.X, ALU.max, negate=True).then_inc(s_red, 1)

            def take_pv(c, first=False):
                for f in range(4):
                    ps = bank[6 + f % 2][:, 0:HS * (DK + 1)].rearrange("p (h d) -> p h d", h=HS)
                    dv.wait_ge(s_of, 4 * c + f + 1)
                    if f > 1 or not first:
                        dv.wait_ge(s_oe, 4 * c + f - 1)
                    v.reciprocal(rden[:, f % 2, :].unsqueeze(2), ps[:, :, DK:DK + 1]).then_inc(s_rd, 1)
                    dv.wait_ge(s_rd, 4 * c + f + 1)
                    if f == 0 and not first:
                        dv.wait_ge(s_ot, 2 * c)
                    v.tensor_tensor(O[:, f * HS * DK:(f + 1) * HS * DK].rearrange("p (h d) -> p h d", h=HS), ps[:, :, 0:DK],
                                    rden[:, f % 2, :].unsqueeze(2).to_broadcast([P, HS, DK]), ALU.mult).then_inc(s_oe, 1)

            def take_qk(b, par, first):
                for r in range(4):
                    dv.wait_ge(s_qf, 6 * b + r + 1)
                    if not (first and r < 2):
                        dv.wait_ge(s_ql, 4 * b + r - 1)
                    v.scalar_tensor_tensor(qt[:, r % 2, :, :], bank[4 + r % 2][:, :].rearrange("p (c n) -> p c n", c=HS), 1.0 / WSC,
                                           bqk[:, r // 2, HS * (r % 2):HS * (r % 2) + HS].unsqueeze(2).to_broadcast([P, HS, N]),
                                           ALU.mult, ALU.add).then_inc(s_qe, 1)

            def take_v(b, par):
                for r in range(2):
                    dv.wait_ge(s_qf, 6 * b + 4 + r + 1)
                    v.scalar_tensor_tensor(vv[:, par, 8 * r:8 * r + 8, 0:DK], bank[4 + r][:, :].rearrange("p (h d) -> p h d", h=8), 1.0 / WSC,
                                           bv[:, 512 * r:512 * r + 512].rearrange("p (h d) -> p h d", h=8),
                                           ALU.mult, ALU.add).then_inc(s_qe, 1)

            def residual(c):
                dv.wait_ge(s_op, c + 1)
                v.tensor_tensor(otmp[:, :], bank[7][:, 0:D], bo[:, :], ALU.add).then_inc(s_opt, 1)
                dv.wait_ge(s_opt, c + 1)
                xb = X[:, bass.ds(c, 1), :]
                v.scalar_tensor_tensor(xb, otmp[:, :].unsqueeze(1), tg[:, 0:1], xb, ALU.mult, ALU.add).then_inc(s_xu, 1)

            def probs(b):
                for g in range(4):
                    dv.wait_ge(s_gf, 4 * b + g + 1)
                    if g == 0:
                        dv.wait_ge(s_exp, 4 * b + 4)
                    for jj in range(2):
                        j = 2 * g + jj
                        v.scalar_tensor_tensor(PT[:, :, j * NN:(j + 1) * NN],
                                               bank[2 + g % 2][:, jj * 256:(jj + 1) * 256].rearrange("p (h n) -> p h n", h=H), EPS_G,
                                               EX[:, :, j * NN:(j + 1) * NN], ALU.max, ALU.mult).then_inc(s_pm, 1)

            dv.wait_ge(s_o, 64)
            dv.wait_ge(s_tg, 1)
            norm(0, None)
            xn_low(0, 0)
            norm(1, 1)
            xn_low(1, 1)
            take_qk(0, 0, True)
            take_v(0, 0)

            def iteration(b, par, has_c, has_q, has_x, first=False):
                if has_x:
                    norm(b + 2, b + 2)
                row_max(b)
                if has_c:
                    take_pv(b - 1, first)
                if has_q:
                    take_qk(b + 1, 1 - par, False)
                if has_x:
                    xn_low(b + 2, par)
                if has_q:
                    take_v(b + 1, 1 - par)
                if has_c:
                    residual(b - 1)
                probs(b)

            iteration(0, 0, False, True, True)
            iteration(1, 1, True, True, True, True)
            with dv.Fori(0, B // 2 - 2) as i:
                for par in range(2):
                    iteration(i * 2 + 2 + par, par, True, True, True)
            iteration(B - 2, 0, True, True, False)
            iteration(B - 1, 1, True, False, False)
            take_pv(B - 1)
            residual(B - 1)

            if stages > 1:
                dv.wait_ge(s_xu, B)
                tile_stats()
                make_rstd()
                dv.wait_ge(f_ld, 64)
                step(v.tensor_reduce(thr[:, 0, 0:FC], wfc[:, :, :], AX.X, ALU.add, apply_absolute_value=True))
                step(v.tensor_reduce(thr[:, 0, FC:], wpj[:, :, :], AX.X, ALU.add, apply_absolute_value=True))
                step(v.tensor_scalar(thr[:, 0, 0:FC], thr[:, 0, 0:FC], 1.0 / D, 1e-5, ALU.mult, ALU.max))
                step(v.tensor_scalar(thr[:, 0, FC:], thr[:, 0, FC:], 1.0 / FF, 1e-5, ALU.mult, ALU.max))
                for r, k in ((1, 0.5), (2, -0.5), (3, -1.0)):
                    ins = v.tensor_scalar(thr[:, r, :], thr[:, 0, :], k, None, ALU.mult)
                step(ins)
                for c in range(FC):
                    v.tensor_scalar(wfa[:, c, :], wfc[:, c, :], thr[:, 1, c:c + 1], thr[:, 0, c:c + 1], ALU.is_gt, ALU.mult)
                    ins = v.tensor_scalar(wfb[:, c, :], wfc[:, c, :], thr[:, 2, c:c + 1], thr[:, 3, c:c + 1], ALU.is_lt, ALU.mult)
                step(ins)
                step(v.tensor_tensor(wfa[:, :, :], wfa[:, :, :], wfb[:, :, :], ALU.add))
                for c in range(KD):
                    ins = v.tensor_scalar(wpa[:, c, :], wpj[:, c, :], thr[:, 2, FC + c:FC + c + 1], -1.0, ALU.is_lt, ALU.mult)
                step(ins)
                for c in range(KD):
                    ins = v.scalar_tensor_tensor(wpa[:, c, :], wpj[:, c, :], thr[:, 1, FC + c:FC + c + 1], wpa[:, c, :], ALU.is_gt, ALU.add)
                ins.then_inc(f_w, 1)
                dv.wait_ge(f_mp, 1)
                v.tensor_copy(lowm[:, :], bank[4][0:RANK, 0:D]).then_inc(f_m, 1)
                for r in range(FC // 2):
                    dv.wait_ge(f_lp, r + 1)
                    v.scalar_tensor_tensor(wfa[:, 2 * r:2 * r + 2, :], bank[r][:, :].rearrange("p (c d) -> p c d", c=2), fgate[:, 0:1],
                                           wfa[:, 2 * r:2 * r + 2, :], ALU.mult, ALU.add).then_inc(f_low, 1)
                for r in range(4):
                    dv.wait_ge(f_hi, r + 1)
                    kk, fh = r // 2, r % 2
                    v.scalar_tensor_tensor(W1T16[:, 1, kk, 512 * fh:512 * fh + 512], bank[r][:, :], WSC,
                                           W1T16[:, 0, kk, 512 * fh:512 * fh + 512], ALU.mult, ALU.subtract).then_inc(f_lo, 1)
                dv.wait_ge(f_sc, 1)
                v.tensor_copy(w2row[:, :], bank[4][:, 0:D]).then_inc(f_w2, 1)

                def ffn_norm(g):
                    for i in range(GT):
                        t = g * GT + i
                        ins = v.tensor_scalar(xng[:, g % 2, i, :], X[:, t, :], mv[:, t, 0:1], rstd[:, t:t + 1], ALU.subtract, ALU.mult)
                    ins.then_inc(f_xn, 1)

                def ffn_low(g):
                    for kk in range(KD):
                        dv.wait_ge(f_xh, 2 * g + kk + 1)
                        v.tensor_tensor(xg16[:, g % 2, 1, kk, :], bank[4 + kk][:, :], xg16[:, g % 2, 0, kk, :], ALU.subtract).then_inc(f_xl, 1)

                def ffn_square(g):
                    for c in range(FC):
                        n = g * FC + c
                        dv.wait_ge(f_r, n + 1)
                        if n > 1:
                            dv.wait_ge(f_l, n - 1)
                        v.tensor_tensor(h2[:, n % 2, :], hr[:, n % 2, :], hr[:, n % 2, :], ALU.mult).then_inc(f_h2, 1)

                def ffn_residual(g):
                    for i in range(GT):
                        t = g * GT + i
                        dv.wait_ge(f_o, t + 1)
                        if t > 1:
                            dv.wait_ge(f_xu, t - 1)
                        v.tensor_tensor(ftmp[:, t % 2, :], bank[6 + t % 2][:, 0:D], w2row[:, :], ALU.mult).then_inc(f_ot, 1)
                        dv.wait_ge(f_ot, t + 1)
                        v.scalar_tensor_tensor(X[:, t, :], ftmp[:, t % 2, :], tg[:, 2:3], X[:, t, :], ALU.mult, ALU.add).then_inc(f_xu, 1)
                        dv.wait_ge(f_xu, t + 1)
                        ins = v.bn_stats(bst[:, t, :], X[:, t, :])
                    if g == NG - 1:
                        ins.then_inc(s_bs, 1)

                ffn_norm(0)
                ffn_norm(1)
                ffn_low(0)
                for g in range(NG):
                    ffn_square(g)
                    if g + 2 < NG:
                        ffn_norm(g + 2)
                    if g + 1 < NG:
                        ffn_low(g + 1)
                    if g:
                        ffn_residual(g - 1)
                ffn_residual(NG - 1)

            if stages > 2:
                aggregate()
                make_rstd()
                dv.wait_ge(a_w, 1)
                v.scalar_tensor_tensor(w1_16[:, 1, :, :], wst1[:, :, :], WSC, w1_16[:, 0, :, :], ALU.mult, ALU.subtract).then_inc(a_wl, 1)
                v.tensor_tensor(gam[:, 0, :], gam[:, 0, :], gam[:, 1, :], ALU.mult).then_inc(a_g, 1)
                for i in range(B):
                    ins = v.memset(v1[:, i, :, HD:HD + 1], 1.0)
                step(ins)
                step(v.memset(seg[:, :, :, :, 3:4, :].rearrange("a r q h s d -> a (r q h) (s d)"), 0.0))

                def norm1(b, par, first):
                    if not first:
                        dv.wait_ge(a_xt, b - 1)
                    v.tensor_scalar(xn1[:, par, :], X[:, bass.ds(b, 1), :], mv[:, bass.ds(b, 1), 0:1], rstd[:, bass.ds(b, 1)],
                                    ALU.subtract, ALU.mult).then_inc(a_xn, 1)

                def low1(b, par):
                    dv.wait_ge(a_xh, b + 1)
                    v.tensor_tensor(x116[:, par, 1, :, :], bank[par][:, 0:KD * N].rearrange("p (k n) -> p k n", k=KD),
                                    x116[:, par, 0, :, :], ALU.subtract).then_inc(a_xl, 1)

                def sums(b, par):
                    dv.wait_ge(a_kf, b + 1)
                    v.tensor_scalar(v1[:, bass.ds(b, 1), :, 0:HD], bank[4 + par][:, D:].rearrange("p (o h d) -> p o h d", o=1, h=H),
                                    1.0 / WSC, None, ALU.mult).then_inc(a_v, 1)
                    dv.wait_ge(a_raw, b + 1)
                    v.tensor_reduce(ms[:, 0, bass.ds(b, 1), :], sq[:, par:par + 1, :, :].rearrange("p o q (h d) -> p o (q h) d", h=H),
                                    AX.X, ALU.add).then_inc(a_red, 1)

                norm1(0, 0, True)
                norm1(1, 1, True)
                low1(0, 0)
                low1(1, 1)
                with dv.Fori(1, B // 2) as i:
                    for par in range(2):
                        norm1(i * 2 + par, par, False)
                    for par in range(2):
                        sums(i * 2 - 2 + par, par)
                    for par in range(2):
                        low1(i * 2 + par, par)
                sums(B - 2, 0)
                sums(B - 1, 1)
                dv.wait_ge(a_red, B)
                v.tensor_scalar(ms[:, 0, :, :], ms[:, 0, :, :], 1.0 / HD, 1e-6, ALU.mult, ALU.add).then_inc(a_ms, 1)
                dv.wait_ge(a_sq, 1)
                step(v.reciprocal(ms[:, 2, :, :], ms[:, 1, :, :]))
                step(v.tensor_tensor(ms[:, 1, :, :], ms[:, 2, :, :], ms[:, 2, :, :], ALU.mult))
                step(v.tensor_tensor(ms[:, 1, :, :], ms[:, 1, :, :], ms[:, 0, :, :], ALU.mult))
                step(v.tensor_scalar(ms[:, 1, :, :], ms[:, 1, :, :], -0.5, 1.5, ALU.mult, ALU.add))
                step(v.tensor_tensor(ms[:, 3, :, :], ms[:, 1, :, :], ms[:, 2, :, :], ALU.mult))

                def scale1(b, par, first):
                    if not first:
                        dv.wait_ge(a_sh, b - 1)
                        dv.wait_ge(a_sl, b - 1)
                    v.tensor_tensor(qn[:, par, :, :].rearrange("p q (h d) -> p (q h) d", h=H),
                                    raw[:, bass.ds(b, 1), :, :].rearrange("p o q (h d) -> p (o q h) d", h=H),
                                    ms[:, 3, bass.ds(b, 1), :].rearrange("p o h -> p (o h)").unsqueeze(2).to_broadcast([P, 2 * H, HD]), ALU.mult).then_inc(a_qn, 1)
                    dv.wait_ge(a_qn, b + 1)
                    v.tensor_tensor(qn[:, par, 1, :], qn[:, par, 1, :], gam[:, 0, :], ALU.mult).then_inc(a_gn, 1)

                def seg_low(b, par):
                    dv.wait_ge(a_sh, b + 1)
                    for w, sg in ((0, 2), (1, 1)):
                        ins = v.tensor_tensor(seg[:, par, w, :, sg, :], qn[:, par, w, :].rearrange("p (h d) -> p h d", h=H),
                                              seg[:, par, w, :, 0, :], ALU.subtract)
                    ins.then_inc(a_sl, 1)

                def copy_k(b, par):
                    dv.wait_ge(a_tk, b + 1)
                    v.tensor_copy(qT1[:, par, 1, :, :].rearrange("p c n -> p (c n)"), bank[3][:, :].bitcast(F16)).then_inc(a_ck, 1)

                def row_max1(b):
                    for g in range(NHG):
                        dv.wait_ge(a_sm, 4 * b + g + 1)
                        v.tensor_reduce(nmx1[:, HS * g:HS * g + HS], bank[g % 2][:, :].rearrange("p (h n) -> p h n", h=HS),
                                        AX.X, ALU.max, negate=True).then_inc(a_mx, 1)

                def take_pv1(c, first):
                    ps = bank[6][:, 0:H * (HD + 1)].rearrange("p (h d) -> p h d", h=H)
                    dv.wait_ge(a_pv, c + 1)
                    if not first:
                        dv.wait_ge(a_o, c)
                    v.reciprocal(rden1[:, :].unsqueeze(2), ps[:, :, HD:HD + 1]).then_inc(a_rd, 1)
                    dv.wait_ge(a_rd, c + 1)
                    if not first:
                        dv.wait_ge(a_ot, c)
                    v.tensor_tensor(O1[:, :].rearrange("p (h d) -> p h d", h=H), ps[:, :, 0:HD],
                                    rden1[:, :].unsqueeze(2).to_broadcast([P, H, HD]), ALU.mult).then_inc(a_o, 1)

                def residual1(c):
                    dv.wait_ge(a_op, c + 1)
                    xb = X[:, bass.ds(c, 1), :]
                    v.scalar_tensor_tensor(xb, bank[5][:, 0:D].unsqueeze(1), tg[:, 1:2], xb, ALU.mult, ALU.add).then_inc(a_xu, 1)

                scale1(0, 0, True)
                scale1(1, 1, True)
                seg_low(0, 0)
                seg_low(1, 1)
                copy_k(0, 0)

                def iteration1(b, par, c, has_q, has_x):
                    if has_x:
                        scale1(b + 2, par, False)
                    row_max1(b)
                    if c:
                        take_pv1(b - 1, c == 1)
                    if has_q:
                        copy_k(b + 1, 1 - par)
                    if has_x:
                        seg_low(b + 2, par)
                    if c:
                        residual1(b - 1)

                iteration1(0, 0, 0, True, True)
                iteration1(1, 1, 1, True, True)
                with dv.Fori(0, B // 2 - 2) as i:
                    for par in range(2):
                        iteration1(i * 2 + 2 + par, par, 2, True, True)
                iteration1(B - 2, 0, 2, True, False)
                iteration1(B - 1, 1, 2, False, False)
                take_pv1(B - 1, False)
                residual1(B - 1)

            if stages > 3:
                dv.wait_ge(a_xu, B)
                tile_stats()
                make_rstd()
                v4 = Count(m_v)

                def then(ins):
                    dv.wait_ge(m_v, v4.up(ins))

                def norm_m(b, par, first):
                    if not first:
                        dv.wait_ge(m_xt, b - 1)
                        dv.wait_ge(m_xl, b - 1)
                    v.tensor_scalar(xnm[:, par, :], X[:, bass.ds(b, 1), :], mv[:, bass.ds(b, 1), 0:1], rstd[:, bass.ds(b, 1)],
                                    ALU.subtract, ALU.mult).then_inc(m_xn, 1)

                dv.wait_ge(a_op, B)
                norm_m(0, 0, True)
                norm_m(1, 1, True)
                with dv.Fori(1, B // 2) as i:
                    for par in range(2):
                        norm_m(i * 2 + par, par, False)
                dv.wait_ge(m_lg, B)
                then(v.tensor_copy(lg[:, :, :], bank[7][:, 0:B * E].rearrange("p (b e) -> p b e", e=E)))
                for b in range(B):
                    ins = v.max(top[:, b, :], lg[:, b, :])
                then(ins)
                for b in range(B):
                    v.max_index(topi[:, b, :], top[:, b, :], lg[:, b, :])
                v.tensor_tensor(ex[:, :, 0:E], lg[:, :, :], top[:, :, 0:1].to_broadcast([P, B, E]), ALU.subtract)
                then(v.tensor_tensor(ex[:, :, E], top[:, :, 1], top[:, :, 0], ALU.subtract))
                v.engine_nop().then_inc(m_ex, 1)
                then(v.tensor_copy(idf[:, :, :], topi[:, :, 0:2]))
                dv.wait_ge(m_c, 5)
                then(v.tensor_tensor(oh[:, :, :], idf[:, :, :].rearrange("p b k -> p (b k)").unsqueeze(1).to_broadcast([P, E, B * 2]),
                                     ioe[:, :].unsqueeze(2).to_broadcast([P, E, B * 2]), ALU.is_equal))
                v.tensor_copy(oh16[:, :], oh[:, :, :].rearrange("p e n -> p (e n)")).then_inc(m_oh, 1)
                dv.wait_ge(m_er, 1)
                then(v.tensor_reduce(den[:, 0, :], ex[:, :, 0:E], AX.X, ALU.add))
                then(v.reciprocal(den[:, 1, :], den[:, 0, :]))
                then(v.tensor_scalar(wk[:, 0, :], den[:, 1, :], tg[:, 3:4], None, ALU.mult))
                then(v.tensor_tensor(wk[:, 1, :], wk[:, 0, :], ex[:, :, E], ALU.mult))
                dv.wait_ge(m_pr, 1)
                then(v.tensor_copy(tot[:, :], bank[6][:, 256:512]))
                v.tensor_tensor_scan(cum[:, :], one[:, :], tot[:, :], 0.0, ALU.mult, ALU.add)
                then(v.tensor_reduce(cnt[:, 0, :], tot[:, :].rearrange("p (e n) -> p e n", e=E), AX.X, ALU.add))
                then(v.tensor_tensor_scan(cnt[:, 1, :], one[:, 0:E], cnt[:, 0, :], 0.0, ALU.mult, ALU.add))
                then(v.tensor_scalar(cnt[:, 2, :], cnt[:, 0, :], 1.0 / MT, (MT - 1.0) / MT - 0.5 + 0.5 / MT, ALU.mult, ALU.add))
                then(v.tensor_scalar(cnt[:, 2, :], cnt[:, 2, :], ROUND, ROUND, ALU.add, ALU.subtract))
                then(v.tensor_tensor_scan(cnt[:, 3, :], one[:, 0:E], cnt[:, 2, :], 0.0, ALU.mult, ALU.add))
                then(v.tensor_tensor(cnt[:, 4, :], cnt[:, 3, :], cnt[:, 2, :], ALU.subtract))
                then(v.tensor_tensor(cnt[:, 5, :], cnt[:, 1, :], cnt[:, 0, :], ALU.subtract))
                then(v.scalar_tensor_tensor(cnt[:, 4, :], cnt[:, 4, :], float(MT), cnt[:, 5, :], ALU.mult, ALU.subtract))
                then(v.tensor_tensor(pos[:, :, :].rearrange("p e n -> p (e n)"), cum[:, :], tot[:, :], ALU.subtract))
                then(v.tensor_tensor(pos[:, :, :].rearrange("p e n -> p (e n)"), pos[:, :, :].rearrange("p e n -> p (e n)"), bank[6][:, 0:256], ALU.add))
                then(v.tensor_tensor(pos[:, :, :], pos[:, :, :], cnt[:, 4, :].unsqueeze(2).to_broadcast([P, E, B * 2]), ALU.add))
                then(v.tensor_tensor(pos[:, :, :], pos[:, :, :], oh[:, :, :], ALU.mult))
                then(v.tensor_reduce(slotf[:, :], pos[:, :, :].rearrange("p e n -> p n e"), AX.X, ALU.add))
                v.tensor_copy(slot[:, :], slotf[:, :]).then_inc(m_sl, 1)
                then(v.tensor_tensor(cmp[:, :, :], cnt[:, 3, :].unsqueeze(1).to_broadcast([P, NT, E]),
                                     iot[:, :].unsqueeze(2).to_broadcast([P, NT, E]), ALU.is_le))
                then(v.tensor_reduce(etf[:, :], cmp[:, :, :], AX.X, ALU.add))
                v.tensor_scalar(eti[:, :], etf[:, :], float(E - 1), None, ALU.min).then_inc(m_sl, 1)

                def bias_scale(t, par, first):
                    dv.wait_ge(m_w[par], (t - par) * 16 + 32)
                    if not first:
                        dv.wait_ge(m_u, FC * (t - 1))
                        dv.wait_ge(m_g, FC * (t - 1))
                    v.tensor_copy(bms[:, par, :], wsm[:, par, WM:WB]).then_inc(m_bs, 1)
                    dv.wait_ge(m_bs, t + 1)

                def products(t, par, c0, c1, first):
                    for c in range(c0, c1):
                        dv.wait_ge(m_g, FC * t + c + 1)
                        if c % 2 == 0 and not (first and c < 4):
                            dv.wait_ge(m_hh, 4 * t + c // 2 - 1)
                            dv.wait_ge(m_hl, 4 * t + c // 2 - 1)
                        v.scalar_tensor_tensor(hf[:, (c // 2) % 2, c % 2, :], bank[c % 4][:, MT:2 * MT], bms[:, par, FC + c:FC + c + 1],
                                               yg[:, c % 4, :], ALU.add, ALU.mult).then_inc(m_u, 1)
                        if c % 2:
                            q = c // 2
                            dv.wait_ge(m_hh, 4 * t + q + 1)
                            v.tensor_tensor(hm16[:, par, 1, c - 1:c + 1, :], hf[:, q % 2, :, :], hm16[:, par, 0, c - 1:c + 1, :], ALU.subtract).then_inc(m_hl, 1)

                def copy_tokens(t, par):
                    dv.wait_ge(m_tt, t + 1)
                    v.tensor_copy(xT16[:, par, :, :].rearrange("p a n -> p (a n)"), bank[4][:, :].bitcast(F16)).then_inc(m_tc, 1)

                def take_out(t, par, first):
                    dv.wait_ge(m_o, t + 1)
                    if not first:
                        dv.wait_ge(m_ys[par], (t - par) * 8)
                    v.scalar_tensor_tensor(ys[:, par, :, :], bank[5 + par][:, :].rearrange("p (h d) -> p h d", h=2), 1.0,
                                           b2r[:, par, :].unsqueeze(1).to_broadcast([P, MT // P, D]), ALU.mult, ALU.add).then_inc(m_y, 1)

                def expert_v(t, par, prev, nxt, first=False):
                    products(t, par, 0, 4, first)
                    if prev:
                        take_out(t - 1, 1 - par, prev == 1)
                    if nxt:
                        copy_tokens(t + 1, 1 - par)
                        bias_scale(t + 1, 1 - par, first)
                    products(t, par, 4, 8, False)

                bias_scale(0, 0, True)
                copy_tokens(0, 0)
                expert_v(0, 0, 0, True, True)
                expert_v(1, 1, 1, True)
                expert_v(2, 0, 1, True)
                with dv.Fori(0, (NT - 5) // 2) as i:
                    for q in range(2):
                        expert_v(i * 2 + 3 + q, 1 - q, 2, True)
                expert_v(NT - 2, 1, 2, True)
                expert_v(NT - 1, 0, 2, False)
                take_out(NT - 1, 0, False)
                for b in range(B):
                    for k in range(2):
                        n = 2 * b + k
                        dv.wait_ge(m_gk[n % 4], 16 * (n // 4 + 1))
                        ins = v.scalar_tensor_tensor(X[:, b, :], yk[:, n % 4, :], wk[:, k, b:b + 1], X[:, b, :], ALU.mult, ALU.add)
                        if k == 0:
                            then(ins)
                    ins.then_inc(m_f, 1)

        @block.scalar
        def _(ac):
            s = nc.scalar
            ac.dma_start(X[:, :, :], a["x"].rearrange("b n d -> n b d")).then_inc(s_x, 16)
            ac.dma_start(gates[:, 0:2], a["g_xattn"].partition_broadcast(P)).then_inc(s_c, 16)
            ac.dma_start(gates[:, 2:4], a["g_ffn"].partition_broadcast(P)).then_inc(s_c, 16)
            ac.wait_ge(s_c, 32)
            s.activation(tg[:, :], gates[:, :], ACT.Tanh).then_inc(s_tg, 1)
            ac.wait_ge(s_var, 1)
            s.activation(rstd_t[:, 1, :], rstd_t[:, 0, :], ACT.Sqrt).then_inc(s_sqrt, 1)
            for j in range(3):
                ac.wait_ge(s_w, 16 * j + 16)
                s.activation(wqkv16[:, j, 0, :, :], wst[:, :, :], ACT.Copy, scale=WSC).then_inc(s_wfree, 1)
            with ac.Fori(0, B) as b:
                ac.wait_ge(s_u, b + 1)
                fb = F[:, bass.ds(b, 1), :]
                s.activation(fb, fb, ACT.Abs).then_inc(s_abs, 1)
            ac.wait_ge(s_whw, 1)
            s.activation(wha[:, :, :], wha[:, :, :], ACT.Ln).then_inc(s_whl, 1)
            with ac.Fori(0, B) as b:
                ac.wait_ge(s_max, b + 1)
                fb = F[:, bass.ds(b, 1), :]
                s.activation(fb, fb, ACT.Ln).then_inc(s_ln, 1)
            ac.wait_ge(s_wht, 1)
            s.activation(wht[:, :, :, :], wht[:, :, :, :], ACT.Sin, scale=TWO_PI).then_inc(s_whs, 1)
            ac.wait_ge(s_r, B)
            for b in range(2):
                s.activation(kr[:, b:b + 1, :], F[:, b:b + 1, :], ACT.Sin, scale=TWO_PI).then_inc(s_sin, 1)
            with ac.Fori(1, B // 2) as i:
                for par in range(2):
                    b = i * 2 + par
                    ac.wait_ge(s_fhi, b - 1)
                    ac.wait_ge(s_flo, b - 1)
                    s.activation(kr[:, par:par + 1, :], F[:, bass.ds(b, 1), :], ACT.Sin, scale=TWO_PI).then_inc(s_sin, 1)

            def xn_high(b, par):
                ac.wait_ge(s_xt, b + 1)
                s.activation(xn16[:, par, 0, :, :], bank[6][:, 0:KD * N].rearrange("p (k n) -> p k n", k=KD), ACT.Copy).then_inc(s_xh, 1)

            def take_o(c, first):
                for r in range(2):
                    ac.wait_ge(s_ot, 2 * c + r + 1)
                    if r == 0 and not first:
                        ac.wait_ge(s_op, c)
                    s.activation(OT[:, 4 * r:4 * r + 4, :], bank[6 + r][:, :].rearrange("p (c n) -> p c n", c=4), ACT.Copy).then_inc(s_oc, 1)

            def exps(b, first):
                for g in range(4):
                    ac.wait_ge(s_st, 4 * b + g + 1)
                    if g == 0 and not first:
                        ac.wait_ge(s_pm, 8 * b)
                    s.activation(EX[:, HS * g:HS * g + HS, :], bank[g % 2][:, :].rearrange("p (h n) -> p h n", h=HS), ACT.Exp,
                                 scale=DK ** -0.5).then_inc(s_exp, 1)

            def ctx_high(b, par, first):
                ac.wait_ge(s_cf[par], (b - par) * 8 + 16)
                if not first:
                    ac.wait_ge(s_qf, 6 * b - 6)
                s.activation(ctx16[:, par, 0, :, :], ctxf[:, par, :, :], ACT.Copy).then_inc(s_ch, 1)

            def qk_high(b, par):
                for r in range(4):
                    w, g = r // 2, r % 2
                    ac.wait_ge(s_qe, 6 * b + r + 1)
                    s.activation(q16[:, par, w, 0, HS * g:HS * g + HS, :], qt[:, r % 2, :, :], ACT.Copy).then_inc(s_qh, 1)

            ac.wait_ge(s_flo, B)
            ctx_high(0, 0, True)
            ctx_high(1, 1, True)
            xn_high(0, 0)
            xn_high(1, 1)
            qk_high(0, 0)

            def iteration(b, par, c, has_x, has_q=True):
                if has_x:
                    ctx_high(b + 2, par, False)
                if has_q:
                    qk_high(b + 1, 1 - par)
                if c:
                    take_o(b - 1, c == 1)
                if has_x:
                    xn_high(b + 2, par)
                exps(b, c == 0)

            iteration(0, 0, 0, True)
            iteration(1, 1, 1, True)
            with ac.Fori(0, B // 2 - 2) as i:
                for par in range(2):
                    iteration(i * 2 + 2 + par, par, 2, True)
            iteration(B - 2, 0, 2, False)
            iteration(B - 1, 1, 2, False, False)
            take_o(B - 1, False)

            if stages > 1:
                ac.wait_ge(s_var, 2)
                s.activation(rstd_t[:, 1, :], rstd_t[:, 0, :], ACT.Sqrt).then_inc(s_sqrt, 1)
                for r in range(4):
                    ac.wait_ge(f_tp, r + 1)
                    kk, fh = r // 2, r % 2
                    s.activation(W1T16[:, 0, kk, 512 * fh:512 * fh + 512], bank[r][:, :], ACT.Copy, scale=WSC).then_inc(f_hi, 1)
                for r in range(4):
                    ac.wait_ge(f_tp, r + 5)
                    s.activation(W2T16[:, 2 * r:2 * r + 2, :], bank[r][:, :].rearrange("p (f d) -> p f d", f=2), ACT.Copy).then_inc(f_hi, 1)

                def ffn_high(g):
                    for kk in range(KD):
                        ac.wait_ge(f_xt, 2 * g + kk + 1)
                        s.activation(xg16[:, g % 2, 0, kk, :], bank[4 + kk][:, :], ACT.Copy).then_inc(f_xh, 1)

                def ffn_relu(g):
                    for c in range(FC):
                        n = g * FC + c
                        ac.wait_ge(f_h, n + 1)
                        if n > 1:
                            ac.wait_ge(f_sq, n - 1)
                            ac.wait_ge(f_h2, n - 1)
                        s.activation(hr[:, n % 2, :], bank[n % 4][:, :], ACT.Relu, scale=1.0 / WSC).then_inc(f_r, 1)
                        ac.wait_ge(f_r, n + 1)
                        if c == 0 and g > 1:
                            ac.wait_ge(f_o, GT * (g - 1))
                        s.activation(h216[:, g % 2, 0, c, :], hr[:, n % 2, :], ACT.Square).then_inc(f_sq, 1)

                ffn_high(0)
                for g in range(NG):
                    if g + 1 < NG:
                        ffn_high(g + 1)
                    ffn_relu(g)

            if stages > 2:
                ac.wait_ge(s_var, 3)
                s.activation(rstd_t[:, 1, :], rstd_t[:, 0, :], ACT.Sqrt).then_inc(s_sqrt, 1)
                ac.wait_ge(a_ld, 80)
                s.activation(w1_16[:, 0, :, :], wst1[:, :, :], ACT.Copy, scale=WSC).then_inc(a_w, 1)

                def high1(b, par):
                    ac.wait_ge(a_xt, b + 1)
                    s.activation(x116[:, par, 0, :, :], bank[par][:, 0:KD * N].rearrange("p (k n) -> p k n", k=KD), ACT.Copy).then_inc(a_xh, 1)

                def copy_raw(b, par, first):
                    ac.wait_ge(a_qf, b + 1)
                    ac.wait_ge(a_kf, b + 1)
                    if not first:
                        ac.wait_ge(a_red, b - 1)
                    for w, ps in ((0, bank[2 + par][:, 0:D]), (1, bank[4 + par][:, 0:D])):
                        if w:
                            ac.wait_ge(a_v, b + 1)
                        s.activation(sq[:, par, w, :], ps, ACT.Square, scale=1.0 / WSC)
                        ins = s.activation(raw[:, bass.ds(b, 1), w, :], ps.unsqueeze(1), ACT.Copy, scale=1.0 / WSC)
                    ins.then_inc(a_raw, 1)

                def ctx_high1(b, par, first):
                    ac.wait_ge(a_cf[par], (b - par) * 8 + 16)
                    if not first:
                        ac.wait_ge(a_kf, b - 1)
                    s.activation(c116[:, par, 0, :, :], c1f[:, par, :, :], ACT.Copy).then_inc(a_ch, 1)

                ctx_high1(0, 0, True)
                ctx_high1(1, 1, True)
                high1(0, 0)
                high1(1, 1)
                copy_raw(0, 0, True)
                copy_raw(1, 1, True)
                with ac.Fori(1, B // 2) as i:
                    for par in range(2):
                        ctx_high1(i * 2 + par, par, False)
                        high1(i * 2 + par, par)
                    for par in range(2):
                        copy_raw(i * 2 + par, par, False)
                ac.wait_ge(a_ms, 1)
                s.activation(ms[:, 1, :, :], ms[:, 0, :, :], ACT.Sqrt).then_inc(a_sq, 1)

                def seg_high(b, par, first):
                    ac.wait_ge(a_gn, b + 1)
                    if not first:
                        ac.wait_ge(a_tq, b - 1)
                        ac.wait_ge(a_tk, b - 1)
                    for w in range(2):
                        src = qn[:, par, w, :].rearrange("p (h d) -> p h d", h=H)
                        dst = seg[:, par, w, :, 0:2, :] if w == 0 else seg[:, par, w, :, 0:3:2, :]
                        ins = s.activation(dst, src.unsqueeze(2).to_broadcast([P, H, 2, HD]), ACT.Copy)
                    ins.then_inc(a_sh, 1)

                def copy_q(b, par):
                    ac.wait_ge(a_tq, b + 1)
                    s.activation(qT1[:, par, 0, :, :].rearrange("p c n -> p (c n)"), bank[2][:, :].bitcast(F16), ACT.Copy).then_inc(a_cq, 1)

                def take_o1(c, first):
                    ac.wait_ge(a_ot, c + 1)
                    if not first:
                        ac.wait_ge(a_op, c)
                    s.activation(OT1[:, :, :], bank[4][:, 0:KD * N].rearrange("p (k n) -> p k n", k=KD), ACT.Copy).then_inc(a_oc, 1)

                def exps1(b):
                    for g in range(NHG):
                        ac.wait_ge(a_st, 4 * b + g + 1)
                        s.activation(P1[:, HS * g:HS * g + HS, :], bank[g % 2][:, :].rearrange("p (h n) -> p h n", h=HS), ACT.Exp,
                                     scale=HD ** -0.5).then_inc(a_ex, 1)

                seg_high(0, 0, True)
                seg_high(1, 1, True)
                copy_q(0, 0)

                def iteration1(b, par, c, has_q, has_x):
                    if has_q:
                        copy_q(b + 1, 1 - par)
                    if has_x:
                        seg_high(b + 2, par, False)
                    if c:
                        take_o1(b - 1, c == 1)
                    exps1(b)

                iteration1(0, 0, 0, True, True)
                iteration1(1, 1, 1, True, True)
                with ac.Fori(0, B // 2 - 2) as i:
                    for par in range(2):
                        iteration1(i * 2 + 2 + par, par, 2, True, True)
                iteration1(B - 2, 0, 2, True, False)
                iteration1(B - 1, 1, 2, False, False)
                take_o1(B - 1, False)

            if stages > 3:
                ac.wait_ge(s_var, 4)
                s.activation(rstd_t[:, 1, :], rstd_t[:, 0, :], ACT.Sqrt).then_inc(s_sqrt, 1)

                def turned_m(b, par, first):
                    ac.wait_ge(m_xn, b + 1)
                    s.activation(xm16[:, bass.ds(b, 1), 0, :], xnm[:, par:par + 1, :], ACT.Copy).then_inc(m_xh, 1)
                    ac.wait_ge(m_xt, b + 1)
                    if not first:
                        ac.wait_ge(m_lg, b - 1)
                    s.activation(xTm[:, par, :, :], bank[par][:, 0:KD * N].rearrange("p (k n) -> p k n", k=KD), ACT.Copy).then_inc(m_xc, 1)

                turned_m(0, 0, True)
                turned_m(1, 1, True)
                with ac.Fori(1, B // 2) as i:
                    for par in range(2):
                        turned_m(i * 2 + par, par, False)
                ac.wait_ge(m_ex, 1)
                s.activation(ex[:, :, :], ex[:, :, :], ACT.Exp).then_inc(m_er, 1)

                def split_high(t, par, q, first):
                    if q == 0:
                        ac.wait_ge(m_bs, t + 1)
                        if not first:
                            ac.wait_ge(m_o, t - 1)
                    cut = WM // 3
                    s.activation(wm16[:, par, 0, q * cut:(q + 1) * cut], wsm[:, par, q * cut:(q + 1) * cut], ACT.Copy).then_inc(m_wh, 1)

                def expert_a(t, par, first, nxt):
                    for c in range(FC):
                        ac.wait_ge(m_h, FC * t + c + 1)
                        if not (first and c < 4):
                            ac.wait_ge(m_u, FC * t + c - 3)
                        s.activation(yg[:, c % 4, :], bank[c % 4][:, 0:MT], ACT.Gelu, bias=bms[:, par, c:c + 1]).then_inc(m_g, 1)
                        if c % 2 == 0 and c:
                            hidden_high(t, par, c // 2 - 1)
                        if nxt and c in (4, 5, 6):
                            split_high(t + 1, 1 - par, c - 4, first)
                    hidden_high(t, par, 3)

                def hidden_high(t, par, q):
                    ac.wait_ge(m_u, FC * t + 2 * q + 2)
                    s.activation(hm16[:, par, 0, 2 * q:2 * q + 2, :], hf[:, q % 2, :, :], ACT.Copy).then_inc(m_hh, 1)

                for q in range(3):
                    split_high(0, 0, q, True)
                expert_a(0, 0, True, True)
                expert_a(1, 1, False, True)
                expert_a(2, 0, False, True)
                with ac.Fori(0, (NT - 5) // 2) as i:
                    for q in range(2):
                        expert_a(i * 2 + 3 + q, 1 - q, False, True)
                expert_a(NT - 2, 1, False, True)
                expert_a(NT - 1, 0, False, False)

        @block.tensor
        def _(pe):
            t = nc.tensor

            def turn_xn(b, c):
                pe.wait_ge(s_xn, b + 1)
                if c is None:
                    if b:
                        pe.wait_ge(s_xh, b)
                        pe.wait_ge(s_xl, b)
                else:
                    pe.wait_ge(s_oc, c)
                for kk in range(KD):
                    ins = t.transpose(bank[6][:, kk * N:(kk + 1) * N], xn[:, kk * P:(kk + 1) * P], ident[:, :])
                ins.then_inc(s_xt, 1)

            PAIRS = [(0, 0), (0, 1), (1, 0)]

            def project_qk(b, par, first):
                pe.wait_ge(s_xh, b + 1)
                pe.wait_ge(s_xl, b + 1)
                for r in range(4):
                    w = r // 2
                    src = (xn16, ctx16)[w]
                    if r == 2:
                        pe.wait_ge(s_ch, b + 1)
                        pe.wait_ge(s_cl, b + 1)
                    if not (first and r < 2):
                        pe.wait_ge(s_qe, 6 * b + r - 1)
                    for c in range(HS):
                        col = (HS * (r % 2) + c) * P
                        n = 0
                        for (wp, xp) in PAIRS:
                            for kk in range(KD):
                                ins = t.matmul(bank[4 + r % 2][:, c * N:(c + 1) * N], wqkv16[:, w, wp, kk, col:col + P],
                                               src[:, par, xp, kk, :], start=(n == 0), stop=(n == 5))
                                n += 1
                    ins.then_inc(s_qf, 1)

            def project_v(b, par):
                for r in range(2):
                    pe.wait_ge(s_qe, 6 * b + 4 + r - 1)
                    n = 0
                    for (wp, xp) in PAIRS:
                        for kk in range(KD):
                            ins = t.matmul(bank[4 + r][:, :], ctx16[:, par, xp, kk, :], wqkv16[:, 2, wp, kk, 512 * r:512 * r + 512],
                                           start=(n == 0), stop=(n == 5))
                            n += 1
                    ins.then_inc(s_qf, 1)

            def row_scores(b, par, first):
                pe.wait_ge(s_qh, 4 * b + 4)
                for g in range(NHG):
                    if g < 2:
                        if not first:
                            pe.wait_ge(s_exp, 4 * b - 4 + 3 + g)
                    else:
                        pe.wait_ge(s_red, 4 * b + g - 1)
                    half = 64 * (g % 2)
                    for i in range(HS):
                        ch = HS * (g // 2) + i
                        ins = t.matmul(bank[g % 2][:, i * N:(i + 1) * N], q16[half:half + 64, par, 0, 0, ch, :],
                                       q16[half:half + 64, par, 1, 0, ch, :], start=True, stop=True)
                    ins.then_inc(s_sm, 1)

            def scores(b, par, g):
                if g < 2:
                    pe.wait_ge(s_red, 4 * b + 3 + g)
                else:
                    pe.wait_ge(s_exp, 4 * b + g - 1)
                if g == 0:
                    pe.wait_ge(s_red, 4 * b + 4)
                    pe.wait_ge(s_ql, 4 * b + 4)
                half = 64 * (g % 2)
                for i in range(HS):
                    ch = HS * (g // 2) + i
                    o = bank[g % 2][:, i * N:(i + 1) * N]
                    sl = HS * g + i
                    t.matmul(o, nmx[:, sl:sl + 1].to_broadcast([P, N]), ident16[:, :], start=True, stop=False)
                    for n, (qp, kp) in enumerate(PAIRS):
                        ins = t.matmul(o, q16[half:half + 64, par, 1, kp, ch, :], q16[half:half + 64, par, 0, qp, ch, :],
                                       start=False, stop=(n == 2))
                ins.then_inc(s_st, 1)

            def gate(b, g, first, grp):
                if g < 2:
                    if not first:
                        pe.wait_ge(s_pm, 8 * b - 8 + 6 + 2 * g)
                else:
                    pe.wait_ge(s_pm, 8 * b + 2 * g - 2)
                bk = bank[2 + g % 2]
                for n, (lp, rp) in enumerate(PAIRS):
                    t.matmul(bk[:, :], Rm16[:, bass.ds(b, 1), rp, :], Lw16[:, grp, lp, 2 * g:2 * g + 2, :], start=(n == 0), stop=(n == 2))
                for jj in range(2):
                    j = 2 * g + jj
                    for n, (wp, fp) in enumerate(PAIRS):
                        f = F[:, bass.ds(b, 1), fp * 512 + j * 64:fp * 512 + j * 64 + 64].bitcast(F16)
                        ins = t.matmul(bk[:, jj * 256:(jj + 1) * 256], f, We16[:, wp, :], start=False,
                                       stop=(n == 2), skip_group_check=True)
                ins.then_inc(s_gf, 1)

            def pv(c, par, first):
                pe.wait_ge(s_pm, 8 * c + 8)
                for f in range(4):
                    if f == 0:
                        pe.wait_ge(s_xh, xl_of(c))
                        pe.wait_ge(s_xl, xl_of(c))
                        pe.wait_ge(s_qe, 6 * c + 6)
                    elif f == 1:
                        if not first:
                            pe.wait_ge(s_opt, c)
                    else:
                        pe.wait_ge(s_oe, 4 * c + f - 1)
                    for i in range(HS):
                        sl = HS * f + i
                        ins = t.matmul(bank[6 + f % 2][:, i * (DK + 1):(i + 1) * (DK + 1)], PT[:, sl, :], vv[:, par, sl, :],
                                       start=True, stop=True)
                    ins.then_inc(s_of, 1)

            def xl_of(c):
                return xl_cap[0] if xl_cap[0] else c + 3

            xl_cap = [0]

            def turn_o(c):
                for r in range(2):
                    pe.wait_ge(s_oe, 4 * c + 3 + r)
                    for i in range(4):
                        ch = 4 * r + i
                        ins = t.transpose(bank[6 + r][:, i * N:(i + 1) * N], O[:, ch * P:(ch + 1) * P], ident[:, :])
                    ins.then_inc(s_ot, 1)

            def project_o(c):
                pe.wait_ge(s_oc, 2 * c + 2)
                for ch in range(CH):
                    ins = t.matmul(bank[7][:, 0:D], OT[:, ch, :], WoT[:, ch, :], start=(ch == 0), stop=(ch == CH - 1))
                ins.then_inc(s_op, 1)

            pe.wait_ge(s_pp, 3)
            pe.wait_ge(s_wlo, 3)
            pe.wait_ge(s_flo, B)
            pe.wait_ge(s_small, 1)
            pe.wait_ge(s_o, 64)
            turn_xn(0, None)
            turn_xn(1, None)
            project_qk(0, 0, True)
            project_v(0, 0)

            def iteration(b, par, c, has_q, has_x, grp):
                row_scores(b, par, c == 0)
                if c:
                    pv(b - 1, 1 - par, c == 1)
                if has_q:
                    project_qk(b + 1, 1 - par, False)
                if c:
                    turn_o(b - 1)
                if has_x:
                    turn_xn(b + 2, (None if c == 0 else 2 * b - 1))
                if has_q:
                    project_v(b + 1, 1 - par)
                if c:
                    project_o(b - 1)
                scores(b, par, 0)
                gate(b, 0, c == 0, grp)
                scores(b, par, 1)
                gate(b, 1, c == 0, grp)
                scores(b, par, 2)
                scores(b, par, 3)
                gate(b, 2, c == 0, grp)
                gate(b, 3, c == 0, grp)

            iteration(0, 0, 0, True, True, 0)
            iteration(1, 1, 1, True, True, 0)
            with pe.Fori(0, 3) as i:
                for par in range(2):
                    iteration(i * 2 + 2 + par, par, 2, True, True, 0)
            with pe.Fori(0, 3) as i:
                for par in range(2):
                    iteration(i * 2 + 8 + par, par, 2, True, True, 1)
            iteration(B - 2, 0, 2, True, False, 1)
            xl_cap[0] = B
            iteration(B - 1, 1, 2, False, False, 1)
            pv(B - 1, 1, False)
            turn_o(B - 1)
            project_o(B - 1)

            if stages > 1:
                pe.wait_ge(f_ld, 64)
                pe.wait_ge(s_qe, 6 * B)
                pe.wait_ge(s_opt, B)
                t.matmul(bank[4][0:RANK, 0:D], lowr[:, FF:FF + RANK], lowr[:, FF + RANK:], start=True, stop=True).then_inc(f_mp, 1)
                pe.wait_ge(f_m, 1)
                for r in range(FC // 2):
                    for i in range(2):
                        c = 2 * r + i
                        ins = t.matmul(bank[r][:, i * D:(i + 1) * D], lowr[:, c * P:(c + 1) * P], lowm[:, :], start=True, stop=True)
                    ins.then_inc(f_lp, 1)
                for r in range(4):
                    kk, fh = r // 2, r % 2
                    pe.wait_ge(f_low, FC // 2)
                    for i in range(4):
                        c = 4 * fh + i
                        ins = t.transpose(bank[r][:, i * P:(i + 1) * P], wfa[:, c, kk * P:(kk + 1) * P], ident[:, :])
                    ins.then_inc(f_tp, 1)
                for r in range(4):
                    pe.wait_ge(f_lo, r + 1)
                    for i in range(4):
                        c, kk = 2 * r + i // 2, i % 2
                        ins = t.transpose(bank[r][:, i * P:(i + 1) * P], wpa[:, kk, c * P:(c + 1) * P], ident[:, :])
                    ins.then_inc(f_tp, 1)
                for kk in range(KD):
                    ins = t.matmul(bank[4][:, kk * P:(kk + 1) * P], thr[:, 0, FC + kk:FC + kk + 1].to_broadcast([P, P]), ident[:, :],
                                   start=True, stop=True)
                ins.then_inc(f_sc, 1)
                pe.wait_ge(f_w2, 1)
                pe.wait_ge(f_hi, 8)

                def ffn_turn(g):
                    pe.wait_ge(f_xn, g + 1)
                    for kk in range(KD):
                        if g:
                            pe.wait_ge(f_xl, 2 * g - 1 + kk)
                        for i in range(GT):
                            ins = t.transpose(bank[4 + kk][:, i * N:(i + 1) * N], xng[:, g % 2, i, kk * P:(kk + 1) * P], ident[:, :])
                        ins.then_inc(f_xt, 1)

                def ffn_hidden(g):
                    pe.wait_ge(f_xh, 2 * g + 2)
                    pe.wait_ge(f_xl, 2 * g + 2)
                    for c in range(FC):
                        n = g * FC + c
                        if n > 3:
                            pe.wait_ge(f_r, n - 3)
                        m = 0
                        for (wp, xp) in PAIRS:
                            for kk in range(KD):
                                ins = t.matmul(bank[n % 4][:, :], W1T16[:, wp, kk, c * P:(c + 1) * P], xg16[:, g % 2, xp, kk, :],
                                               start=(m == 0), stop=(m == 5))
                                m += 1
                        ins.then_inc(f_h, 1)

                def ffn_out(g):
                    pe.wait_ge(f_l, FC * (g + 1))
                    for i in range(GT):
                        n = g * GT + i
                        if n > 1:
                            pe.wait_ge(f_ot, n - 1)
                        for m in range(2 * FC):
                            ins = t.matmul(bank[6 + n % 2][:, 0:D], h216[:, g % 2, m // FC, m % FC, i * N:(i + 1) * N], W2T16[:, m % FC, :],
                                           start=(m == 0), stop=(m == 2 * FC - 1))
                        ins.then_inc(f_o, 1)

                ffn_turn(0)
                for g in range(NG):
                    if g + 1 < NG:
                        ffn_turn(g + 1)
                    ffn_hidden(g)
                    if g:
                        ffn_out(g - 1)
                ffn_out(NG - 1)

            if stages > 2:
                pe.wait_ge(a_w, 1)
                pe.wait_ge(a_wl, 1)

                def turn1(b, par, first):
                    pe.wait_ge(a_xn, b + 1)
                    if not first:
                        pe.wait_ge(a_xh, b - 1)
                        pe.wait_ge(a_xl, b - 1)
                    for kk in range(KD):
                        ins = t.transpose(bank[par][:, kk * N:(kk + 1) * N], xn1[:, par, kk * P:(kk + 1) * P], ident[:, :])
                    ins.then_inc(a_xt, 1)

                def project1(b, par, first):
                    pe.wait_ge(a_xh, b + 1)
                    pe.wait_ge(a_xl, b + 1)
                    if not first:
                        pe.wait_ge(a_raw, b - 1)
                        pe.wait_ge(a_v, b - 1)
                    for src, bk, c0, c1, done in ((x116, bank[2 + par], 0, D, a_qf), (c116, bank[4 + par], D, 3 * D, a_kf)):
                        if done is a_kf:
                            pe.wait_ge(a_ch, b + 1)
                            pe.wait_ge(a_cl, b + 1)
                        n = 0
                        for (wp, xp) in PAIRS:
                            for kk in range(KD):
                                ins = t.matmul(bk[:, 0:c1 - c0], src[:, par, xp, kk, :], w1_16[:, wp, kk, c0:c1], start=(n == 0), stop=(n == 5))
                                n += 1
                        ins.then_inc(done, 1)

                turn1(0, 0, True)
                turn1(1, 1, True)
                project1(0, 0, True)
                project1(1, 1, True)
                with pe.Fori(1, B // 2) as i:
                    for par in range(2):
                        turn1(i * 2 + par, par, False)
                    for par in range(2):
                        project1(i * 2 + par, par, False)

                def turn_qk1(b, par, first):
                    for w, ready, done in ((0, a_cq, a_tq), (1, a_ck, a_tk)):
                        if w == 0:
                            pe.wait_ge(a_sh, b + 1)
                            pe.wait_ge(a_sl, b + 1)
                        if not first:
                            pe.wait_ge(ready, b)
                        bk = bank[2 + w][:, :].bitcast(F16)
                        for c in range(CH):
                            ins = t.transpose(bk[:, c * N:(c + 1) * N], seg[:, par, w, 2 * c:2 * c + 2, :, :].rearrange("p h s d -> p (h s d)"), ident16[:, :])
                        ins.then_inc(done, 1)

                def row_scores1(b, par, first):
                    pe.wait_ge(a_cq, b + 1)
                    pe.wait_ge(a_ck, b + 1)
                    for g in range(NHG):
                        if g < 2:
                            if not first:
                                pe.wait_ge(a_ex, 4 * b - 1 + g)
                        else:
                            pe.wait_ge(a_mx, 4 * b + g - 1)
                        half = 64 * (g % 2)
                        for i in range(HS):
                            ch = HS * (g // 2) + i
                            ins = t.matmul(bank[g % 2][:, i * N:(i + 1) * N], qT1[half:half + 64, par, 0, ch, :],
                                           qT1[half:half + 64, par, 1, ch, :], start=True, stop=True)
                        ins.then_inc(a_sm, 1)

                def scores1(b, par):
                    for g in range(NHG):
                        if g < 2:
                            pe.wait_ge(a_mx, 4 * b + 3 + g)
                        else:
                            pe.wait_ge(a_ex, 4 * b + g - 1)
                        half = 64 * (g % 2)
                        for i in range(HS):
                            ch = HS * (g // 2) + i
                            sl = HS * g + i
                            o = bank[g % 2][:, i * N:(i + 1) * N]
                            t.matmul(o, nmx1[:, sl:sl + 1].to_broadcast([P, N]), ident16[:, :], start=True, stop=False)
                            ins = t.matmul(o, qT1[half:half + 64, par, 1, ch, :], qT1[half:half + 64, par, 0, ch, :], start=False, stop=True)
                        ins.then_inc(a_st, 1)

                def pv1(c, first):
                    pe.wait_ge(a_ex, 4 * c + 4)
                    if not first:
                        pe.wait_ge(a_o, c)
                    for sl in range(H):
                        h = HEAD_OF[sl]
                        ins = t.matmul(bank[6][:, h * (HD + 1):(h + 1) * (HD + 1)], P1[:, sl, :],
                                       v1[:, bass.ds(c, 1), h, :], start=True, stop=True)
                    ins.then_inc(a_pv, 1)

                def turn_o1(c, first):
                    pe.wait_ge(a_o, c + 1)
                    if not first:
                        pe.wait_ge(a_oc, c)
                    for kk in range(KD):
                        ins = t.transpose(bank[4][:, kk * N:(kk + 1) * N], O1[:, kk * P:(kk + 1) * P], ident[:, :])
                    ins.then_inc(a_ot, 1)

                def project_o1(c, first):
                    pe.wait_ge(a_oc, c + 1)
                    if not first:
                        pe.wait_ge(a_xu, c)
                    for kk in range(KD):
                        ins = t.matmul(bank[5][:, 0:D], OT1[:, kk, :], wpr[:, kk, :], start=(kk == 0), stop=(kk == KD - 1))
                    ins.then_inc(a_op, 1)

                pe.wait_ge(a_raw, B)
                pe.wait_ge(a_v, B)
                turn_qk1(0, 0, True)

                def iteration1(b, par, c, has_q):
                    row_scores1(b, par, c == 0)
                    if c:
                        pv1(b - 1, c == 1)
                    if has_q:
                        turn_qk1(b + 1, 1 - par, False)
                    if c:
                        turn_o1(b - 1, c == 1)
                    scores1(b, par)
                    if c:
                        project_o1(b - 1, c == 1)

                iteration1(0, 0, 0, True)
                iteration1(1, 1, 1, True)
                with pe.Fori(0, B // 2 - 2) as i:
                    for par in range(2):
                        iteration1(i * 2 + 2 + par, par, 2, True)
                iteration1(B - 2, 0, 2, True)
                iteration1(B - 1, 1, 2, False)
                pv1(B - 1, False)
                turn_o1(B - 1, False)
                project_o1(B - 1, False)

            if stages > 3:
                pe.wait_ge(m_ld, 16)

                def turn_m(b, par, first):
                    pe.wait_ge(m_xn, b + 1)
                    if not first:
                        pe.wait_ge(m_xc, b - 1)
                    for kk in range(KD):
                        ins = t.transpose(bank[par][:, kk * N:(kk + 1) * N], xnm[:, par, kk * P:(kk + 1) * P], ident[:, :])
                    ins.then_inc(m_xt, 1)

                def logits(b, par):
                    pe.wait_ge(m_xc, b + 1)
                    for kk in range(KD):
                        ins = t.matmul(bank[7][:, bass.ds(b * E, E)], xTm[:, par, kk, :], rwt[:, kk, :], start=(kk == 0), stop=(kk == KD - 1))
                    ins.then_inc(m_lg, 1)

                turn_m(0, 0, True)
                turn_m(1, 1, True)
                logits(0, 0)
                logits(1, 1)
                with pe.Fori(1, B // 2) as i:
                    for par in range(2):
                        turn_m(i * 2 + par, par, False)
                    for par in range(2):
                        logits(i * 2 + par, par)
                pe.wait_ge(m_oh, 1)
                pe.wait_ge(m_c, 5)
                t.matmul(bank[6][:, 0:256], tri[:, :], oh16[:, :], start=True, stop=True)
                t.matmul(bank[6][:, 256:512], one16[:, :], oh16[:, :], start=True, stop=True).then_inc(m_pr, 1)

                def turn_tokens(t_, par, first):
                    pe.wait_ge(m_x[par], (t_ - par) * 8 + 16)
                    if not first:
                        pe.wait_ge(m_tc, t_)
                    bk = bank[4][:, :].bitcast(F16)
                    for a4 in range(2 * KD):
                        for h in range(MT // P):
                            ins = t.transpose(bk[:, a4 * MT + h * P:a4 * MT + (h + 1) * P], xin[:, par, h, a4 * P:(a4 + 1) * P], ident16[:, :])
                    ins.then_inc(m_tt, 1)

                def hidden(t_, par, c0, c1, first):
                    for c in range(c0, c1):
                        if c == 0:
                            pe.wait_ge(m_tc, t_ + 1)
                            pe.wait_ge(m_wl, 3 * t_ + 2)
                        if not (first and c < 4):
                            pe.wait_ge(m_u, FC * t_ + c - 3)
                        for w in range(2):
                            n = 0
                            for (wp, xp) in PAIRS:
                                for kk in range(KD):
                                    col = (w * KD + kk) * FF + c * P
                                    ins = t.matmul(bank[c % 4][:, w * MT:(w + 1) * MT], wm16[:, par, wp, col:col + P], xT16[:, par, xp * KD + kk, :],
                                                   start=(n == 0), stop=(n == 5))
                                    n += 1
                        ins.then_inc(m_h, 1)

                def expert_out(t_, par, first):
                    pe.wait_ge(m_hl, 4 * t_ + 4)
                    pe.wait_ge(m_wl, 3 * t_ + 3)
                    if not first:
                        pe.wait_ge(m_y, t_ - 1)
                    for h in range(MT // P):
                        n = 0
                        for (wp, xp) in PAIRS:
                            for c in range(FC):
                                col = 2 * KD * FF + c * D
                                ins = t.matmul(bank[5 + par][:, h * D:(h + 1) * D], hm16[:, par, xp, c, h * P:(h + 1) * P], wm16[:, par, wp, col:col + D],
                                               start=(n == 0), stop=(n == 3 * FC - 1))
                                n += 1
                    ins.then_inc(m_o, 1)

                def expert_p(t_, par, prev, nxt, first=False):
                    hidden(t_, par, 0, 2, first)
                    if prev:
                        expert_out(t_ - 1, 1 - par, prev == 1)
                    if nxt:
                        turn_tokens(t_ + 1, 1 - par, False)
                    hidden(t_, par, 2, 8, first)

                turn_tokens(0, 0, True)
                expert_p(0, 0, 0, True, True)
                expert_p(1, 1, 1, True)
                expert_p(2, 0, 1, True)
                with pe.Fori(0, (NT - 5) // 2) as i:
                    for q in range(2):
                        expert_p(i * 2 + 3 + q, 1 - q, 2, True)
                expert_p(NT - 2, 1, 2, True)
                expert_p(NT - 1, 0, 2, False)
                expert_out(NT - 1, 0, False)


def arrange(inputs):
    f = lambda n: np.asarray(inputs[n], np.float32)
    c = np.ascontiguousarray
    boxes = f("fside_BxSx4_0")
    heads = np.array(HEAD_OF)
    cols = (heads[:, None] * DK + np.arange(DK)[None, :]).reshape(-1)
    a = {"x": f("x"), "g_xattn": f("g_xattn"), "g_ffn": f("g_ffn")}
    a["ctxT"] = c(f("ctx_1024").reshape(T, D).T)
    lohi = boxes.reshape(B, NJ, NN, 2, 2)
    bn = lohi.transpose(4, 2, 0, 1, 3)
    a["boxn"] = c(np.broadcast_to(bn[:, None], (2, 4, NN, B, NJ, 2)).reshape(P, B * NJ, 2))
    a["boxm"] = c(boxes.reshape(T, 2, 2).transpose(2, 1, 0))
    delta = np.array([(s >> 1) & 1 if s < 8 else 0 for s in range(SLOTS)])
    wh = boxes.reshape(2, 8, N, 2, 2)[..., delta]
    a["whc"] = c(wh.transpose(1, 4, 0, 3, 2).reshape(P, 2, 2, N))
    Wg = f("L0_xattn_Wg")[heads]
    feat = lambda sc, dl, fr: Wg[:, sc * 8 + dl * 2 + fr]
    We = np.zeros((2, 2, 2, NN, H, NN), np.float32)
    for xy in range(2):
        for sc in range(2):
            for fr in range(2):
                for nn in range(NN):
                    We[xy, sc, fr, nn, :, nn] = feat(sc, xy, fr)
    a["We"] = We.reshape(P, H * NN)
    AB = np.zeros((SLOTS, 2, H), np.float32)
    for s in range(4):
        dl, fr = 2 + (s >> 1), s & 1
        AB[s, 0], AB[s, 1] = feat(1, dl, fr), feat(0, dl, fr)
        AB[4 + s, 0], AB[4 + s, 1] = feat(0, dl, fr), feat(1, dl, fr)
    AB[8, 1] = f("L0_xattn_bg")[heads]
    a["AB"] = c(np.broadcast_to(AB[None], (8, SLOTS, 2, H)).reshape(P, 2, H))
    turn = [100.0 / (1000.0 ** (fr / 2)) / (2 * np.pi) for fr in range(2)]
    cst = np.zeros((P, 8), np.float32)
    for p in range(P):
        sc, fr = (p >> 5) & 1, (p >> 4) & 1
        cst[p, 0], cst[p, 1] = turn[fr], 0.25 * sc
        s = p % SLOTS
        cst[p, 2] = turn[s & 1] if s < 8 else 0.0
        cst[p, 3], cst[p, 4], cst[p, 5] = 0.0, (-0.25 if s < 4 else 0.25), (0.0 if s < 4 else 0.25)
    a["cst"] = cst
    a["mask"] = c((np.arange(P)[:, None] // SLOTS == np.arange(8)[None, :]).astype(np.float32))
    a["wqkv"] = np.stack([f("L0_xattn_Wq").T, f("L0_xattn_Wk").T, f("L0_xattn_Wv")[cols].T])
    a["bqk"] = c(np.stack([f("L0_xattn_bq").reshape(CH, P).T, f("L0_xattn_bk").reshape(CH, P).T], 1))
    a["bv"] = c(f("L0_xattn_bv")[cols])
    a["woT"] = c(f("L0_xattn_Wo")[:, cols].T)
    a["bo"] = f("L0_xattn_bo")
    a["w_fc"], a["w_proj"] = f("L0_ffn_w_fc"), f("L0_ffn_w_proj")
    a["low"] = c(np.concatenate([f("L0_ffn_u").T, f("L0_ffn_fast_b").T, f("L0_ffn_v")], 1))
    a["wq1"], a["wkv1"], a["wpr1"] = f("L1_xattn_Wq"), f("L1_xattn_Wkv"), f("L1_xattn_Wproj")
    a["gq"], a["gk"] = np.tile(f("L1_xattn_q_gamma"), H), np.tile(f("L1_xattn_k_gamma"), H)
    a["rwt"] = c(f("L1_ffn_router_w").T)
    turned = lambda n: f(n).transpose(0, 2, 1).reshape(E, KD, P, FF).transpose(0, 2, 1, 3).reshape(E, P, KD * FF)
    down = f("L1_ffn_w2_w").transpose(0, 2, 1).reshape(E, FC, P, D).transpose(0, 2, 1, 3).reshape(E, P, FC * D)
    bias = lambda n: f(n).reshape(E, FC, P).transpose(0, 2, 1)
    a["wcat"] = c(np.concatenate([turned("L1_ffn_wg_w"), turned("L1_ffn_w1_w"), down, bias("L1_ffn_wg_b"), bias("L1_ffn_w1_b")], 2))
    a["b2"] = f("L1_ffn_w2_b")
    a["fgate"] = f("L0_ffn_gate").reshape(1)
    return a


def kernel(**inputs):
    import concourse.bacc as bacc
    from concourse.bass_utils import run_bass_kernel_spmd

    nc = bacc.Bacc("TRN2", target_bir_lowering=False, num_devices=1)
    arrays = {f"in_{n}": np.ascontiguousarray(v) for n, v in arrange(inputs).items()}
    aps = {n[3:]: nc.dram_tensor(n, v.shape, mybir.dt.from_np(v.dtype), kind="ExternalInput").ap() for n, v in arrays.items()}
    aps["out"] = nc.dram_tensor("out_x", (B, N, D), F32, kind="ExternalOutput").ap()
    build(nc, aps)
    r = run_bass_kernel_spmd(nc, [arrays], core_ids=[0])
    return r.results[0]["out_x"]
```

```python
from contextlib import ExitStack

import numpy as np
import concourse.bass as bass
from concourse import mybir

ALU = mybir.AluOpType
ACT = mybir.ActivationFunctionType
AX = mybir.AxisListType
F32 = mybir.dt.float32
F16 = mybir.dt.float16
I32 = mybir.dt.int32
U32 = mybir.dt.uint32

P = 128
B = 16
N = 128
D = 256
T = B * N
KD = D // P
H = 16
DK = 64
HD = D // H
CH = H * DK // P
NN = 16
NJ = N // NN
HS = 4
NHG = H // HS
SLOTS = 16
GSC = 1024.0
WSC = 64.0
FF = 1024
FC = FF // P
E = 8
MT = 256
NT = (2 * T + E * (MT - 1)) // MT
WM = 2 * KD * FF + FC * D
HC = WM // 2
NSP = 3
WB = WM + 2 * FC
GT = 4
NG = B // GT
RANK = 16
ROUND = 12582912.0
TWO_PI = 6.2831845

HEAD_OF = [8 * (g // 2) + 2 * i + g % 2 for g in range(NHG) for i in range(HS)]


class Count:

    def __init__(self, sem):
        self.sem, self.n = sem, 0

    def up(self, ins):
        ins.then_inc(self.sem, 1)
        self.n += 1
        return self.n


def build(nc, a, dbg=None):
    stages = {"x1": 1, "x2": 2, "x3": 3}.get(dbg, 4)
    with ExitStack() as ctx:
        def sem(name):
            return ctx.enter_context(nc.semaphore(name))

        def sb(name, shape, dt=F32, scope=None):
            return (scope or ctx).enter_context(nc.sbuf_tensor(name, shape, dt))

        bank = [ctx.enter_context(nc.psum_tensor(f"bank{i}", [P, 512], F32)) for i in range(8)]

        X = sb("X", [P, B, D])
        mv = sb("mv", [P, B, 2])
        bst = sb("bst", [P, B, 6])
        rstd = sb("rstd", [P, B])
        rstd_t = sb("rstd_t", [P, 3, B])
        ident = sb("ident", [P, P])
        ident16 = sb("ident16", [P, P], F16)
        gates = sb("gates", [P, 4])
        tg = sb("tg", [P, 4])
        xn = sb("xn", [P, D])

        zero = sb("zero", [P, 2 * D], F16)

        l0 = ExitStack()
        fu = sb("fu", [P, NJ * N], F32, l0)
        fk = sb("fk", [P, NJ * N], F32, l0)
        fs = sb("fs", [P, NJ * N], F32, l0)
        F16s = sb("F16s", [P, 2, 2, NJ * N], F16, l0)
        cm = sb("cm", [P, T], F32, l0)
        cn = sb("cn", [P, B * NJ], F32, l0)
        rw = sb("rw", [P, B * NJ], F32, l0)
        cst = sb("cst", [P, 8], F32, l0)
        Lw16 = sb("Lw16", [P, 2, 2, NJ, H * NN], F16, l0)
        Rm16 = sb("Rm16", [P, B, 2, N], F16, l0)
        We = sb("We", [P, H * NN], F32, l0)
        We16 = sb("We16", [P, 2, H * NN], F16, l0)
        wqkv16 = sb("wqkv16", [P, 3, 2, KD, H * DK], F16, l0)
        WoT = sb("WoT", [P, CH, D], F32, l0)
        bqk = sb("bqk", [P, 2, CH], F32, l0)
        bv = sb("bv", [P, H * DK], F32, l0)
        bo = sb("bo", [P, D], F32, l0)
        att = ExitStack()
        q16 = sb("q16", [P, 2, 2, 2, CH, N], F16, att)
        qt = sb("qt", [P, 4, HS, N], F32, att)
        vf = sb("vf", [P, 2, 8, DK], F32, att)
        vv16 = sb("vv16", [P, 2, 2, H, DK + 1], F16, att)
        ctxf = sb("ctxf", [P, 2, KD, N], F32, att)
        ctx16 = sb("ctx16", [P, 2, 2, KD, N], F16, att)
        xn16 = sb("xn16", [P, 2, 2, KD, N], F16, att)
        nmx = sb("nmx", [P, H], F16, att)
        rden = sb("rden", [P, 2, HS], F32, att)
        otmp = sb("otmp", [P, D], F32, att)
        pre = ExitStack()
        rows = sb("rows", [P, 2, T], F32, pre)
        boxn = sb("boxn", [P, B * NJ, 2], F32, pre)
        whc = sb("whc", [P, 2, 2, N], F32, pre)
        wha = sb("wha", [P, 2, N], F32, pre)
        wht = sb("wht", [P, 3, 2, N], F32, pre)
        whk = sb("whk", [P, 3, 2, N], F32, pre)
        AB = sb("AB", [P, 2, H], F32, pre)
        mask = sb("mask", [P, 8], F32, pre)
        Lt = sb("Lt", [P, 2, NJ, H * NN], F32, pre)
        wst = [Lt[:, r, :, :].rearrange("p j c -> p (j c)").rearrange("p (k f) -> p k f", k=KD) for r in range(2)]
        pre.close()
        EX = sb("EX", [P, H, N], F32, att)
        PT = sb("PT", [P, H, N], F32, att)
        PT16 = sb("PT16", [P, 2, H, N], F16, att)
        O = sb("O", [P, H * DK], F32, att)
        OT = sb("OT", [P, CH, N], F32, att)
        att.close()
        l0.close()

        l1w = ExitStack()
        wst1 = sb("wst1", [P, KD, 3 * D], F32, l1w)
        w1_16 = sb("w1_16", [P, 2, KD, 3 * D], F16, l1w)
        wpr = sb("wpr", [P, KD, D], F32, l1w)
        gam = sb("gam", [P, 2, D], F32, l1w)
        ws = sb("ws", [P, 2, HC], F32, l1w)
        ws16 = sb("ws16", [P, 2, 2, HC], F16, l1w)

        l0f = ExitStack()
        W1T16 = sb("W1T16", [P, 2, KD, FF], F16, l0f)
        W2T16 = sb("W2T16", [P, FC, D], F16, l0f)
        w2row = sb("w2row", [P, D], F32, l0f)
        xg16 = sb("xg16", [P, 2, 2, KD, GT * N], F16, l0f)
        hr = sb("hr", [P, 2, GT * N], F32, l0f)
        h2 = sb("h2", [P, 2, GT * N], F32, l0f)
        h216 = sb("h216", [P, 2, 2, FC, GT * N], F16, l0f)
        xng = sb("xng", [P, 2, GT, D], F32, l0f)
        ftmp = sb("ftmp", [P, 2, D], F32, l0f)
        fpre = ExitStack()
        wfc = sb("wfc", [P, FC, D], F32, fpre)
        wfa = sb("wfa", [P, FC, D], F32, fpre)
        wfb = sb("wfb", [P, FC, D], F32, fpre)
        wpj = sb("wpj", [P, KD, FF], F32, fpre)
        wpa = sb("wpa", [P, KD, FF], F32, fpre)
        thr = sb("thr", [P, 4, FC + KD], F32, fpre)
        lowr = sb("lowr", [RANK, FF + RANK + D], F32, fpre)
        lowm = sb("lowm", [RANK, D], F32, fpre)
        fgate = sb("fgate", [P, 1], F32, fpre)
        fpre.close()
        l0f.close()

        l1 = ExitStack()
        raw = sb("raw", [P, B, 2, D], F32, l1)
        v1 = sb("v1", [P, B, 2, H, HD + 1], F16, l1)
        ms = sb("ms", [P, 4, B, 2 * H], F32, l1)
        sq = sb("sq", [P, 2, 2, D], F32, l1)
        xn1 = sb("xn1", [P, 2, D], F32, l1)
        x116 = sb("x116", [P, 2, 2, KD, N], F16, l1)
        c1f = sb("c1f", [P, 2, KD, N], F32, l1)
        c116 = sb("c116", [P, 2, 2, KD, N], F16, l1)
        qn = sb("qn", [P, 2, 2, D], F32, l1)
        seg = sb("seg", [P, 2, 2, H, 4, HD], F16, l1)
        qT1 = sb("qT1", [P, 2, 2, CH, N], F16, l1)
        P1 = sb("P1", [P, H, N], F32, l1)
        P116 = sb("P116", [P, 2, H, N], F16, l1)
        O1 = sb("O1", [P, D], F32, l1)
        OT1 = sb("OT1", [P, KD, N], F32, l1)
        rden1 = sb("rden1", [P, H], F32, l1)
        nmx1 = sb("nmx1", [P, H], F16, l1)
        l1.close()
        l1w.close()

        mo = ExitStack()
        rwt = sb("rwt", [P, KD, E], F32, mo)
        xnm = sb("xnm", [P, 2, D], F32, mo)
        xm16 = sb("xm16", [P, B, 2, D], F16, mo)
        xTm = sb("xTm", [P, 2, KD, N], F32, mo)
        lg = sb("lg", [P, B, E], F32, mo)
        top = sb("top", [P, B, 8], F32, mo)
        topi = sb("topi", [P, B, 8], U32, mo)
        ex = sb("ex", [P, B, E + 1], F32, mo)
        den = sb("den", [P, 2, B], F32, mo)
        wk = sb("wk", [P, 2, B], F32, mo)
        idf = sb("idf", [P, B, 2], F32, mo)
        oh = sb("oh", [P, E, B * 2], F32, mo)
        oh16 = sb("oh16", [P, E * B * 2], F16, mo)
        tot = sb("tot", [P, E * B * 2], F32, mo)
        cum = sb("cum", [P, E * B * 2], F32, mo)
        pos = sb("pos", [P, E, B * 2], F32, mo)
        one = sb("one", [P, E * B * 2], F32, mo)
        cnt = sb("cnt", [P, 6, E], F32, mo)
        slotf = sb("slotf", [P, B * 2], F32, mo)
        slot = sb("slot", [P, B * 2], U32, mo)
        tri = sb("tri", [P, P], F16, mo)
        one16 = sb("one16", [P, P], F16, mo)
        ioe = sb("ioe", [P, E], F32, mo)
        iot = sb("iot", [P, NT], F32, mo)
        cmp = sb("cmp", [P, NT, E], F32, mo)
        etf = sb("etf", [P, NT], F32, mo)
        eti = sb("eti", [P, NT], I32, mo)
        chg = sb("chg", [P, NT], I32, mo)
        wm16 = sb("wm16", [P, 2, 2, WM], F16, mo)
        bms = sb("bms", [P, 2, 2 * FC], F32, mo)
        b2r = sb("b2r", [P, 2, D], F32, mo)
        xin = sb("xin", [P, 2, MT // P, 2 * D], F16, mo)
        xT16 = sb("xT16", [P, 2, 2 * KD, MT], F16, mo)
        yg = sb("yg", [P, 4, MT], F32, mo)
        hf = sb("hf", [P, 2, 2, MT], F32, mo)
        hm16 = sb("hm16", [P, 2, 2, FC, MT], F16, mo)
        ys = sb("ys", [P, 2, MT // P, D], F32, mo)
        yk = sb("yk", [P, 4, D], F32, mo)
        mo.close()
        w16_dram = nc.dram_tensor("expert_weights", [E, P, 2, WM], F16)
        xs_dram = nc.dram_tensor("expert_tokens", [NT * MT, 2 * D], F16)
        ys_dram = nc.dram_tensor("expert_outputs", [NT * MT, D], F32)

        s_var, s_sqrt = sem("var_ready"), sem("sqrt_ready")
        s_whv, s_wha = sem("sizes_vector"), sem("sizes_scalar")
        s_tg = sem("tanh_ready")
        s_x, s_c, s_cw = sem("x_loaded"), sem("consts_loaded"), sem("gate_inputs_loaded")
        s_w, s_wfree = [sem("weight_staged_even"), sem("weight_staged_odd")], sem("weight_split")
        s_wlo = sem("weight_split_lo")
        s_o = sem("out_weights_loaded")
        s_pv, s_pp = sem("prefix_vector"), sem("prefix_pool")
        s_fv, s_fa, s_fhi, s_flo = (sem("gate_" + n) for n in ("vector", "scalar", "high", "low"))
        s_xn, s_xt, s_xh, s_xl = sem("xn_ready"), sem("xn_turned"), sem("xn_high"), sem("xn_low")
        s_cf, s_ch, s_cl = [sem("ctx_loaded_even"), sem("ctx_loaded_odd")], sem("ctx_high"), sem("ctx_low")
        s_qf, s_qe, s_qh, s_ql = sem("qkv_full"), sem("qkv_taken"), sem("qk_high"), sem("qk_low")
        s_sm, s_red = sem("row_scores"), sem("row_max")
        s_st, s_exp = sem("scores_full"), sem("exp_done")
        s_gf, s_pm, s_ph, s_pl = sem("gate_full"), sem("probs_ready"), sem("probs_high"), sem("probs_low")
        s_vh, s_vl = sem("values_high"), sem("values_low")
        s_of, s_rd, s_oe = sem("pv_full"), sem("den_inverse"), sem("pv_taken")
        s_ot, s_oc = sem("o_turned"), sem("o_turned_taken")
        s_op, s_opt, s_xu, s_bs, s_bn = sem("proj_full"), sem("proj_taken"), sem("x_updated"), sem("bn_stats_done"), sem("stats_ready")
        s_out = sem("stored")
        f_ld, f_w, f_m, f_lp, f_low, f_tp, f_hi, f_lo = (sem("ffn_" + n) for n in (
            "weights_loaded", "ternary_ready", "product_ready", "low_rank_full", "low_rank_added", "weights_turned",
            "weights_high", "weights_low"))
        f_mp = sem("ffn_small_full")
        f_xn, f_xt, f_xh, f_xl = (sem("ffn_" + n) for n in ("xn_ready", "xn_turned", "xn_high", "xn_low"))
        f_h, f_r, f_sq, f_h2, f_l = (sem("ffn_" + n) for n in ("hidden_full", "relu_done", "square_high", "square_done", "square_low"))
        m_ld, m_zf = sem("router_loaded"), sem("slots_zeroed")
        m_xn, m_xt, m_xc, m_xh, m_xl = (sem("router_" + n) for n in ("xn_ready", "xn_turned", "xn_copied", "xn_high", "xn_low"))
        m_lg, m_ex, m_er, m_pr, m_sl, m_c = (sem("route_" + n) for n in (
            "logits_full", "exponents_then_onehot_ready", "exp_done", "counts_full", "slots_ready", "constants_ready"))
        m_v = sem("route_vector")
        m_sc = sem("tokens_scattered")
        m_w = [sem("expert_weights_even"), sem("expert_weights_odd")]
        m_x = [sem("expert_tokens_even"), sem("expert_tokens_odd")]
        m_wd = [sem("expert_down_even"), sem("expert_down_odd")]
        w_ld = [sem("half_expert_loaded_even"), sem("half_expert_loaded_odd")]
        w_hi, w_lo = sem("half_expert_high"), sem("half_expert_low")
        w_st = [sem("half_expert_stored_even"), sem("half_expert_stored_odd")]
        m_tt, m_tc = sem("expert_tokens_turned"), sem("expert_tokens_copied")
        m_h, m_g, m_u, m_hh, m_hl = (sem("expert_" + n) for n in ("hidden_full", "gelu_done", "product_done", "hidden_high", "hidden_low"))
        m_o, m_y = sem("expert_out_full"), sem("expert_out_taken")
        m_ys = [sem("expert_stored_even"), sem("expert_stored_odd")]
        m_gk = [sem(f"gathered_{i}") for i in range(4)]
        m_f = sem("x_final")
        a_ld, a_w, a_wl = (sem("l1_" + n) for n in ("weights_loaded", "weights_high", "weights_low"))
        a_xn, a_xt, a_xh, a_xl = (sem("l1_" + n) for n in ("xn_ready", "xn_turned", "xn_high", "xn_low"))
        a_cf = [sem("l1_ctx_loaded_even"), sem("l1_ctx_loaded_odd")]
        a_ch, a_cl = sem("l1_ctx_high"), sem("l1_ctx_low")
        a_qf, a_kf, a_raw, a_red, a_v = (sem("l1_" + n) for n in ("q_full", "kv_full", "raw_copied", "squares_summed", "v_copied"))
        a_ms, a_sq = sem("l1_mean_ready"), sem("l1_root_ready")
        a_qn, a_gn, a_sh, a_sl = (sem("l1_" + n) for n in ("qk_scaled", "k_gamma_done", "segments_high", "segments_low"))
        a_tq, a_tk, a_cq, a_ck = (sem("l1_" + n) for n in ("q_turned", "k_turned", "q_copied", "k_copied"))
        a_sm, a_mx, a_st, a_ex, a_ph, a_pl = (sem("l1_" + n) for n in ("row_scores", "row_max", "scores_full", "exp_done", "probs_high", "probs_low"))
        a_pv, a_rd, a_o, a_ot, a_oc, a_op, a_xu = (sem("l1_" + n) for n in (
            "pv_full", "den_inverse", "pv_taken", "o_turned", "o_turned_taken", "proj_full", "x_updated"))
        f_o, f_ot, f_xu = sem("ffn_out_full"), sem("ffn_out_taken"), sem("ffn_x_updated")

        block = ctx.enter_context(nc.Block())

        @block.sync
        def _(sp):
            sp.dma_start(boxn[:, :, :], a["boxn"]).then_inc(s_cw, 16)
            for xy in range(2):
                for e in range(2):
                    sp.dma_start(rows[64 * xy:64 * xy + 64, e, :], a["boxm"][xy, e, :].partition_broadcast(64)).then_inc(s_cw, 16)
            sp.dma_start(cst[:, :], a["cst"]).then_inc(s_cw, 16)
            sp.dma_start(whc[:, :, :, :], a["whc"]).then_inc(s_cw, 16)
            sp.dma_start(AB[:, :, :], a["AB"]).then_inc(s_cw, 16)
            sp.dma_start(mask[:, :], a["mask"]).then_inc(s_cw, 16)
            sp.dma_start(We[:, :], a["We"]).then_inc(s_cw, 16)
            for j in range(3):
                if j == 2:
                    sp.wait_ge(s_wfree, 1)
                    sp.wait_ge(s_wlo, 1)
                sp.dma_start(wst[j % 2], a["wqkv"][j].rearrange("(k p) f -> p k f", p=P)).then_inc(s_w[j % 2], 16)

            def load_ctx(b, par):
                sp.dma_start(ctxf[:, par, :, :], a["ctxT"][:, bass.ds(b * N, N)].rearrange("(k p) n -> p k n", p=P)).then_inc(s_cf[par], 16)

            load_ctx(0, 0)
            load_ctx(1, 1)
            sp.dma_start(bqk[:, :, :], a["bqk"]).then_inc(s_o, 16)
            sp.dma_start(bv[:, :], a["bv"].partition_broadcast(P)).then_inc(s_o, 16)
            sp.dma_start(bo[:, :], a["bo"].partition_broadcast(P)).then_inc(s_o, 16)
            sp.dma_start(WoT[:, :, :], a["woT"].rearrange("(c p) f -> p c f", p=P)).then_inc(s_o, 16)
            with sp.Fori(0, B // 2 - 1) as i:
                for par in range(2):
                    b = i * 2 + par
                    sp.wait_ge(s_ch, b + 1)
                    sp.wait_ge(s_cl, b + 1)
                    load_ctx(b + 2, par)
            if stages > 1:
                sp.wait_ge(s_op, B)
                sp.wait_ge(s_xu, B)
                sp.wait_ge(s_oc, 2 * B)
                sp.wait_ge(s_ql, 4 * B)
                sp.wait_ge(s_cl, B)
                sp.dma_start(wfc[:, :, :], a["w_fc"].rearrange("(c p) d -> p c d", p=P)).then_inc(f_ld, 16)
                sp.dma_start(wpj[:, :, :], a["w_proj"].rearrange("(c p) f -> p c f", p=P)).then_inc(f_ld, 16)
                sp.dma_start(lowr[:, :], a["low"]).then_inc(f_ld, 16)
                sp.dma_start(fgate[:, :], a["fgate"].partition_broadcast(P)).then_inc(f_ld, 16)
            if stages > 2:
                sp.dma_start(wst1[:, :, 0:D], a["wq1"].rearrange("(k p) f -> p k f", p=P)).then_inc(a_ld, 16)
                sp.dma_start(wst1[:, :, D:], a["wkv1"].rearrange("(k p) f -> p k f", p=P)).then_inc(a_ld, 16)
                sp.dma_start(wpr[:, :, :], a["wpr1"].rearrange("(k p) f -> p k f", p=P)).then_inc(a_ld, 16)
                sp.dma_start(gam[:, 0, :], a["gq"].partition_broadcast(P)).then_inc(a_ld, 16)
                sp.dma_start(gam[:, 1, :], a["gk"].partition_broadcast(P)).then_inc(a_ld, 16)
                sp.wait_ge(f_xu, B)

                def load_ctx1(b, par):
                    sp.dma_start(c1f[:, par, :, :], a["ctxT"][:, bass.ds(b * N, N)].rearrange("(k p) n -> p k n", p=P)).then_inc(a_cf[par], 16)

                load_ctx1(0, 0)
                load_ctx1(1, 1)
                with sp.Fori(0, B // 2 - 1) as i:
                    for par in range(2):
                        b = i * 2 + par
                        sp.wait_ge(a_ch, b + 1)
                        sp.wait_ge(a_cl, b + 1)
                        load_ctx1(b + 2, par)
            if stages > 3:
                def store_half(e, half):
                    sp.wait_ge(w_hi, (e * 2 + half) * NSP + NSP)
                    sp.wait_ge(w_lo, (e * 2 + half) * NSP + NSP)
                    sp.dma_start(w16_dram.ap()[bass.ds(e, 1), :, :, half * HC:(half + 1) * HC].rearrange("o p r c -> (o p) r c"), ws16[:, half, :, :]).then_inc(w_st[half], 16)

                def load_half(e, half):
                    sp.dma_start(ws[:, half, :], a["wcat"][bass.ds(e, 1), :, half * HC:(half + 1) * HC].rearrange("o p c -> (o p) c")).then_inc(w_ld[half], 16)

                load_half(0, 0)
                load_half(0, 1)
                with sp.Fori(0, E - 1) as e:
                    for half in range(2):
                        store_half(e, half)
                        load_half(e + 1, half)
                store_half(E - 1, 0)
                store_half(E - 1, 1)
                sp.wait_ge(a_xu, B)
                sp.wait_ge(a_op, B)
                sp.wait_ge(w_st[0], 16 * E)
                sp.wait_ge(w_st[1], 16 * E)
                sp.dma_start(rwt[:, :, :], a["rwt"].rearrange("(k p) e -> p k e", p=P)).then_inc(m_ld, 16)
                sp.wait_ge(m_sl, 2)

                def load_hidden(t, par, first):
                    e = sp.value_load(eti[0:1, bass.ds(t, 1)], min_val=0, max_val=E - 1)
                    new = sp.value_load(chg[0:1, bass.ds(t, 1)], min_val=0, max_val=1)
                    if not first:
                        sp.wait_ge(m_u, FC * (t - 1))
                    sp.dma_start(wm16[:, par, :, 0:2 * KD * FF], w16_dram.ap()[bass.ds(e, 1), :, :, 0:2 * KD * FF].rearrange("o p r c -> (o p) r c"),
                                 cond=new).then_inc(m_w[par], 16)
                    sp.dma_start(bms[:, par, :], a["wcat"][bass.ds(e, 1), :, WM:WB].rearrange("o p c -> (o p) c")).then_inc(m_w[par], 16)

                def load_down(t, par, first):
                    e = sp.value_load(eti[0:1, bass.ds(t, 1)], min_val=0, max_val=E - 1)
                    new = sp.value_load(chg[0:1, bass.ds(t, 1)], min_val=0, max_val=1)
                    if not first:
                        sp.wait_ge(m_y, t - 1)
                    sp.dma_start(wm16[:, par, :, 2 * KD * FF:], w16_dram.ap()[bass.ds(e, 1), :, :, 2 * KD * FF:].rearrange("o p r c -> (o p) r c"),
                                 cond=new).then_inc(m_wd[par], 16)
                    sp.dma_start(b2r[:, par, :], a["b2"][bass.ds(e, 1), :].rearrange("o c -> (o c)").partition_broadcast(P)).then_inc(m_wd[par], 16)

                def load_tokens(t, par, first):
                    if not first:
                        sp.wait_ge(m_tt, t - 1)
                    sp.dma_start(xin[:, par, :, :], xs_dram.ap()[bass.ds(t * MT, MT), :].rearrange("(h p) c -> p h c", p=P)).then_inc(m_x[par], 16)

                def store(t, par):
                    sp.wait_ge(m_y, t + 1)
                    sp.dma_start(ys_dram.ap()[bass.ds(t * MT, MT), :].rearrange("(h p) c -> p h c", p=P), ys[:, par, :, :]).then_inc(m_ys[par], 16)

                load_hidden(0, 0, True)
                load_down(0, 0, True)
                load_hidden(1, 1, True)
                load_down(1, 1, True)
                sp.wait_ge(m_sc, 16 * 2 * B)
                load_tokens(0, 0, True)
                load_tokens(1, 1, True)
                load_tokens(2, 0, False)
                load_hidden(2, 0, False)
                with sp.Fori(0, (NT - 3) // 2) as i:
                    for par in (1, 0):
                        t = i * 2 + 2 - par
                        load_tokens(t + 2, par, False)
                        store(t - 1, 1 - par)
                        load_down(t + 1, 1 - par, False)
                        load_hidden(t + 2, par, False)
                store(NT - 3, 0)
                load_down(NT - 1, 0, False)
                store(NT - 2, 1)
                store(NT - 1, 0)
                sp.wait_ge(m_f, B)
                sp.dma_start(a["out"].rearrange("b n d -> n b d"), X[:, :, :]).then_inc(s_out, 16)
                sp.wait_ge(s_out, 16)
            if dbg == "x3":
                sp.wait_ge(a_xu, B)
                sp.dma_start(a["out"].rearrange("b n d -> n b d"), X[:, :, :]).then_inc(s_out, 16)
                sp.wait_ge(s_out, 16)
            if dbg == "x2":
                sp.wait_ge(f_xu, B)
                sp.dma_start(a["out"].rearrange("b n d -> n b d"), X[:, :, :]).then_inc(s_out, 16)
                sp.wait_ge(s_out, 16)
            if dbg == "x1":
                sp.wait_ge(s_xu, B)
                sp.dma_start(a["out"].rearrange("b n d -> n b d"), X[:, :, :]).then_inc(s_out, 16)
                sp.wait_ge(s_out, 16)

        @block.gpsimd
        def _(gp):
            pc = Count(s_pp)
            pc.up(nc.gpsimd.memset(ident[:, :], 0.0))
            gp.wait_ge(s_pp, 1)
            n = pc.up(nc.gpsimd.affine_select(out=ident[:, :], in_=ident[:, :], compare_op=ALU.not_equal, fill=1.0,
                                              base=0, pattern=[[-1, P]], channel_multiplier=1))
            gp.wait_ge(s_pp, n)
            pc.up(nc.gpsimd.tensor_copy(ident16[:, :], ident[:, :]))
            nc.gpsimd.memset(zero[:, :], 0.0).then_inc(m_c, 1)
            gp.wait_ge(m_c, 1)
            gp.dma_start(xs_dram.ap().rearrange("(a p) c -> p a c", p=P), zero[:, :].unsqueeze(1).to_broadcast([P, NT * MT // P, 2 * D])).then_inc(m_zf, 16)
            def split_ctx(b, par):
                gp.wait_ge(s_ch, b + 1)
                nc.gpsimd.tensor_tensor(ctx16[:, par, 1, :, :], ctxf[:, par, :, :], ctx16[:, par, 0, :, :], ALU.subtract).then_inc(s_cl, 1)

            def split_qk(b, par):
                for r in range(4):
                    w, g = r // 2, r % 2
                    hi = q16[:, par, w, 0, HS * g:HS * g + HS, :]
                    gp.wait_ge(s_qh, 4 * b + r + 1)
                    nc.gpsimd.tensor_tensor(q16[:, par, w, 1, HS * g:HS * g + HS, :], qt[:, r, :, :], hi, ALU.subtract).then_inc(s_ql, 1)

            def split_v(b, par):
                for r in range(2):
                    gp.wait_ge(s_vh, 2 * b + r + 1)
                    nc.gpsimd.tensor_tensor(vv16[:, par, 1, 8 * r:8 * r + 8, 0:DK], vf[:, r, :, :], vv16[:, par, 0, 8 * r:8 * r + 8, 0:DK], ALU.subtract).then_inc(s_vl, 1)

            def feature_low(n, par):
                gp.wait_ge(s_fhi, n + 1)
                nc.gpsimd.tensor_tensor(F16s[:, par, 1, :], fs[:, :], F16s[:, par, 0, :], ALU.subtract).then_inc(s_flo, 1)

            def probs_low(c):
                for g in range(4):
                    gp.wait_ge(s_ph, 4 * c + g + 1)
                    nc.gpsimd.tensor_tensor(PT16[:, 1, HS * g:HS * g + HS, :], PT[:, HS * g:HS * g + HS, :],
                                            PT16[:, 0, HS * g:HS * g + HS, :], ALU.subtract).then_inc(s_pl, 1)

            split_ctx(0, 0)
            split_ctx(1, 1)
            split_qk(0, 0)
            split_v(0, 0)
            feature_low(0, 0)

            def iteration(b, par, c, has_q, has_x):
                if c:
                    probs_low(b - 1)
                if has_q:
                    split_qk(b + 1, 1 - par)
                    split_v(b + 1, 1 - par)
                if has_x:
                    split_ctx(b + 2, par)
                if has_q:
                    feature_low(b + 1, 1 - par)

            iteration(0, 0, 0, True, True)
            iteration(1, 1, 1, True, True)
            with gp.Fori(1, B // 2 - 1) as i:
                for par in range(2):
                    iteration(i * 2 + par, par, 2, True, True)
            iteration(B - 2, 0, 2, True, False)
            iteration(B - 1, 1, 2, False, False)
            probs_low(B - 1)

            if stages > 1:
                for g in range(NG):
                    for c in range(FC):
                        n = g * FC + c
                        gp.wait_ge(f_sq, n + 1)
                        gp.wait_ge(f_h2, n + 1)
                        if g > 1:
                            gp.wait_ge(f_o, GT * (g - 1))
                        nc.gpsimd.tensor_tensor(h216[:, g % 2, 1, c, :], h2[:, n % 2, :], h216[:, g % 2, 0, c, :], ALU.subtract).then_inc(f_l, 1)

            if stages > 2:
                def split_ctx1(b, par):
                    gp.wait_ge(a_ch, b + 1)
                    nc.gpsimd.tensor_tensor(c116[:, par, 1, :, :], c1f[:, par, :, :], c116[:, par, 0, :, :], ALU.subtract).then_inc(a_cl, 1)

                split_ctx1(0, 0)
                split_ctx1(1, 1)
                with gp.Fori(1, B // 2) as i:
                    for par in range(2):
                        split_ctx1(i * 2 + par, par)

                def lows1(h, par):
                    for g in range(NHG):
                        gp.wait_ge(a_ph, h * NHG + g + 1)
                        nc.gpsimd.tensor_tensor(P116[:, 1, HS * g:HS * g + HS, :], P1[:, HS * g:HS * g + HS, :],
                                                P116[:, 0, HS * g:HS * g + HS, :], ALU.subtract).then_inc(a_pl, 1)
                    for q in range(NSP):
                        c0, c1 = q * HC // NSP, (q + 1) * HC // NSP
                        gp.wait_ge(w_hi, h * NSP + q + 1)
                        nc.gpsimd.tensor_tensor(ws16[:, par, 1, c0:c1], ws[:, par, c0:c1], ws16[:, par, 0, c0:c1], ALU.subtract).then_inc(w_lo, 1)

                with gp.Fori(0, B // 2) as i:
                    for par in range(2):
                        lows1(i * 2 + par, par)
            if stages > 3:
                gp.wait_ge(a_xu, B)
                gp.wait_ge(a_op, B)
                gp.wait_ge(w_st[0], 16 * E)
                gp.wait_ge(w_st[1], 16 * E)
                nc.gpsimd.memset(one16[:, :], 1.0).then_inc(m_c, 1)
                nc.gpsimd.memset(one[:, :], 1.0).then_inc(m_c, 1)
                gp.wait_ge(m_c, 3)
                nc.gpsimd.affine_select(out=tri[:, :], in_=one16[:, :], compare_op=ALU.is_gt, fill=0.0, base=0,
                                        pattern=[[1, P]], channel_multiplier=-1).then_inc(m_c, 1)
                nc.gpsimd.iota(ioe[:, :], pattern=[[1, E]], base=0, channel_multiplier=0, allow_small_or_imprecise_dtypes=True).then_inc(m_c, 1)
                nc.gpsimd.iota(iot[:, :], pattern=[[1, NT]], base=0, channel_multiplier=0, allow_small_or_imprecise_dtypes=True).then_inc(m_c, 1)

                with gp.Fori(0, B // 2) as i:
                    for par in range(2):
                        b = i * 2 + par
                        gp.wait_ge(m_xh, b + 1)
                        nc.gpsimd.tensor_tensor(xm16[:, bass.ds(b, 1), 1, :], xnm[:, par:par + 1, :], xm16[:, bass.ds(b, 1), 0, :], ALU.subtract).then_inc(m_xl, 1)
                gp.wait_ge(m_xl, B)
                gp.wait_ge(m_zf, 16)
                gp.wait_ge(m_sl, 1)
                for b in range(B):
                    for k in range(2):
                        nc.gpsimd.indirect_dma_start(out=xs_dram.ap(), out_offset=bass.IndirectOffsetOnAxis(ap=slot[:, 2 * b + k:2 * b + k + 1], axis=0),
                                                     in_=xm16[:, b, :, :].rearrange("p h d -> p (h d)"), in_offset=None).then_inc(m_sc, 16)

                gp.wait_ge(m_ys[0], 16 * ((NT + 1) // 2))
                gp.wait_ge(m_ys[1], 16 * (NT // 2))
                for b in range(B):
                    for k in range(2):
                        n = 2 * b + k
                        if n > 3:
                            gp.wait_ge(m_f, (n - 4) // 2 + 1)
                        nc.gpsimd.indirect_dma_start(out=yk[:, n % 4, :], out_offset=None, in_=ys_dram.ap(),
                                                     in_offset=bass.IndirectOffsetOnAxis(ap=slot[:, n:n + 1], axis=0)).then_inc(m_gk[n % 4], 16)

        @block.vector
        def _(dv):
            v = nc.vector
            vc = Count(s_pv)

            def step(ins):
                dv.wait_ge(s_pv, vc.up(ins))

            dv.wait_ge(s_x, 16)
            stats = [1]

            def tile_stats():
                for b in range(B):
                    ins = v.bn_stats(bst[:, b, :], X[:, b, :])
                ins.then_inc(s_bs, 1)
                aggregate()

            def aggregate():
                k = stats[0]
                dv.wait_ge(s_bs, k)
                for b in range(B):
                    ins = v.bn_aggr(mv[:, b, :], bst[:, b, :])
                ins.then_inc(s_bn, 1)

            tile_stats()

            def make_rstd():
                k = stats[0]
                dv.wait_ge(s_bn, k)
                v.tensor_scalar(rstd_t[:, 0, :], mv[:, :, 1], 1e-5, None, ALU.add).then_inc(s_var, 1)
                dv.wait_ge(s_sqrt, k)
                step(v.reciprocal(rstd_t[:, 2, :], rstd_t[:, 1, :]))
                step(v.tensor_tensor(rstd_t[:, 1, :], rstd_t[:, 2, :], rstd_t[:, 2, :], ALU.mult))
                step(v.tensor_tensor(rstd_t[:, 1, :], rstd_t[:, 1, :], rstd_t[:, 0, :], ALU.mult))
                step(v.tensor_scalar(rstd_t[:, 1, :], rstd_t[:, 1, :], -0.5, 1.5, ALU.mult, ALU.add))
                step(v.tensor_tensor(rstd[:, :], rstd_t[:, 1, :], rstd_t[:, 2, :], ALU.mult))
                stats[0] += 1

            make_rstd()
            dv.wait_ge(s_cw, 16 * 10)
            step(v.tensor_tensor(cn[:, :], boxn[:, :, 0], boxn[:, :, 1], ALU.add))
            step(v.tensor_scalar(cn[:, :], cn[:, :], 0.5, None, ALU.mult))
            step(v.tensor_tensor(rw[:, :], boxn[:, :, 1], boxn[:, :, 0], ALU.subtract))
            step(v.tensor_scalar(rw[:, :], rw[:, :], 1.0, None, ALU.add))
            step(v.reciprocal(rw[:, :], rw[:, :]))
            step(v.tensor_tensor(cm[:, :], rows[:, 0, :], rows[:, 1, :], ALU.add))
            step(v.tensor_scalar(cm[:, :], cm[:, :], 0.5, None, ALU.mult))
            step(v.tensor_tensor(wha[:, :, :], whc[:, :, 1, :], whc[:, :, 0, :], ALU.subtract))
            v.tensor_scalar(wha[:, :, :], wha[:, :, :], 1.0, None, ALU.add).then_inc(s_whv, 1)
            step(v.tensor_scalar(We[:, :], We[:, :], GSC, None, ALU.mult))
            step(v.tensor_scalar(AB[:, :, :], AB[:, :, :], GSC, None, ALU.mult))
            step(v.tensor_copy(We16[:, 0, :], We[:, :]))
            step(v.tensor_tensor(We16[:, 1, :], We[:, :], We16[:, 0, :], ALU.subtract))
            for j in range(3):
                dv.wait_ge(s_wfree, j + 1)
                v.scalar_tensor_tensor(wqkv16[:, j, 1, :, :], wst[j % 2], WSC, wqkv16[:, j, 0, :, :], ALU.mult, ALU.subtract).then_inc(s_wlo, 1)
            for par in range(2):
                v.memset(vv16[:, par, 0, :, DK:DK + 1], 1.0)
                ins = v.memset(vv16[:, par, 1, :, DK:DK + 1], 0.0)
            step(ins)

            def feature_distance(n, first=False):
                if not first:
                    dv.wait_ge(s_fa, 3 * n)
                for j in range(NJ):
                    ins = v.tensor_scalar(fu[:, j * N:(j + 1) * N], cm[:, bass.ds(n * N, N)],
                                          cn[:, bass.ds(n * NJ + j, 1)], rw[:, bass.ds(n * NJ + j, 1)],
                                          ALU.subtract, ALU.mult)
                ins.then_inc(s_fv, 1)

            def feature_floor(n):
                dv.wait_ge(s_fa, 3 * n + 1)
                v.tensor_scalar(fu[:, :], fu[:, :], 1e-3, None, ALU.max).then_inc(s_fv, 1)

            def feature_turns(n):
                dv.wait_ge(s_fa, 3 * n + 2)
                v.tensor_scalar(fu[:, :], fu[:, :], cst[:, 0:1], cst[:, 1:2], ALU.mult, ALU.add).then_inc(s_fv, 1)
                dv.wait_ge(s_fv, 5 * n + 3)
                v.tensor_scalar(fk[:, :], fu[:, :], ROUND, ROUND, ALU.add, ALU.subtract).then_inc(s_fv, 1)
                dv.wait_ge(s_fv, 5 * n + 4)
                v.tensor_tensor(fu[:, :], fu[:, :], fk[:, :], ALU.subtract).then_inc(s_fv, 1)

            def separable():
                dv.wait_ge(s_wha, 2)
                for g in range(2):
                    for r in range(2):
                        o = Lt[:, r, :, :].rearrange("p j (h n) -> p j h n", h=H)
                        for j in range(NJ):
                            ins = v.tensor_tensor(o[:, j], AB[:, r, :].unsqueeze(2).to_broadcast([P, H, NN]),
                                                  wht[:, r, g, j * NN:(j + 1) * NN].unsqueeze(1).to_broadcast([P, H, NN]), ALU.mult)
                        step(ins)
                    step(v.tensor_tensor(Lt[:, 0, :, :], Lt[:, 0, :, :], Lt[:, 1, :, :], ALU.add))
                    step(v.tensor_copy(Lw16[:, g, 0, :, :], Lt[:, 0, :, :]))
                    step(v.tensor_tensor(Lw16[:, g, 1, :, :], Lt[:, 0, :, :], Lw16[:, g, 0, :, :], ALU.subtract))
                for b in range(B):
                    ins = v.tensor_scalar(Rm16[:, b, 0, :], wht[:, 2, b // 8, :], mask[:, b % 8:b % 8 + 1], None, ALU.mult)
                step(ins)
                for b in range(B):
                    ins = v.scalar_tensor_tensor(Rm16[:, b, 1, :], wht[:, 2, b // 8, :], mask[:, b % 8:b % 8 + 1],
                                                 Rm16[:, b, 0, :], ALU.mult, ALU.subtract)
                ins.then_inc(s_whv, 1)

            def norm(b, wait):
                if wait is not None:
                    dv.wait_ge(s_xt, wait)
                v.tensor_scalar(xn[:, :], X[:, bass.ds(b, 1), :], mv[:, bass.ds(b, 1), 0:1], rstd[:, bass.ds(b, 1)],
                                ALU.subtract, ALU.mult).then_inc(s_xn, 1)

            def xn_low(b, par):
                dv.wait_ge(s_xh, b + 1)
                v.tensor_tensor(xn16[:, par, 1, :, :], bank[6][:, 0:KD * N].rearrange("p (k n) -> p k n", k=KD),
                                xn16[:, par, 0, :, :], ALU.subtract).then_inc(s_xl, 1)

            def row_max(b, gs):
                for g in gs:
                    dv.wait_ge(s_sm, 4 * b + g + 1)
                    v.tensor_reduce(nmx[:, HS * g:HS * g + HS], bank[g % 2][:, :].rearrange("p (h n) -> p h n", h=HS),
                                    AX.X, ALU.max, negate=True).then_inc(s_red, 1)

            def take_pv(c, first=False):
                for f in range(4):
                    ps = bank[6 + f % 2][:, 0:HS * (DK + 1)].rearrange("p (h d) -> p h d", h=HS)
                    dv.wait_ge(s_of, 4 * c + f + 1)
                    if f > 1 or not first:
                        dv.wait_ge(s_oe, 4 * c + f - 1)
                    v.reciprocal(rden[:, f % 2, :].unsqueeze(2), ps[:, :, DK:DK + 1]).then_inc(s_rd, 1)
                    dv.wait_ge(s_rd, 4 * c + f + 1)
                    if f == 0 and not first:
                        dv.wait_ge(s_ot, 2 * c)
                    v.tensor_tensor(O[:, f * HS * DK:(f + 1) * HS * DK].rearrange("p (h d) -> p h d", h=HS), ps[:, :, 0:DK],
                                    rden[:, f % 2, :].unsqueeze(2).to_broadcast([P, HS, DK]), ALU.mult).then_inc(s_oe, 1)

            def take_qk(b, rs, first=False):
                for r in rs:
                    dv.wait_ge(s_qf, 6 * b + r + 1)
                    if not first:
                        dv.wait_ge(s_ql, 4 * b + r - 3)
                    v.scalar_tensor_tensor(qt[:, r, :, :], bank[4 + r % 2][:, :].rearrange("p (c n) -> p c n", c=HS), 1.0 / WSC,
                                           bqk[:, r // 2, HS * (r % 2):HS * (r % 2) + HS].unsqueeze(2).to_broadcast([P, HS, N]),
                                           ALU.mult, ALU.add).then_inc(s_qe, 1)

            def take_v(b, first=False):
                for r in range(2):
                    dv.wait_ge(s_qf, 6 * b + 4 + r + 1)
                    if not first:
                        dv.wait_ge(s_vl, 2 * b + r - 1)
                    v.scalar_tensor_tensor(vf[:, r, :, :], bank[4 + r][:, :].rearrange("p (h d) -> p h d", h=8), 1.0 / WSC,
                                           bv[:, 512 * r:512 * r + 512].rearrange("p (h d) -> p h d", h=8),
                                           ALU.mult, ALU.add).then_inc(s_qe, 1)

            def residual(c):
                dv.wait_ge(s_op, c + 1)
                v.tensor_tensor(otmp[:, :], bank[7][:, 0:D], bo[:, :], ALU.add).then_inc(s_opt, 1)
                dv.wait_ge(s_opt, c + 1)
                xb = X[:, bass.ds(c, 1), :]
                v.scalar_tensor_tensor(xb, otmp[:, :].unsqueeze(1), tg[:, 0:1], xb, ALU.mult, ALU.add).then_inc(s_xu, 1)

            def probs(b, first):
                for g in range(4):
                    dv.wait_ge(s_gf, 4 * b + g + 1)
                    if g == 0:
                        dv.wait_ge(s_exp, 4 * b + 4)
                        if not first:
                            dv.wait_ge(s_pl, 4 * b)
                    for jj in range(2):
                        j = 2 * g + jj
                        v.scalar_tensor_tensor(PT[:, :, j * NN:(j + 1) * NN],
                                               bank[2 + g % 2][:, jj * 256:(jj + 1) * 256].rearrange("p (h n) -> p h n", h=H), 1e-6 * GSC,
                                               EX[:, :, j * NN:(j + 1) * NN], ALU.max, ALU.mult).then_inc(s_pm, 1)

            norm(0, None)
            feature_distance(0, True)
            norm(1, 1)
            feature_floor(0)
            dv.wait_ge(s_wha, 1)
            for r in range(3):
                ins = v.tensor_scalar(wht[:, r, :, :], wha[:, :, :], cst[:, 2:3], cst[:, 3 + r:4 + r], ALU.mult, ALU.add)
            step(ins)
            step(v.tensor_scalar(whk[:, :, :, :], wht[:, :, :, :], ROUND, ROUND, ALU.add, ALU.subtract))
            v.tensor_tensor(wht[:, :, :, :], wht[:, :, :, :], whk[:, :, :, :], ALU.subtract).then_inc(s_whv, 1)
            feature_turns(0)
            xn_low(0, 0)
            xn_low(1, 1)
            dv.wait_ge(s_o, 64)
            take_qk(0, range(4), True)
            take_v(0, True)
            separable()
            dv.wait_ge(s_tg, 1)

            def iteration(b, par, has_c, has_q, has_x, first=False):
                if has_x:
                    norm(b + 2, b + 2)
                row_max(b, (0, 1))
                if has_q:
                    feature_distance(b + 1)
                    take_qk(b + 1, (0, 1))
                row_max(b, (2, 3))
                if has_q:
                    feature_floor(b + 1)
                    take_qk(b + 1, (2, 3))
                if has_c:
                    take_pv(b - 1, first)
                if has_q:
                    take_v(b + 1)
                if has_x:
                    xn_low(b + 2, par)
                if has_q:
                    feature_turns(b + 1)
                if has_c:
                    residual(b - 1)
                probs(b, not has_c)

            iteration(0, 0, False, True, True)
            iteration(1, 1, True, True, True, True)
            with dv.Fori(0, B // 2 - 2) as i:
                for par in range(2):
                    iteration(i * 2 + 2 + par, par, True, True, True)
            iteration(B - 2, 0, True, True, False)
            iteration(B - 1, 1, True, False, False)
            take_pv(B - 1)
            residual(B - 1)

            if stages > 1:
                dv.wait_ge(s_xu, B)
                tile_stats()
                make_rstd()
                dv.wait_ge(f_ld, 64)
                step(v.tensor_reduce(thr[:, 0, 0:FC], wfc[:, :, :], AX.X, ALU.add, apply_absolute_value=True))
                step(v.tensor_reduce(thr[:, 0, FC:], wpj[:, :, :], AX.X, ALU.add, apply_absolute_value=True))
                step(v.tensor_scalar(thr[:, 0, 0:FC], thr[:, 0, 0:FC], 1.0 / D, 1e-5, ALU.mult, ALU.max))
                step(v.tensor_scalar(thr[:, 0, FC:], thr[:, 0, FC:], 1.0 / FF, 1e-5, ALU.mult, ALU.max))
                for r, k in ((1, 0.5), (2, -0.5), (3, -1.0)):
                    ins = v.tensor_scalar(thr[:, r, :], thr[:, 0, :], k, None, ALU.mult)
                step(ins)
                for c in range(FC):
                    v.tensor_scalar(wfa[:, c, :], wfc[:, c, :], thr[:, 1, c:c + 1], thr[:, 0, c:c + 1], ALU.is_gt, ALU.mult)
                    ins = v.tensor_scalar(wfb[:, c, :], wfc[:, c, :], thr[:, 2, c:c + 1], thr[:, 3, c:c + 1], ALU.is_lt, ALU.mult)
                step(ins)
                step(v.tensor_tensor(wfa[:, :, :], wfa[:, :, :], wfb[:, :, :], ALU.add))
                for c in range(KD):
                    ins = v.tensor_scalar(wpa[:, c, :], wpj[:, c, :], thr[:, 2, FC + c:FC + c + 1], -1.0, ALU.is_lt, ALU.mult)
                step(ins)
                for c in range(KD):
                    ins = v.scalar_tensor_tensor(wpa[:, c, :], wpj[:, c, :], thr[:, 1, FC + c:FC + c + 1], wpa[:, c, :], ALU.is_gt, ALU.add)
                ins.then_inc(f_w, 1)
                dv.wait_ge(f_mp, 1)
                v.tensor_copy(lowm[:, :], bank[4][0:RANK, 0:D]).then_inc(f_m, 1)
                for r in range(FC // 2):
                    dv.wait_ge(f_lp, r + 1)
                    v.scalar_tensor_tensor(wfa[:, 2 * r:2 * r + 2, :], bank[r][:, :].rearrange("p (c d) -> p c d", c=2), fgate[:, 0:1],
                                           wfa[:, 2 * r:2 * r + 2, :], ALU.mult, ALU.add).then_inc(f_low, 1)
                for r in range(4):
                    dv.wait_ge(f_hi, r + 1)
                    kk, fh = r // 2, r % 2
                    v.scalar_tensor_tensor(W1T16[:, 1, kk, 512 * fh:512 * fh + 512], bank[r][:, :], WSC,
                                           W1T16[:, 0, kk, 512 * fh:512 * fh + 512], ALU.mult, ALU.subtract).then_inc(f_lo, 1)
                dv.wait_ge(f_mp, 2)
                v.tensor_copy(w2row[:, :], bank[4][:, 0:D]).then_inc(f_m, 1)

                def ffn_norm(g):
                    for i in range(GT):
                        t = g * GT + i
                        ins = v.tensor_scalar(xng[:, g % 2, i, :], X[:, t, :], mv[:, t, 0:1], rstd[:, t:t + 1], ALU.subtract, ALU.mult)
                    ins.then_inc(f_xn, 1)

                def ffn_low(g):
                    for kk in range(KD):
                        dv.wait_ge(f_xh, 2 * g + kk + 1)
                        v.tensor_tensor(xg16[:, g % 2, 1, kk, :], bank[4 + kk][:, :], xg16[:, g % 2, 0, kk, :], ALU.subtract).then_inc(f_xl, 1)

                def ffn_square(g):
                    for c in range(FC):
                        n = g * FC + c
                        dv.wait_ge(f_r, n + 1)
                        if n > 1:
                            dv.wait_ge(f_l, n - 1)
                        v.tensor_tensor(h2[:, n % 2, :], hr[:, n % 2, :], hr[:, n % 2, :], ALU.mult).then_inc(f_h2, 1)

                def ffn_residual(g):
                    for i in range(GT):
                        t = g * GT + i
                        dv.wait_ge(f_o, t + 1)
                        if t > 1:
                            dv.wait_ge(f_xu, t - 1)
                        v.tensor_tensor(ftmp[:, t % 2, :], bank[6 + t % 2][:, 0:D], w2row[:, :], ALU.mult).then_inc(f_ot, 1)
                        dv.wait_ge(f_ot, t + 1)
                        v.scalar_tensor_tensor(X[:, t, :], ftmp[:, t % 2, :], tg[:, 2:3], X[:, t, :], ALU.mult, ALU.add).then_inc(f_xu, 1)
                        dv.wait_ge(f_xu, t + 1)
                        ins = v.bn_stats(bst[:, t, :], X[:, t, :])
                    if g == NG - 1:
                        ins.then_inc(s_bs, 1)

                ffn_norm(0)
                ffn_norm(1)
                ffn_low(0)
                for g in range(NG):
                    ffn_square(g)
                    if g + 2 < NG:
                        ffn_norm(g + 2)
                    if g + 1 < NG:
                        ffn_low(g + 1)
                    if g:
                        ffn_residual(g - 1)
                ffn_residual(NG - 1)

            if stages > 2:
                aggregate()
                make_rstd()
                dv.wait_ge(a_w, 1)
                v.scalar_tensor_tensor(w1_16[:, 1, :, :], wst1[:, :, :], WSC, w1_16[:, 0, :, :], ALU.mult, ALU.subtract).then_inc(a_wl, 1)
                step(v.tensor_tensor(gam[:, 0, :], gam[:, 0, :], gam[:, 1, :], ALU.mult))
                for i in range(B):
                    v.memset(v1[:, i, 0, :, HD:HD + 1], 1.0)
                    ins = v.memset(v1[:, i, 1, :, HD:HD + 1], 0.0)
                step(ins)
                step(v.memset(seg[:, :, :, :, 3:4, :].rearrange("a r q h s d -> a (r q h) (s d)"), 0.0))

                def norm1(b, par, first):
                    if not first:
                        dv.wait_ge(a_xt, b - 1)
                    v.tensor_scalar(xn1[:, par, :], X[:, bass.ds(b, 1), :], mv[:, bass.ds(b, 1), 0:1], rstd[:, bass.ds(b, 1)],
                                    ALU.subtract, ALU.mult).then_inc(a_xn, 1)

                def low1(b, par):
                    dv.wait_ge(a_xh, b + 1)
                    v.tensor_tensor(x116[:, par, 1, :, :], bank[par][:, 0:KD * N].rearrange("p (k n) -> p k n", k=KD),
                                    x116[:, par, 0, :, :], ALU.subtract).then_inc(a_xl, 1)

                def sums(b, par):
                    dv.wait_ge(a_kf, b + 1)
                    full = bank[4 + par][:, D:].rearrange("p (o h d) -> p o h d", o=1, h=H)
                    high = v1[:, bass.ds(b, 1), 0, :, 0:HD]
                    v.tensor_scalar(high, full, 1.0 / WSC, None, ALU.mult).then_inc(a_v, 1)
                    dv.wait_ge(a_v, 2 * b + 1)
                    v.scalar_tensor_tensor(v1[:, bass.ds(b, 1), 1, :, 0:HD], full, 1.0 / WSC, high, ALU.mult, ALU.subtract).then_inc(a_v, 1)
                    dv.wait_ge(a_raw, b + 1)
                    v.tensor_reduce(ms[:, 0, bass.ds(b, 1), :], sq[:, par:par + 1, :, :].rearrange("p o q (h d) -> p o (q h) d", h=H),
                                    AX.X, ALU.add).then_inc(a_red, 1)

                norm1(0, 0, True)
                norm1(1, 1, True)
                low1(0, 0)
                low1(1, 1)
                with dv.Fori(1, B // 2) as i:
                    for par in range(2):
                        norm1(i * 2 + par, par, False)
                    for par in range(2):
                        sums(i * 2 - 2 + par, par)
                    for par in range(2):
                        low1(i * 2 + par, par)
                sums(B - 2, 0)
                sums(B - 1, 1)
                dv.wait_ge(a_red, B)
                v.tensor_scalar(ms[:, 0, :, :], ms[:, 0, :, :], 1.0 / HD, 1e-6, ALU.mult, ALU.add).then_inc(a_ms, 1)
                dv.wait_ge(a_sq, 1)
                step(v.reciprocal(ms[:, 2, :, :], ms[:, 1, :, :]))
                step(v.tensor_tensor(ms[:, 1, :, :], ms[:, 2, :, :], ms[:, 2, :, :], ALU.mult))
                step(v.tensor_tensor(ms[:, 1, :, :], ms[:, 1, :, :], ms[:, 0, :, :], ALU.mult))
                step(v.tensor_scalar(ms[:, 1, :, :], ms[:, 1, :, :], -0.5, 1.5, ALU.mult, ALU.add))
                step(v.tensor_tensor(ms[:, 3, :, :], ms[:, 1, :, :], ms[:, 2, :, :], ALU.mult))

                def scale1(b, par, first):
                    if not first:
                        dv.wait_ge(a_sh, b - 1)
                        dv.wait_ge(a_sl, b - 1)
                    v.tensor_tensor(qn[:, par, :, :].rearrange("p q (h d) -> p (q h) d", h=H),
                                    raw[:, bass.ds(b, 1), :, :].rearrange("p o q (h d) -> p (o q h) d", h=H),
                                    ms[:, 3, bass.ds(b, 1), :].rearrange("p o h -> p (o h)").unsqueeze(2).to_broadcast([P, 2 * H, HD]), ALU.mult).then_inc(a_qn, 1)
                    dv.wait_ge(a_qn, b + 1)
                    v.tensor_tensor(qn[:, par, 1, :], qn[:, par, 1, :], gam[:, 0, :], ALU.mult).then_inc(a_gn, 1)

                def seg_low(b, par):
                    dv.wait_ge(a_sh, b + 1)
                    for w, sg in ((0, 2), (1, 1)):
                        ins = v.tensor_tensor(seg[:, par, w, :, sg, :], qn[:, par, w, :].rearrange("p (h d) -> p h d", h=H),
                                              seg[:, par, w, :, 0, :], ALU.subtract)
                    ins.then_inc(a_sl, 1)

                def copy_k(b, par):
                    dv.wait_ge(a_tk, b + 1)
                    v.tensor_copy(qT1[:, par, 1, :, :].rearrange("p c n -> p (c n)"), bank[3][:, :].bitcast(F16)).then_inc(a_ck, 1)

                def row_max1(b):
                    for g in range(NHG):
                        dv.wait_ge(a_sm, 4 * b + g + 1)
                        v.tensor_reduce(nmx1[:, HS * g:HS * g + HS], bank[g % 2][:, :].rearrange("p (h n) -> p h n", h=HS),
                                        AX.X, ALU.max, negate=True).then_inc(a_mx, 1)

                def take_pv1(c, first):
                    ps = bank[6][:, 0:H * (HD + 1)].rearrange("p (h d) -> p h d", h=H)
                    dv.wait_ge(a_pv, c + 1)
                    if not first:
                        dv.wait_ge(a_o, c)
                    v.reciprocal(rden1[:, :].unsqueeze(2), ps[:, :, HD:HD + 1]).then_inc(a_rd, 1)
                    dv.wait_ge(a_rd, c + 1)
                    if not first:
                        dv.wait_ge(a_ot, c)
                    v.tensor_tensor(O1[:, :].rearrange("p (h d) -> p h d", h=H), ps[:, :, 0:HD],
                                    rden1[:, :].unsqueeze(2).to_broadcast([P, H, HD]), ALU.mult).then_inc(a_o, 1)

                def residual1(c):
                    dv.wait_ge(a_op, c + 1)
                    xb = X[:, bass.ds(c, 1), :]
                    v.scalar_tensor_tensor(xb, bank[5][:, 0:D].unsqueeze(1), tg[:, 1:2], xb, ALU.mult, ALU.add).then_inc(a_xu, 1)

                scale1(0, 0, True)
                scale1(1, 1, True)
                seg_low(0, 0)
                seg_low(1, 1)
                copy_k(0, 0)

                def iteration1(b, par, c, has_q, has_x):
                    row_max1(b)
                    if has_q:
                        copy_k(b + 1, 1 - par)
                    if has_x:
                        scale1(b + 2, par, False)
                    if c > 1:
                        residual1(b - 2)
                    if c:
                        take_pv1(b - 1, c == 1)
                    if has_x:
                        seg_low(b + 2, par)

                iteration1(0, 0, 0, True, True)
                iteration1(1, 1, 1, True, True)
                iteration1(2, 0, 2, True, True)
                iteration1(3, 1, 3, True, True)
                with dv.Fori(2, B // 2 - 1) as i:
                    for par in range(2):
                        iteration1(i * 2 + par, par, 3, True, True)
                iteration1(B - 2, 0, 3, True, False)
                iteration1(B - 1, 1, 3, False, False)
                residual1(B - 2)
                take_pv1(B - 1, False)
                residual1(B - 1)

            if stages > 3:
                dv.wait_ge(a_xu, B)
                tile_stats()
                make_rstd()
                v4 = Count(m_v)

                def then(ins):
                    dv.wait_ge(m_v, v4.up(ins))

                def norm_m(b, par, first):
                    if not first:
                        dv.wait_ge(m_xt, b - 1)
                        dv.wait_ge(m_xl, b - 1)
                    v.tensor_scalar(xnm[:, par, :], X[:, bass.ds(b, 1), :], mv[:, bass.ds(b, 1), 0:1], rstd[:, bass.ds(b, 1)],
                                    ALU.subtract, ALU.mult).then_inc(m_xn, 1)

                dv.wait_ge(a_op, B)
                dv.wait_ge(w_st[0], 16 * E)
                dv.wait_ge(w_st[1], 16 * E)
                norm_m(0, 0, True)
                norm_m(1, 1, True)
                with dv.Fori(1, B // 2) as i:
                    for par in range(2):
                        norm_m(i * 2 + par, par, False)
                dv.wait_ge(m_lg, B)
                then(v.tensor_copy(lg[:, :, :], bank[7][:, 0:B * E].rearrange("p (b e) -> p b e", e=E)))
                for b in range(B):
                    ins = v.max(top[:, b, :], lg[:, b, :])
                then(ins)
                for b in range(B):
                    v.max_index(topi[:, b, :], top[:, b, :], lg[:, b, :])
                v.tensor_tensor(ex[:, :, 0:E], lg[:, :, :], top[:, :, 0:1].to_broadcast([P, B, E]), ALU.subtract)
                then(v.tensor_tensor(ex[:, :, E], top[:, :, 1], top[:, :, 0], ALU.subtract))
                v.engine_nop().then_inc(m_ex, 1)
                then(v.tensor_copy(idf[:, :, :], topi[:, :, 0:2]))
                dv.wait_ge(m_c, 6)
                then(v.tensor_tensor(oh[:, :, :], idf[:, :, :].rearrange("p b k -> p (b k)").unsqueeze(1).to_broadcast([P, E, B * 2]),
                                     ioe[:, :].unsqueeze(2).to_broadcast([P, E, B * 2]), ALU.is_equal))
                v.tensor_copy(oh16[:, :], oh[:, :, :].rearrange("p e n -> p (e n)")).then_inc(m_ex, 1)
                dv.wait_ge(m_er, 1)
                then(v.tensor_reduce(den[:, 0, :], ex[:, :, 0:E], AX.X, ALU.add))
                then(v.reciprocal(den[:, 1, :], den[:, 0, :]))
                then(v.tensor_scalar(wk[:, 0, :], den[:, 1, :], tg[:, 3:4], None, ALU.mult))
                then(v.tensor_tensor(wk[:, 1, :], wk[:, 0, :], ex[:, :, E], ALU.mult))
                dv.wait_ge(m_pr, 1)
                then(v.tensor_copy(tot[:, :], bank[6][:, 256:512]))
                v.tensor_tensor_scan(cum[:, :], one[:, :], tot[:, :], 0.0, ALU.mult, ALU.add)
                then(v.tensor_reduce(cnt[:, 0, :], tot[:, :].rearrange("p (e n) -> p e n", e=E), AX.X, ALU.add))
                then(v.tensor_tensor_scan(cnt[:, 1, :], one[:, 0:E], cnt[:, 0, :], 0.0, ALU.mult, ALU.add))
                then(v.tensor_scalar(cnt[:, 2, :], cnt[:, 0, :], 1.0 / MT, (MT - 1.0) / MT - 0.5 + 0.5 / MT, ALU.mult, ALU.add))
                then(v.tensor_scalar(cnt[:, 2, :], cnt[:, 2, :], ROUND, ROUND, ALU.add, ALU.subtract))
                then(v.tensor_tensor_scan(cnt[:, 3, :], one[:, 0:E], cnt[:, 2, :], 0.0, ALU.mult, ALU.add))
                then(v.tensor_tensor(cnt[:, 4, :], cnt[:, 3, :], cnt[:, 2, :], ALU.subtract))
                then(v.tensor_tensor(cnt[:, 5, :], cnt[:, 1, :], cnt[:, 0, :], ALU.subtract))
                then(v.scalar_tensor_tensor(cnt[:, 4, :], cnt[:, 4, :], float(MT), cnt[:, 5, :], ALU.mult, ALU.subtract))
                then(v.tensor_tensor(pos[:, :, :].rearrange("p e n -> p (e n)"), cum[:, :], tot[:, :], ALU.subtract))
                then(v.tensor_tensor(pos[:, :, :].rearrange("p e n -> p (e n)"), pos[:, :, :].rearrange("p e n -> p (e n)"), bank[6][:, 0:256], ALU.add))
                then(v.tensor_tensor(pos[:, :, :], pos[:, :, :], cnt[:, 4, :].unsqueeze(2).to_broadcast([P, E, B * 2]), ALU.add))
                then(v.tensor_tensor(pos[:, :, :], pos[:, :, :], oh[:, :, :], ALU.mult))
                then(v.tensor_reduce(slotf[:, :], pos[:, :, :].rearrange("p e n -> p n e"), AX.X, ALU.add))
                v.tensor_copy(slot[:, :], slotf[:, :]).then_inc(m_sl, 1)
                then(v.tensor_tensor(cmp[:, :, :], cnt[:, 3, :].unsqueeze(1).to_broadcast([P, NT, E]),
                                     iot[:, :].unsqueeze(2).to_broadcast([P, NT, E]), ALU.is_le))
                then(v.tensor_reduce(etf[:, :], cmp[:, :, :], AX.X, ALU.add))
                then(v.tensor_scalar(etf[:, :], etf[:, :], float(E - 1), None, ALU.min))
                then(v.memset(chg[:, 0:2], 1))
                then(v.tensor_tensor(chg[:, 2:], etf[:, 2:], etf[:, 0:NT - 2], ALU.not_equal))
                v.tensor_copy(eti[:, :], etf[:, :]).then_inc(m_sl, 1)

                def products(t, par, c0, c1, first):
                    for c in range(c0, c1):
                        dv.wait_ge(m_g, FC * t + c + 1)
                        if c % 2 == 0 and not (first and c < 4):
                            dv.wait_ge(m_hh, 4 * t + c // 2 - 1)
                            dv.wait_ge(m_hl, 4 * t + c // 2 - 1)
                        v.scalar_tensor_tensor(hf[:, (c // 2) % 2, c % 2, :], bank[c % 4][:, MT:2 * MT], bms[:, par, FC + c:FC + c + 1],
                                               yg[:, c % 4, :], ALU.add, ALU.mult).then_inc(m_u, 1)
                        if c % 2:
                            q = c // 2
                            dv.wait_ge(m_hh, 4 * t + q + 1)
                            v.tensor_tensor(hm16[:, par, 1, c - 1:c + 1, :], hf[:, q % 2, :, :], hm16[:, par, 0, c - 1:c + 1, :], ALU.subtract).then_inc(m_hl, 1)

                def copy_tokens(t, par):
                    dv.wait_ge(m_tt, t + 1)
                    v.tensor_copy(xT16[:, par, :, :].rearrange("p a n -> p (a n)"), bank[4][:, :].bitcast(F16)).then_inc(m_tc, 1)

                def take_out(t, par, first):
                    dv.wait_ge(m_o, t + 1)
                    if not first:
                        dv.wait_ge(m_ys[par], (t - par) * 8)
                    v.scalar_tensor_tensor(ys[:, par, :, :], bank[5 + par][:, :].rearrange("p (h d) -> p h d", h=2), 1.0,
                                           b2r[:, par, :].unsqueeze(1).to_broadcast([P, MT // P, D]), ALU.mult, ALU.add).then_inc(m_y, 1)

                def expert_v(t, par, prev, nxt, first=False):
                    products(t, par, 0, 4, first)
                    if prev:
                        take_out(t - 1, 1 - par, prev == 1)
                    if nxt:
                        copy_tokens(t + 1, 1 - par)
                    products(t, par, 4, 8, False)

                copy_tokens(0, 0)
                expert_v(0, 0, 0, True, True)
                expert_v(1, 1, 1, True)
                expert_v(2, 0, 1, True)
                with dv.Fori(0, (NT - 5) // 2) as i:
                    for q in range(2):
                        expert_v(i * 2 + 3 + q, 1 - q, 2, True)
                expert_v(NT - 2, 1, 2, True)
                expert_v(NT - 1, 0, 2, False)
                take_out(NT - 1, 0, False)
                for b in range(B):
                    for k in range(2):
                        n = 2 * b + k
                        dv.wait_ge(m_gk[n % 4], 16 * (n // 4 + 1))
                        ins = v.scalar_tensor_tensor(X[:, b, :], yk[:, n % 4, :], wk[:, k, b:b + 1], X[:, b, :], ALU.mult, ALU.add)
                        if k == 0:
                            then(ins)
                    ins.then_inc(m_f, 1)

        @block.scalar
        def _(ac):
            s = nc.scalar
            ac.dma_start(X[:, :, :], a["x"].rearrange("b n d -> n b d")).then_inc(s_x, 16)
            ac.dma_start(gates[:, 0:2], a["g_xattn"].partition_broadcast(P)).then_inc(s_c, 16)
            ac.dma_start(gates[:, 2:4], a["g_ffn"].partition_broadcast(P)).then_inc(s_c, 16)
            ac.wait_ge(s_c, 32)
            s.activation(tg[:, :], gates[:, :], ACT.Tanh).then_inc(s_tg, 1)
            ac.wait_ge(s_var, 1)
            s.activation(rstd_t[:, 1, :], rstd_t[:, 0, :], ACT.Sqrt).then_inc(s_sqrt, 1)
            for j in range(3):
                ac.wait_ge(s_w[j % 2], 16 * (j // 2) + 16)
                s.activation(wqkv16[:, j, 0, :, :], wst[j % 2], ACT.Copy, scale=WSC).then_inc(s_wfree, 1)

            def feature_abs(n):
                ac.wait_ge(s_fv, 5 * n + 1)
                s.activation(fu[:, :], fu[:, :], ACT.Abs).then_inc(s_fa, 1)

            def feature_log(n):
                ac.wait_ge(s_fv, 5 * n + 2)
                s.activation(fu[:, :], fu[:, :], ACT.Ln).then_inc(s_fa, 1)

            def feature_sine(n, par, first):
                ac.wait_ge(s_fv, 5 * n + 5)
                if first:
                    ac.wait_ge(s_flo, n)
                s.activation(fs[:, :], fu[:, :], ACT.Sin, scale=TWO_PI).then_inc(s_fa, 1)
                ac.wait_ge(s_fa, 3 * n + 3)
                if first > 1:
                    ac.wait_ge(s_gf, 4 * n - 4)
                s.activation(F16s[:, par, 0, :], fs[:, :], ACT.Copy).then_inc(s_fhi, 1)

            def xn_high(b, par):
                ac.wait_ge(s_xt, b + 1)
                s.activation(xn16[:, par, 0, :, :], bank[6][:, 0:KD * N].rearrange("p (k n) -> p k n", k=KD), ACT.Copy).then_inc(s_xh, 1)

            def take_o(c, first):
                for r in range(2):
                    ac.wait_ge(s_ot, 2 * c + r + 1)
                    if r == 0 and not first:
                        ac.wait_ge(s_op, c)
                    s.activation(OT[:, 4 * r:4 * r + 4, :], bank[6 + r][:, :].rearrange("p (c n) -> p c n", c=4), ACT.Copy).then_inc(s_oc, 1)

            def exps(b, first):
                for g in range(4):
                    ac.wait_ge(s_st, 4 * b + g + 1)
                    if g == 0 and not first:
                        ac.wait_ge(s_pm, 8 * b)
                    s.activation(EX[:, HS * g:HS * g + HS, :], bank[g % 2][:, :].rearrange("p (h n) -> p h n", h=HS), ACT.Exp,
                                 scale=DK ** -0.5).then_inc(s_exp, 1)

            def ctx_high(b, par, first):
                ac.wait_ge(s_cf[par], (b - par) * 8 + 16)
                if not first:
                    ac.wait_ge(s_qf, 6 * b - 6)
                s.activation(ctx16[:, par, 0, :, :], ctxf[:, par, :, :], ACT.Copy).then_inc(s_ch, 1)

            def qk_high(b, par, rs, first=False):
                for r in rs:
                    w, g = r // 2, r % 2
                    ac.wait_ge(s_qe, 6 * b + r + 1)
                    s.activation(q16[:, par, w, 0, HS * g:HS * g + HS, :], qt[:, r, :, :], ACT.Copy).then_inc(s_qh, 1)

            def v_high(b, par):
                for r in range(2):
                    ac.wait_ge(s_qe, 6 * b + 4 + r + 1)
                    s.activation(vv16[:, par, 0, 8 * r:8 * r + 8, 0:DK], vf[:, r, :, :], ACT.Copy).then_inc(s_vh, 1)

            def probs_high(c, first):
                for g in range(4):
                    if g == 0:
                        ac.wait_ge(s_pm, 8 * c + 8)
                        if not first:
                            ac.wait_ge(s_of, 4 * c)
                    s.activation(PT16[:, 0, HS * g:HS * g + HS, :], PT[:, HS * g:HS * g + HS, :], ACT.Copy).then_inc(s_ph, 1)

            feature_abs(0)
            ac.wait_ge(s_whv, 1)
            s.activation(wha[:, :, :], wha[:, :, :], ACT.Ln).then_inc(s_wha, 1)
            feature_log(0)
            xn_high(0, 0)
            xn_high(1, 1)
            ctx_high(0, 0, True)
            ctx_high(1, 1, True)
            ac.wait_ge(s_whv, 2)
            s.activation(wht[:, :, :, :], wht[:, :, :, :], ACT.Sin, scale=TWO_PI).then_inc(s_wha, 1)
            feature_sine(0, 0, 0)
            qk_high(0, 0, range(4))
            v_high(0, 0)

            def iteration(b, par, c, has_x, has_q=True):
                if c:
                    probs_high(b - 1, c == 1)
                if has_x:
                    ctx_high(b + 2, par, False)
                if has_q:
                    feature_abs(b + 1)
                    qk_high(b + 1, 1 - par, (0, 1))
                    feature_log(b + 1)
                    qk_high(b + 1, 1 - par, (2, 3))
                    v_high(b + 1, 1 - par)
                if c:
                    take_o(b - 1, c == 1)
                if has_x:
                    xn_high(b + 2, par)
                exps(b, c == 0)
                if has_q:
                    feature_sine(b + 1, 1 - par, min(c + 1, 2))

            iteration(0, 0, 0, True)
            iteration(1, 1, 1, True)
            with ac.Fori(0, B // 2 - 2) as i:
                for par in range(2):
                    iteration(i * 2 + 2 + par, par, 2, True)
            iteration(B - 2, 0, 2, False)
            iteration(B - 1, 1, 2, False, False)
            probs_high(B - 1, False)
            take_o(B - 1, False)

            if stages > 1:
                ac.wait_ge(s_var, 2)
                s.activation(rstd_t[:, 1, :], rstd_t[:, 0, :], ACT.Sqrt).then_inc(s_sqrt, 1)
                for r in range(4):
                    ac.wait_ge(f_tp, r + 1)
                    kk, fh = r // 2, r % 2
                    s.activation(W1T16[:, 0, kk, 512 * fh:512 * fh + 512], bank[r][:, :], ACT.Copy, scale=WSC).then_inc(f_hi, 1)
                for r in range(4):
                    ac.wait_ge(f_tp, r + 5)
                    s.activation(W2T16[:, 2 * r:2 * r + 2, :], bank[r][:, :].rearrange("p (f d) -> p f d", f=2), ACT.Copy).then_inc(f_hi, 1)

                def ffn_high(g):
                    for kk in range(KD):
                        ac.wait_ge(f_xt, 2 * g + kk + 1)
                        s.activation(xg16[:, g % 2, 0, kk, :], bank[4 + kk][:, :], ACT.Copy).then_inc(f_xh, 1)

                def ffn_relu(g):
                    for c in range(FC):
                        n = g * FC + c
                        ac.wait_ge(f_h, n + 1)
                        if n > 1:
                            ac.wait_ge(f_sq, n - 1)
                            ac.wait_ge(f_h2, n - 1)
                        s.activation(hr[:, n % 2, :], bank[n % 4][:, :], ACT.Relu, scale=1.0 / WSC).then_inc(f_r, 1)
                        ac.wait_ge(f_r, n + 1)
                        if c == 0 and g > 1:
                            ac.wait_ge(f_o, GT * (g - 1))
                        s.activation(h216[:, g % 2, 0, c, :], hr[:, n % 2, :], ACT.Square).then_inc(f_sq, 1)

                ffn_high(0)
                for g in range(NG):
                    if g + 1 < NG:
                        ffn_high(g + 1)
                    ffn_relu(g)

            if stages > 2:
                ac.wait_ge(s_var, 3)
                s.activation(rstd_t[:, 1, :], rstd_t[:, 0, :], ACT.Sqrt).then_inc(s_sqrt, 1)
                ac.wait_ge(a_ld, 80)
                s.activation(w1_16[:, 0, :, :], wst1[:, :, :], ACT.Copy, scale=WSC).then_inc(a_w, 1)

                def high1(b, par):
                    ac.wait_ge(a_xt, b + 1)
                    s.activation(x116[:, par, 0, :, :], bank[par][:, 0:KD * N].rearrange("p (k n) -> p k n", k=KD), ACT.Copy).then_inc(a_xh, 1)

                def copy_raw(b, par, first):
                    ac.wait_ge(a_qf, b + 1)
                    ac.wait_ge(a_kf, b + 1)
                    if not first:
                        ac.wait_ge(a_red, b - 1)
                    for w, ps in ((0, bank[2 + par][:, 0:D]), (1, bank[4 + par][:, 0:D])):
                        if w:
                            ac.wait_ge(a_v, 2 * b + 2)
                        s.activation(sq[:, par, w, :], ps, ACT.Square, scale=1.0 / WSC)
                        ins = s.activation(raw[:, bass.ds(b, 1), w, :], ps.unsqueeze(1), ACT.Copy, scale=1.0 / WSC)
                    ins.then_inc(a_raw, 1)

                def ctx_high1(b, par, first):
                    ac.wait_ge(a_cf[par], (b - par) * 8 + 16)
                    if not first:
                        ac.wait_ge(a_kf, b - 1)
                    s.activation(c116[:, par, 0, :, :], c1f[:, par, :, :], ACT.Copy).then_inc(a_ch, 1)

                ctx_high1(0, 0, True)
                ctx_high1(1, 1, True)
                high1(0, 0)
                high1(1, 1)
                copy_raw(0, 0, True)
                copy_raw(1, 1, True)
                with ac.Fori(1, B // 2) as i:
                    for par in range(2):
                        ctx_high1(i * 2 + par, par, False)
                        high1(i * 2 + par, par)
                    for par in range(2):
                        copy_raw(i * 2 + par, par, False)
                ac.wait_ge(a_ms, 1)
                s.activation(ms[:, 1, :, :], ms[:, 0, :, :], ACT.Sqrt).then_inc(a_sq, 1)

                def seg_high(b, par, first):
                    ac.wait_ge(a_gn, b + 1)
                    if not first:
                        ac.wait_ge(a_tq, b - 1)
                        ac.wait_ge(a_tk, b - 1)
                    for w in range(2):
                        src = qn[:, par, w, :].rearrange("p (h d) -> p h d", h=H)
                        dst = seg[:, par, w, :, 0:2, :] if w == 0 else seg[:, par, w, :, 0:3:2, :]
                        ins = s.activation(dst, src.unsqueeze(2).to_broadcast([P, H, 2, HD]), ACT.Copy)
                    ins.then_inc(a_sh, 1)

                def copy_q(b, par):
                    ac.wait_ge(a_tq, b + 1)
                    s.activation(qT1[:, par, 0, :, :].rearrange("p c n -> p (c n)"), bank[2][:, :].bitcast(F16), ACT.Copy).then_inc(a_cq, 1)

                def take_o1(c, first):
                    ac.wait_ge(a_ot, c + 1)
                    if not first:
                        ac.wait_ge(a_op, c)
                    s.activation(OT1[:, :, :], bank[4][:, 0:KD * N].rearrange("p (k n) -> p k n", k=KD), ACT.Copy).then_inc(a_oc, 1)

                def exps1(b, first):
                    for g in range(NHG):
                        ac.wait_ge(a_st, 4 * b + g + 1)
                        if not first:
                            ac.wait_ge(a_pl, 4 * b - 3 + g)
                        s.activation(P1[:, HS * g:HS * g + HS, :], bank[g % 2][:, :].rearrange("p (h n) -> p h n", h=HS), ACT.Exp,
                                     scale=HD ** -0.5).then_inc(a_ex, 1)

                seg_high(0, 0, True)
                seg_high(1, 1, True)
                copy_q(0, 0)

                def probs_high1(b, first):
                    for g in range(NHG):
                        ac.wait_ge(a_ex, 4 * b + g + 1)
                        if g == 0 and not first:
                            ac.wait_ge(a_pv, b)
                        s.activation(P116[:, 0, HS * g:HS * g + HS, :], P1[:, HS * g:HS * g + HS, :], ACT.Copy).then_inc(a_ph, 1)

                def weights_high(h, par, q, first=False):
                    if q == 0:
                        ac.wait_ge(w_ld[par], (h - par) * 8 + 16)
                        if not first:
                            ac.wait_ge(w_st[par], (h - par) * 8)
                    c0, c1 = q * HC // NSP, (q + 1) * HC // NSP
                    s.activation(ws16[:, par, 0, c0:c1], ws[:, par, c0:c1], ACT.Copy).then_inc(w_hi, 1)

                def iteration1(b, par, c, has_q, has_x):
                    if c > 1:
                        take_o1(b - 2, c == 2)
                    if has_q:
                        copy_q(b + 1, 1 - par)
                    exps1(b, c == 0)
                    if has_x:
                        seg_high(b + 2, par, False)
                    probs_high1(b, c == 0)
                    if stages > 3:
                        for q in range(NSP):
                            weights_high(b, par, q, c < 2)

                iteration1(0, 0, 0, True, True)
                iteration1(1, 1, 1, True, True)
                iteration1(2, 0, 2, True, True)
                iteration1(3, 1, 3, True, True)
                with ac.Fori(2, B // 2 - 1) as i:
                    for par in range(2):
                        iteration1(i * 2 + par, par, 3, True, True)
                iteration1(B - 2, 0, 3, True, False)
                iteration1(B - 1, 1, 3, False, False)
                take_o1(B - 2, False)
                take_o1(B - 1, False)

            if stages > 3:
                ac.wait_ge(s_var, 4)
                s.activation(rstd_t[:, 1, :], rstd_t[:, 0, :], ACT.Sqrt).then_inc(s_sqrt, 1)

                def turned_m(b, par, first):
                    ac.wait_ge(m_xn, b + 1)
                    s.activation(xm16[:, bass.ds(b, 1), 0, :], xnm[:, par:par + 1, :], ACT.Copy).then_inc(m_xh, 1)
                    ac.wait_ge(m_xt, b + 1)
                    if not first:
                        ac.wait_ge(m_lg, b - 1)
                    s.activation(xTm[:, par, :, :], bank[par][:, 0:KD * N].rearrange("p (k n) -> p k n", k=KD), ACT.Copy).then_inc(m_xc, 1)

                turned_m(0, 0, True)
                turned_m(1, 1, True)
                with ac.Fori(1, B // 2) as i:
                    for par in range(2):
                        turned_m(i * 2 + par, par, False)
                ac.wait_ge(m_ex, 1)
                s.activation(ex[:, :, :], ex[:, :, :], ACT.Exp).then_inc(m_er, 1)

                def expert_a(t, par, first, nxt):
                    ac.wait_ge(m_w[par], (t - par) * 16 + 32)
                    for c in range(FC):
                        ac.wait_ge(m_h, FC * t + c + 1)
                        if not (first and c < 4):
                            ac.wait_ge(m_u, FC * t + c - 3)
                        s.activation(yg[:, c % 4, :], bank[c % 4][:, 0:MT], ACT.Gelu, bias=bms[:, par, c:c + 1]).then_inc(m_g, 1)
                        if c % 2 == 0 and c:
                            hidden_high(t, par, c // 2 - 1)
                    hidden_high(t, par, 3)

                def hidden_high(t, par, q):
                    ac.wait_ge(m_u, FC * t + 2 * q + 2)
                    s.activation(hm16[:, par, 0, 2 * q:2 * q + 2, :], hf[:, q % 2, :, :], ACT.Copy).then_inc(m_hh, 1)

                expert_a(0, 0, True, True)
                expert_a(1, 1, False, True)
                expert_a(2, 0, False, True)
                with ac.Fori(0, (NT - 5) // 2) as i:
                    for q in range(2):
                        expert_a(i * 2 + 3 + q, 1 - q, False, True)
                expert_a(NT - 2, 1, False, True)
                expert_a(NT - 1, 0, False, False)

        @block.tensor
        def _(pe):
            t = nc.tensor

            def turn_xn(b, c):
                pe.wait_ge(s_xn, b + 1)
                if c is None:
                    if b:
                        pe.wait_ge(s_xh, b)
                        pe.wait_ge(s_xl, b)
                else:
                    pe.wait_ge(s_oc, c)
                for kk in range(KD):
                    ins = t.transpose(bank[6][:, kk * N:(kk + 1) * N], xn[:, kk * P:(kk + 1) * P], ident[:, :])
                ins.then_inc(s_xt, 1)

            PAIRS = [(0, 0), (0, 1), (1, 0)]

            def project_qk(b, par, rs, first=False):
                pe.wait_ge(s_xh, b + 1)
                pe.wait_ge(s_xl, b + 1)
                for r in rs:
                    w = r // 2
                    src = (xn16, ctx16)[w]
                    if r == 2:
                        pe.wait_ge(s_ch, b + 1)
                        pe.wait_ge(s_cl, b + 1)
                    if not (first and r < 2):
                        pe.wait_ge(s_qe, 6 * b + r - 1)
                    for c in range(HS):
                        col = (HS * (r % 2) + c) * P
                        n = 0
                        for (wp, xp) in PAIRS:
                            for kk in range(KD):
                                ins = t.matmul(bank[4 + r % 2][:, c * N:(c + 1) * N], wqkv16[:, w, wp, kk, col:col + P],
                                               src[:, par, xp, kk, :], start=(n == 0), stop=(n == 5))
                                n += 1
                    ins.then_inc(s_qf, 1)

            def project_v(b, par):
                for r in range(2):
                    pe.wait_ge(s_qe, 6 * b + 4 + r - 1)
                    n = 0
                    for (wp, xp) in PAIRS:
                        for kk in range(KD):
                            ins = t.matmul(bank[4 + r][:, :], ctx16[:, par, xp, kk, :], wqkv16[:, 2, wp, kk, 512 * r:512 * r + 512],
                                           start=(n == 0), stop=(n == 5))
                            n += 1
                    ins.then_inc(s_qf, 1)

            def row_scores(b, par, gs, first):
                pe.wait_ge(s_qh, 4 * b + 4)
                for g in gs:
                    if g < 2:
                        if not first:
                            pe.wait_ge(s_exp, 4 * b - 4 + 3 + g)
                    else:
                        pe.wait_ge(s_red, 4 * b + g - 1)
                    half = 64 * (g % 2)
                    for i in range(HS):
                        ch = HS * (g // 2) + i
                        ins = t.matmul(bank[g % 2][:, i * N:(i + 1) * N], q16[half:half + 64, par, 0, 0, ch, :],
                                       q16[half:half + 64, par, 1, 0, ch, :], start=True, stop=True)
                    ins.then_inc(s_sm, 1)

            def scores(b, par, g):
                if g < 2:
                    pe.wait_ge(s_red, 4 * b + 3 + g)
                else:
                    pe.wait_ge(s_exp, 4 * b + g - 1)
                if g == 0:
                    pe.wait_ge(s_red, 4 * b + 4)
                    pe.wait_ge(s_ql, 4 * b + 4)
                half = 64 * (g % 2)
                for i in range(HS):
                    ch = HS * (g // 2) + i
                    o = bank[g % 2][:, i * N:(i + 1) * N]
                    sl = HS * g + i
                    t.matmul(o, nmx[:, sl:sl + 1].to_broadcast([P, N]), ident16[:, :], start=True, stop=False)
                    for n, (qp, kp) in enumerate(PAIRS):
                        ins = t.matmul(o, q16[half:half + 64, par, 1, kp, ch, :], q16[half:half + 64, par, 0, qp, ch, :],
                                       start=False, stop=(n == 2))
                ins.then_inc(s_st, 1)

            def gate(b, par, g, first, grp):
                if g == 0:
                    pe.wait_ge(s_flo, b + 1)
                    if first:
                        pe.wait_ge(s_whv, 3)
                if g < 2:
                    if not first:
                        pe.wait_ge(s_pm, 8 * b - 8 + 6 + 2 * g)
                else:
                    pe.wait_ge(s_pm, 8 * b + 2 * g - 2)
                bk = bank[2 + g % 2]
                for n, (lp, rp) in enumerate(PAIRS):
                    t.matmul(bk[:, :], Rm16[:, bass.ds(b, 1), rp, :], Lw16[:, grp, lp, 2 * g:2 * g + 2, :], start=(n == 0), stop=(n == 2))
                for jj in range(2):
                    j = 2 * g + jj
                    for n, (wp, fp) in enumerate(PAIRS):
                        ins = t.matmul(bk[:, jj * 256:(jj + 1) * 256], F16s[:, par, fp, j * N:(j + 1) * N], We16[:, wp, :], start=False,
                                       stop=(n == 2), skip_group_check=True)
                ins.then_inc(s_gf, 1)

            def pv(c, par, first):
                pe.wait_ge(s_pl, 4 * c + 4)
                pe.wait_ge(s_vl, 2 * c + 2)
                for f in range(4):
                    if f == 0:
                        pe.wait_ge(s_xh, xl_of(c))
                        pe.wait_ge(s_xl, xl_of(c))
                    elif f == 1:
                        if not first:
                            pe.wait_ge(s_opt, c)
                    else:
                        pe.wait_ge(s_oe, 4 * c + f - 1)
                    for i in range(HS):
                        sl = HS * f + i
                        for n, (pp, vp) in enumerate(PAIRS):
                            ins = t.matmul(bank[6 + f % 2][:, i * (DK + 1):(i + 1) * (DK + 1)], PT16[:, pp, sl, :], vv16[:, par, vp, sl, :],
                                           start=(n == 0), stop=(n == 2))
                    ins.then_inc(s_of, 1)

            def xl_of(c):
                return xl_cap[0] if xl_cap[0] else c + 3

            xl_cap = [0]

            def turn_o(c):
                for r in range(2):
                    pe.wait_ge(s_oe, 4 * c + 3 + r)
                    for i in range(4):
                        ch = 4 * r + i
                        ins = t.transpose(bank[6 + r][:, i * N:(i + 1) * N], O[:, ch * P:(ch + 1) * P], ident[:, :])
                    ins.then_inc(s_ot, 1)

            def project_o(c):
                pe.wait_ge(s_oc, 2 * c + 2)
                for ch in range(CH):
                    ins = t.matmul(bank[7][:, 0:D], OT[:, ch, :], WoT[:, ch, :], start=(ch == 0), stop=(ch == CH - 1))
                ins.then_inc(s_op, 1)

            pe.wait_ge(s_pp, 3)
            turn_xn(0, None)
            turn_xn(1, None)
            pe.wait_ge(s_wlo, 3)
            project_qk(0, 0, range(4), True)
            project_v(0, 0)

            def iteration(b, par, c, has_q, has_x, grp):
                row_scores(b, par, (0, 1), c == 0)
                if has_q:
                    project_qk(b + 1, 1 - par, (0, 1))
                row_scores(b, par, (2, 3), c == 0)
                if has_q:
                    project_qk(b + 1, 1 - par, (2, 3))
                if c:
                    pv(b - 1, 1 - par, c == 1)
                if has_q:
                    project_v(b + 1, 1 - par)
                if c:
                    turn_o(b - 1)
                if has_x:
                    turn_xn(b + 2, (None if c == 0 else 2 * b - 1))
                if c:
                    project_o(b - 1)
                scores(b, par, 0)
                gate(b, par, 0, c == 0, grp)
                scores(b, par, 1)
                gate(b, par, 1, c == 0, grp)
                scores(b, par, 2)
                scores(b, par, 3)
                gate(b, par, 2, c == 0, grp)
                gate(b, par, 3, c == 0, grp)

            iteration(0, 0, 0, True, True, 0)
            iteration(1, 1, 1, True, True, 0)
            with pe.Fori(0, 3) as i:
                for par in range(2):
                    iteration(i * 2 + 2 + par, par, 2, True, True, 0)
            with pe.Fori(0, 3) as i:
                for par in range(2):
                    iteration(i * 2 + 8 + par, par, 2, True, True, 1)
            iteration(B - 2, 0, 2, True, False, 1)
            xl_cap[0] = B
            iteration(B - 1, 1, 2, False, False, 1)
            pv(B - 1, 1, False)
            turn_o(B - 1)
            project_o(B - 1)

            if stages > 1:
                pe.wait_ge(f_ld, 64)
                pe.wait_ge(s_qe, 6 * B)
                pe.wait_ge(s_opt, B)
                t.matmul(bank[4][0:RANK, 0:D], lowr[:, FF:FF + RANK], lowr[:, FF + RANK:], start=True, stop=True).then_inc(f_mp, 1)
                pe.wait_ge(f_m, 1)
                for r in range(FC // 2):
                    for i in range(2):
                        c = 2 * r + i
                        ins = t.matmul(bank[r][:, i * D:(i + 1) * D], lowr[:, c * P:(c + 1) * P], lowm[:, :], start=True, stop=True)
                    ins.then_inc(f_lp, 1)
                for r in range(4):
                    kk, fh = r // 2, r % 2
                    pe.wait_ge(f_low, FC // 2)
                    for i in range(4):
                        c = 4 * fh + i
                        ins = t.transpose(bank[r][:, i * P:(i + 1) * P], wfa[:, c, kk * P:(kk + 1) * P], ident[:, :])
                    ins.then_inc(f_tp, 1)
                for r in range(4):
                    pe.wait_ge(f_lo, r + 1)
                    for i in range(4):
                        c, kk = 2 * r + i // 2, i % 2
                        ins = t.transpose(bank[r][:, i * P:(i + 1) * P], wpa[:, kk, c * P:(c + 1) * P], ident[:, :])
                    ins.then_inc(f_tp, 1)
                for kk in range(KD):
                    ins = t.matmul(bank[4][:, kk * P:(kk + 1) * P], thr[:, 0, FC + kk:FC + kk + 1].to_broadcast([P, P]), ident[:, :],
                                   start=True, stop=True)
                ins.then_inc(f_mp, 1)
                pe.wait_ge(f_m, 2)
                pe.wait_ge(f_hi, 8)

                def ffn_turn(g):
                    pe.wait_ge(f_xn, g + 1)
                    for kk in range(KD):
                        if g:
                            pe.wait_ge(f_xl, 2 * g - 1 + kk)
                        for i in range(GT):
                            ins = t.transpose(bank[4 + kk][:, i * N:(i + 1) * N], xng[:, g % 2, i, kk * P:(kk + 1) * P], ident[:, :])
                        ins.then_inc(f_xt, 1)

                def ffn_hidden(g):
                    pe.wait_ge(f_xh, 2 * g + 2)
                    pe.wait_ge(f_xl, 2 * g + 2)
                    for c in range(FC):
                        n = g * FC + c
                        if n > 3:
                            pe.wait_ge(f_r, n - 3)
                        m = 0
                        for (wp, xp) in PAIRS:
                            for kk in range(KD):
                                ins = t.matmul(bank[n % 4][:, :], W1T16[:, wp, kk, c * P:(c + 1) * P], xg16[:, g % 2, xp, kk, :],
                                               start=(m == 0), stop=(m == 5))
                                m += 1
                        ins.then_inc(f_h, 1)

                def ffn_out(g):
                    pe.wait_ge(f_l, FC * (g + 1))
                    for i in range(GT):
                        n = g * GT + i
                        if n > 1:
                            pe.wait_ge(f_ot, n - 1)
                        for m in range(2 * FC):
                            ins = t.matmul(bank[6 + n % 2][:, 0:D], h216[:, g % 2, m // FC, m % FC, i * N:(i + 1) * N], W2T16[:, m % FC, :],
                                           start=(m == 0), stop=(m == 2 * FC - 1))
                        ins.then_inc(f_o, 1)

                ffn_turn(0)
                for g in range(NG):
                    if g + 1 < NG:
                        ffn_turn(g + 1)
                    ffn_hidden(g)
                    if g:
                        ffn_out(g - 1)
                ffn_out(NG - 1)

            if stages > 2:
                pe.wait_ge(a_w, 1)
                pe.wait_ge(a_wl, 1)

                def turn1(b, par, first):
                    pe.wait_ge(a_xn, b + 1)
                    if not first:
                        pe.wait_ge(a_xh, b - 1)
                        pe.wait_ge(a_xl, b - 1)
                    for kk in range(KD):
                        ins = t.transpose(bank[par][:, kk * N:(kk + 1) * N], xn1[:, par, kk * P:(kk + 1) * P], ident[:, :])
                    ins.then_inc(a_xt, 1)

                def project1(b, par, first):
                    pe.wait_ge(a_xh, b + 1)
                    pe.wait_ge(a_xl, b + 1)
                    if not first:
                        pe.wait_ge(a_raw, b - 1)
                        pe.wait_ge(a_v, 2 * b - 2)
                    for src, bk, c0, c1, done in ((x116, bank[2 + par], 0, D, a_qf), (c116, bank[4 + par], D, 3 * D, a_kf)):
                        if done is a_kf:
                            pe.wait_ge(a_ch, b + 1)
                            pe.wait_ge(a_cl, b + 1)
                        n = 0
                        for (wp, xp) in PAIRS:
                            for kk in range(KD):
                                ins = t.matmul(bk[:, 0:c1 - c0], src[:, par, xp, kk, :], w1_16[:, wp, kk, c0:c1], start=(n == 0), stop=(n == 5))
                                n += 1
                        ins.then_inc(done, 1)

                turn1(0, 0, True)
                turn1(1, 1, True)
                project1(0, 0, True)
                project1(1, 1, True)
                with pe.Fori(1, B // 2) as i:
                    for par in range(2):
                        turn1(i * 2 + par, par, False)
                    for par in range(2):
                        project1(i * 2 + par, par, False)

                def turn_qk1(b, par, first):
                    for w, ready, done in ((0, a_cq, a_tq), (1, a_ck, a_tk)):
                        if w == 0:
                            pe.wait_ge(a_sh, b + 1)
                            pe.wait_ge(a_sl, b + 1)
                        if not first:
                            pe.wait_ge(ready, b)
                        bk = bank[2 + w][:, :].bitcast(F16)
                        for c in range(CH):
                            ins = t.transpose(bk[:, c * N:(c + 1) * N], seg[:, par, w, 2 * c:2 * c + 2, :, :].rearrange("p h s d -> p (h s d)"), ident16[:, :])
                        ins.then_inc(done, 1)

                def row_scores1(b, par, first):
                    pe.wait_ge(a_cq, b + 1)
                    pe.wait_ge(a_ck, b + 1)
                    for g in range(NHG):
                        if g < 2:
                            if not first:
                                pe.wait_ge(a_ex, 4 * b - 1 + g)
                        else:
                            pe.wait_ge(a_mx, 4 * b + g - 1)
                        half = 64 * (g % 2)
                        for i in range(HS):
                            ch = HS * (g // 2) + i
                            ins = t.matmul(bank[g % 2][:, i * N:(i + 1) * N], qT1[half:half + 64, par, 0, ch, :],
                                           qT1[half:half + 64, par, 1, ch, :], start=True, stop=True)
                        ins.then_inc(a_sm, 1)

                def scores1(b, par):
                    for g in range(NHG):
                        if g < 2:
                            pe.wait_ge(a_mx, 4 * b + 3 + g)
                        else:
                            pe.wait_ge(a_ex, 4 * b + g - 1)
                        half = 64 * (g % 2)
                        for i in range(HS):
                            ch = HS * (g // 2) + i
                            sl = HS * g + i
                            o = bank[g % 2][:, i * N:(i + 1) * N]
                            t.matmul(o, nmx1[:, sl:sl + 1].to_broadcast([P, N]), ident16[:, :], start=True, stop=False)
                            ins = t.matmul(o, qT1[half:half + 64, par, 1, ch, :], qT1[half:half + 64, par, 0, ch, :], start=False, stop=True)
                        ins.then_inc(a_st, 1)

                def pv1(c, first):
                    pe.wait_ge(a_ph, 4 * c + 4)
                    pe.wait_ge(a_pl, 4 * c + 4)
                    if not first:
                        pe.wait_ge(a_o, c)
                    for sl in range(H):
                        h = HEAD_OF[sl]
                        for n, (pp, vp) in enumerate(PAIRS):
                            ins = t.matmul(bank[6][:, h * (HD + 1):(h + 1) * (HD + 1)], P116[:, pp, sl, :],
                                           v1[:, bass.ds(c, 1), vp, h, :], start=(n == 0), stop=(n == 2))
                    ins.then_inc(a_pv, 1)

                def turn_o1(c, first):
                    pe.wait_ge(a_o, c + 1)
                    if not first:
                        pe.wait_ge(a_oc, c)
                    for kk in range(KD):
                        ins = t.transpose(bank[4][:, kk * N:(kk + 1) * N], O1[:, kk * P:(kk + 1) * P], ident[:, :])
                    ins.then_inc(a_ot, 1)

                def project_o1(c, first):
                    pe.wait_ge(a_oc, c + 1)
                    if not first:
                        pe.wait_ge(a_xu, c)
                    for kk in range(KD):
                        ins = t.matmul(bank[5][:, 0:D], OT1[:, kk, :], wpr[:, kk, :], start=(kk == 0), stop=(kk == KD - 1))
                    ins.then_inc(a_op, 1)

                pe.wait_ge(a_raw, B)
                pe.wait_ge(a_v, 2 * B)
                turn_qk1(0, 0, True)

                def iteration1(b, par, c, has_q):
                    row_scores1(b, par, c == 0)
                    if c > 1:
                        turn_o1(b - 2, c == 2)
                    if has_q:
                        turn_qk1(b + 1, 1 - par, False)
                    if c > 1:
                        project_o1(b - 2, c == 2)
                    scores1(b, par)
                    if c:
                        pv1(b - 1, c == 1)

                iteration1(0, 0, 0, True)
                iteration1(1, 1, 1, True)
                iteration1(2, 0, 2, True)
                iteration1(3, 1, 3, True)
                with pe.Fori(2, B // 2 - 1) as i:
                    for par in range(2):
                        iteration1(i * 2 + par, par, 3, True)
                iteration1(B - 2, 0, 3, True)
                iteration1(B - 1, 1, 3, False)
                turn_o1(B - 2, False)
                project_o1(B - 2, False)
                pv1(B - 1, False)
                turn_o1(B - 1, False)
                project_o1(B - 1, False)

            if stages > 3:
                pe.wait_ge(m_ld, 16)

                def turn_m(b, par, first):
                    pe.wait_ge(m_xn, b + 1)
                    if not first:
                        pe.wait_ge(m_xc, b - 1)
                    for kk in range(KD):
                        ins = t.transpose(bank[par][:, kk * N:(kk + 1) * N], xnm[:, par, kk * P:(kk + 1) * P], ident[:, :])
                    ins.then_inc(m_xt, 1)

                def logits(b, par):
                    pe.wait_ge(m_xc, b + 1)
                    for kk in range(KD):
                        ins = t.matmul(bank[7][:, bass.ds(b * E, E)], xTm[:, par, kk, :], rwt[:, kk, :], start=(kk == 0), stop=(kk == KD - 1))
                    ins.then_inc(m_lg, 1)

                turn_m(0, 0, True)
                turn_m(1, 1, True)
                logits(0, 0)
                logits(1, 1)
                with pe.Fori(1, B // 2) as i:
                    for par in range(2):
                        turn_m(i * 2 + par, par, False)
                    for par in range(2):
                        logits(i * 2 + par, par)
                pe.wait_ge(m_ex, 2)
                pe.wait_ge(m_c, 6)
                t.matmul(bank[6][:, 0:256], tri[:, :], oh16[:, :], start=True, stop=True)
                t.matmul(bank[6][:, 256:512], one16[:, :], oh16[:, :], start=True, stop=True).then_inc(m_pr, 1)

                def turn_tokens(t_, par, first):
                    pe.wait_ge(m_x[par], (t_ - par) * 8 + 16)
                    if not first:
                        pe.wait_ge(m_tc, t_)
                    bk = bank[4][:, :].bitcast(F16)
                    for a4 in range(2 * KD):
                        for h in range(MT // P):
                            ins = t.transpose(bk[:, a4 * MT + h * P:a4 * MT + (h + 1) * P], xin[:, par, h, a4 * P:(a4 + 1) * P], ident16[:, :])
                    ins.then_inc(m_tt, 1)

                def hidden(t_, par, c0, c1, first):
                    for c in range(c0, c1):
                        if c == 0:
                            pe.wait_ge(m_tc, t_ + 1)
                            pe.wait_ge(m_w[par], (t_ - par) * 16 + 32)
                        if not (first and c < 4):
                            pe.wait_ge(m_u, FC * t_ + c - 3)
                        for w in range(2):
                            n = 0
                            for (wp, xp) in PAIRS:
                                for kk in range(KD):
                                    col = (w * KD + kk) * FF + c * P
                                    ins = t.matmul(bank[c % 4][:, w * MT:(w + 1) * MT], wm16[:, par, wp, col:col + P], xT16[:, par, xp * KD + kk, :],
                                                   start=(n == 0), stop=(n == 5))
                                    n += 1
                        ins.then_inc(m_h, 1)

                def expert_out(t_, par, first):
                    pe.wait_ge(m_hl, 4 * t_ + 4)
                    pe.wait_ge(m_wd[par], (t_ - par) * 16 + 32)
                    if not first:
                        pe.wait_ge(m_y, t_ - 1)
                    for h in range(MT // P):
                        n = 0
                        for (wp, xp) in PAIRS:
                            for c in range(FC):
                                col = 2 * KD * FF + c * D
                                ins = t.matmul(bank[5 + par][:, h * D:(h + 1) * D], hm16[:, par, xp, c, h * P:(h + 1) * P], wm16[:, par, wp, col:col + D],
                                               start=(n == 0), stop=(n == 3 * FC - 1))
                                n += 1
                    ins.then_inc(m_o, 1)

                def expert_p(t_, par, prev, nxt, first=False):
                    hidden(t_, par, 0, 2, first)
                    if prev:
                        expert_out(t_ - 1, 1 - par, prev == 1)
                    if nxt:
                        turn_tokens(t_ + 1, 1 - par, False)
                    hidden(t_, par, 2, 8, first)

                turn_tokens(0, 0, True)
                expert_p(0, 0, 0, True, True)
                expert_p(1, 1, 1, True)
                expert_p(2, 0, 1, True)
                with pe.Fori(0, (NT - 5) // 2) as i:
                    for q in range(2):
                        expert_p(i * 2 + 3 + q, 1 - q, 2, True)
                expert_p(NT - 2, 1, 2, True)
                expert_p(NT - 1, 0, 2, False)
                expert_out(NT - 1, 0, False)


def arrange(inputs):
    f = lambda n: np.asarray(inputs[n], np.float32)
    c = np.ascontiguousarray
    boxes = f("fside_BxSx4_0")
    heads = np.array(HEAD_OF)
    cols = (heads[:, None] * DK + np.arange(DK)[None, :]).reshape(-1)
    a = {"x": f("x"), "g_xattn": f("g_xattn"), "g_ffn": f("g_ffn")}
    a["ctxT"] = c(f("ctx_1024").reshape(T, D).T)
    lohi = boxes.reshape(B, NJ, NN, 2, 2)
    bn = lohi.transpose(4, 2, 0, 1, 3)
    a["boxn"] = c(np.broadcast_to(bn[:, None], (2, 4, NN, B, NJ, 2)).reshape(P, B * NJ, 2))
    a["boxm"] = c(boxes.reshape(T, 2, 2).transpose(2, 1, 0))
    delta = np.array([(s >> 1) & 1 if s < 8 else 0 for s in range(SLOTS)])
    wh = boxes.reshape(2, 8, N, 2, 2)[..., delta]
    a["whc"] = c(wh.transpose(1, 4, 0, 3, 2).reshape(P, 2, 2, N))
    Wg = f("L0_xattn_Wg")[heads]
    feat = lambda sc, dl, fr: Wg[:, sc * 8 + dl * 2 + fr]
    We = np.zeros((2, 2, 2, NN, H, NN), np.float32)
    for xy in range(2):
        for sc in range(2):
            for fr in range(2):
                for nn in range(NN):
                    We[xy, sc, fr, nn, :, nn] = feat(sc, xy, fr)
    a["We"] = We.reshape(P, H * NN)
    AB = np.zeros((SLOTS, 2, H), np.float32)
    for s in range(4):
        dl, fr = 2 + (s >> 1), s & 1
        AB[s, 0], AB[s, 1] = feat(1, dl, fr), feat(0, dl, fr)
        AB[4 + s, 0], AB[4 + s, 1] = feat(0, dl, fr), feat(1, dl, fr)
    AB[8, 1] = f("L0_xattn_bg")[heads]
    a["AB"] = c(np.broadcast_to(AB[None], (8, SLOTS, 2, H)).reshape(P, 2, H))
    turn = [100.0 / (1000.0 ** (fr / 2)) / (2 * np.pi) for fr in range(2)]
    cst = np.zeros((P, 8), np.float32)
    for p in range(P):
        sc, fr = (p >> 5) & 1, (p >> 4) & 1
        cst[p, 0], cst[p, 1] = turn[fr], 0.25 * sc
        s = p % SLOTS
        cst[p, 2] = turn[s & 1] if s < 8 else 0.0
        cst[p, 3], cst[p, 4], cst[p, 5] = 0.0, (-0.25 if s < 4 else 0.25), (0.0 if s < 4 else 0.25)
    a["cst"] = cst
    a["mask"] = c((np.arange(P)[:, None] // SLOTS == np.arange(8)[None, :]).astype(np.float32))
    a["wqkv"] = np.stack([f("L0_xattn_Wq").T, f("L0_xattn_Wk").T, f("L0_xattn_Wv")[cols].T])
    a["bqk"] = c(np.stack([f("L0_xattn_bq").reshape(CH, P).T, f("L0_xattn_bk").reshape(CH, P).T], 1))
    a["bv"] = c(f("L0_xattn_bv")[cols])
    a["woT"] = c(f("L0_xattn_Wo")[:, cols].T)
    a["bo"] = f("L0_xattn_bo")
    a["w_fc"], a["w_proj"] = f("L0_ffn_w_fc"), f("L0_ffn_w_proj")
    a["low"] = c(np.concatenate([f("L0_ffn_u").T, f("L0_ffn_fast_b").T, f("L0_ffn_v")], 1))
    a["wq1"], a["wkv1"], a["wpr1"] = f("L1_xattn_Wq"), f("L1_xattn_Wkv"), f("L1_xattn_Wproj")
    a["gq"], a["gk"] = np.tile(f("L1_xattn_q_gamma"), H), np.tile(f("L1_xattn_k_gamma"), H)
    a["rwt"] = c(f("L1_ffn_router_w").T)
    turned = lambda n: f(n).transpose(0, 2, 1).reshape(E, KD, P, FF).transpose(0, 2, 1, 3).reshape(E, P, KD * FF)
    down = f("L1_ffn_w2_w").transpose(0, 2, 1).reshape(E, FC, P, D).transpose(0, 2, 1, 3).reshape(E, P, FC * D)
    bias = lambda n: f(n).reshape(E, FC, P).transpose(0, 2, 1)
    a["wcat"] = c(np.concatenate([turned("L1_ffn_wg_w"), turned("L1_ffn_w1_w"), down, bias("L1_ffn_wg_b"), bias("L1_ffn_w1_b")], 2))
    a["b2"] = f("L1_ffn_w2_b")
    a["fgate"] = f("L0_ffn_gate").reshape(1)
    return a


def kernel(**inputs):
    import concourse.bacc as bacc
    from concourse.bass_utils import run_bass_kernel_spmd

    nc = bacc.Bacc("TRN2", target_bir_lowering=False, num_devices=1)
    arrays = {f"in_{n}": np.ascontiguousarray(v) for n, v in arrange(inputs).items()}
    aps = {n[3:]: nc.dram_tensor(n, v.shape, mybir.dt.from_np(v.dtype), kind="ExternalInput").ap() for n, v in arrays.items()}
    aps["out"] = nc.dram_tensor("out_x", (B, N, D), F32, kind="ExternalOutput").ap()
    build(nc, aps)
    r = run_bass_kernel_spmd(nc, [arrays], core_ids=[0])
    return r.results[0]["out_x"]
```

```python
from contextlib import ExitStack

import numpy as np
import concourse.bass as bass
from concourse import mybir

ALU = mybir.AluOpType
ACT = mybir.ActivationFunctionType
AX = mybir.AxisListType
F32 = mybir.dt.float32
F16 = mybir.dt.float16
I32 = mybir.dt.int32
U32 = mybir.dt.uint32

P = 128
B = 16
N = 128
D = 256
T = B * N
KD = D // P
H = 16
DK = 64
HD = D // H
CH = H * DK // P
NN = 16
NJ = N // NN
HS = 4
NHG = H // HS
SLOTS = 16
WSC = 64.0
GSC = 1024.0
FF = 1024
FC = FF // P
E = 8
MT = 256
NT = (2 * T + E * (MT - 1)) // MT
WM = 2 * KD * FF + FC * D
HC = WM // 2
NSP = 3
WB = WM + 2 * FC
GT = 4
NG = B // GT
RANK = 16
ROUND = 12582912.0
TWO_PI = 6.2831845

HEAD_OF = [8 * (g // 2) + 2 * i + g % 2 for g in range(NHG) for i in range(HS)]


class Count:

    def __init__(self, sem):
        self.sem, self.n = sem, 0

    def up(self, ins):
        ins.then_inc(self.sem, 1)
        self.n += 1
        return self.n


def build(nc, a):
    with ExitStack() as ctx:
        def sem(name):
            return ctx.enter_context(nc.semaphore(name))

        def sb(name, shape, dt=F32, scope=None):
            return (scope or ctx).enter_context(nc.sbuf_tensor(name, shape, dt))

        bank = [ctx.enter_context(nc.psum_tensor(f"bank{i}", [P, 512], F32)) for i in range(8)]

        X = sb("X", [P, B, D])
        mv = sb("mv", [P, B, 2])
        bst = sb("bst", [P, B, 6])
        rstd = sb("rstd", [P, B])
        rstd_t = sb("rstd_t", [P, 3, B])
        ident = sb("ident", [P, P])
        ident16 = sb("ident16", [P, P], F16)
        gates = sb("gates", [P, 4])
        tg = sb("tg", [P, 4])
        xn = sb("xn", [P, D])

        zero = sb("zero", [P, 2 * D], F16)

        early = ExitStack()
        fu = sb("fu", [P, 2, NJ * N], F32, early)
        fks = sb("fks", [P, 2, NJ * N], F32, early)
        fk, fs = fks[:, 0, :], fks[:, 1, :]
        cm = sb("cm", [P, T], F32, early)
        cn = sb("cn", [P, B * NJ], F32, early)
        rw = sb("rw", [P, B * NJ], F32, early)
        cst = sb("cst", [P, 8], F32, early)
        wqkv16 = sb("wqkv16", [P, 3, 2, KD, H * DK], F16, early)
        thr = sb("thr", [P, 4, FC + KD], F32, early)
        fgate = sb("fgate", [P, 1], F32, early)
        wfc, wpj, wfa = (wqkv16[:, j, :, :, :].rearrange("p r k f -> p (r k f)").bitcast(F32) for j in range(3))
        wfc, wfa = (w.rearrange("p (c d) -> p c d", c=FC) for w in (wfc, wfa))
        wpj = wpj.rearrange("p (c f) -> p c f", c=KD)
        wfb = fu[:, :, :].rearrange("p r c -> p (r c)").rearrange("p (c d) -> p c d", c=FC)
        wpa = fks[:, :, :]
        lowr = cm[0:RANK, 0:FF + RANK + D]
        lowm = cm[0:RANK, FF + RANK + D:FF + RANK + 2 * D]
        l0 = ExitStack()
        F16s = sb("F16s", [P, 2, 2, NJ * N], F16, l0)
        Lw16 = sb("Lw16", [P, 2, 2, NJ, H * NN], F16, l0)
        wht = sb("wht", [P, 3, 2, N], F32, l0)
        AB = sb("AB", [P, 2, H], F32, l0)
        Lp = sb("Lp", [P, 2, H, NN], F32, l0)
        Rm16 = sb("Rm16", [P, B, 2, N], F16, l0)
        We = sb("We", [P, H * NN], F32, l0)
        We16 = sb("We16", [P, 2, H * NN], F16, l0)
        WoT = sb("WoT", [P, CH, D], F32, l0)
        bqk = sb("bqk", [P, 2, CH], F32, l0)
        bv = sb("bv", [P, H * DK], F32, l0)
        bo = sb("bo", [P, D], F32, l0)
        att = ExitStack()
        q16 = sb("q16", [P, 2, 2, 2, CH, N], F16, att)
        qt = sb("qt", [P, 4, HS, N], F32, att)
        vf = sb("vf", [P, 2, 8, DK], F32, att)
        vv16 = sb("vv16", [P, 2, 2, H, DK + 1], F16, att)
        ctxf = sb("ctxf", [P, 2, KD, N], F32, att)
        ctx16 = sb("ctx16", [P, 2, 2, KD, N], F16, att)
        xn16 = sb("xn16", [P, 2, 2, KD, N], F16, att)
        nmx = sb("nmx", [P, H], F16, att)
        rden = sb("rden", [P, 2, HS], F32, att)
        warm = sb("warm", [P, 1], F32, att)
        otmp = sb("otmp", [P, D], F32, att)
        pre = ExitStack()
        rows = sb("rows", [P, T], F32, pre)
        boxn = sb("boxn", [P, B * NJ, 2], F32, pre)
        whc = sb("whc", [P, 2, 2, N], F32, pre)
        wha = sb("wha", [P, 2, N], F32, pre)
        whk = sb("whk", [P, 3, 2, N], F32, pre)
        mask = sb("mask", [P, 8], F32, pre)
        wst = [q16[:, r, :, :, :, :].rearrange("p a b c n -> p (a b c n)").bitcast(F32).rearrange("p (k f) -> p k f", k=KD) for r in range(2)]
        wst.append(sb("wst", [P, KD, H * DK], F32, pre)[:, :, :])
        pre.close()
        EX = sb("EX", [P, H, N], F32, att)
        PT = sb("PT", [P, H, N], F32, att)
        PT16 = sb("PT16", [P, 2, H, N], F16, att)
        O = sb("O", [P, H * DK], F32, att)
        OT = sb("OT", [P, CH, N], F32, att)
        att.close()
        l0.close()

        l1w = ExitStack()
        wst1 = sb("wst1", [P, KD, 3 * D], F32, l1w)
        w1_16 = sb("w1_16", [P, 2, KD, 3 * D], F16, l1w)
        wpr = sb("wpr", [P, KD, D], F32, l1w)
        gam = sb("gam", [P, 2, D], F32, l1w)
        ws = sb("ws", [P, 2, HC], F32, l1w)
        ws16 = sb("ws16", [P, 2, 2, HC], F16, l1w)

        l0f = ExitStack()
        W1T16 = sb("W1T16", [P, 2, KD, FF], F16, l0f)
        W2T16 = sb("W2T16", [P, FC, D], F16, l0f)
        w2row = sb("w2row", [P, D], F32, l0f)
        xg16 = sb("xg16", [P, 2, 2, KD, GT * N], F16, l0f)
        hr = sb("hr", [P, 2, GT * N], F32, l0f)
        h2 = sb("h2", [P, 2, GT * N], F32, l0f)
        h216 = sb("h216", [P, 2, 2, FC, GT * N], F16, l0f)
        xng = sb("xng", [P, 2, GT, D], F32, l0f)
        ftmp = sb("ftmp", [P, 2, D], F32, l0f)
        l0f.close()

        l1 = ExitStack()
        ms = sb("ms", [P, 4, B, 2 * H], F32, l1)
        sq = sb("sq", [P, 2, 2, D], F32, l1)
        xn1 = sb("xn1", [P, 2, D], F32, l1)
        x116 = sb("x116", [P, 2, 2, KD, N], F16, l1)
        c1f = sb("c1f", [P, 2, KD, N], F32, l1)
        c116 = sb("c116", [P, 2, 2, KD, N], F16, l1)
        qn = sb("qn", [P, 2, 2, D], F32, l1)
        seg = sb("seg", [P, 2, 2, H, 4, HD], F16, l1)
        qT1 = sb("qT1", [P, 2, 2, CH, N], F16, l1)
        vb1 = sb("vb1", [P, 2, 2, H * (HD + 1)], F16, l1)
        P1 = sb("P1", [P, H, N], F32, l1)
        P116 = sb("P116", [P, 2, H, N], F16, l1)
        O1 = sb("O1", [P, D], F32, l1)
        OT1 = sb("OT1", [P, KD, N], F32, l1)
        rden1 = sb("rden1", [P, H], F32, l1)
        nmx1 = sb("nmx1", [P, H], F16, l1)
        l1.close()
        l1w.close()
        early.close()
        l1e = ExitStack()
        raw = sb("raw", [P, B, 2, D], F32, l1e)
        v1 = sb("v1", [P, B, 2, H, HD + 1], F16, l1e)
        l1e.close()

        mo = ExitStack()
        rwt = sb("rwt", [P, KD, E], F32, mo)
        xnm = sb("xnm", [P, 2, D], F32, mo)
        xm16 = sb("xm16", [P, B, 2, D], F16, mo)
        xTm = sb("xTm", [P, 2, KD, N], F32, mo)
        lg = sb("lg", [P, B, E], F32, mo)
        top = sb("top", [P, B, 8], F32, mo)
        topi = sb("topi", [P, B, 8], U32, mo)
        ex = sb("ex", [P, B, E + 1], F32, mo)
        den = sb("den", [P, 2, B], F32, mo)
        wk = sb("wk", [P, 2, B], F32, mo)
        idf = sb("idf", [P, B, 2], F32, mo)
        oh = sb("oh", [P, E, B * 2], F32, mo)
        oh16 = sb("oh16", [P, E * B * 2], F16, mo)
        tot = sb("tot", [P, E * B * 2], F32, mo)
        cum = sb("cum", [P, E * B * 2], F32, mo)
        pos = sb("pos", [P, E, B * 2], F32, mo)
        one = sb("one", [P, E * B * 2], F32, mo)
        cnt = sb("cnt", [P, 6, E], F32, mo)
        slotf = sb("slotf", [P, B * 2], F32, mo)
        slot = sb("slot", [P, B * 2], U32, mo)
        tri = sb("tri", [P, P], F16, mo)
        one16 = sb("one16", [P, P], F16, mo)
        ioe = sb("ioe", [P, E], F32, mo)
        iot = sb("iot", [P, NT], F32, mo)
        cmp = sb("cmp", [P, NT, E], F32, mo)
        etf = sb("etf", [P, NT], F32, mo)
        eti = sb("eti", [P, NT], I32, mo)
        chg = sb("chg", [P, NT], I32, mo)
        wm16 = sb("wm16", [P, 2, 2, WM], F16, mo)
        bms = sb("bms", [P, 2, 2 * FC], F32, mo)
        b2r = sb("b2r", [P, 2, D], F32, mo)
        xin = sb("xin", [P, 2, MT // P, 2 * D], F16, mo)
        xT16 = sb("xT16", [P, 2, 2 * KD, MT], F16, mo)
        yg = sb("yg", [P, 4, MT], F32, mo)
        hf = sb("hf", [P, 2, 2, MT], F32, mo)
        hm16 = sb("hm16", [P, 2, 2, FC, MT], F16, mo)
        ys = sb("ys", [P, 2, MT // P, D], F32, mo)
        yk = sb("yk", [P, 4, 2, D], F32, mo)
        early_gelu = sb("early_gelu", [P, 1], F32, mo)
        mo.close()
        w16_dram = nc.dram_tensor("expert_weights", [E, P, 2, WM], F16)
        xs_dram = nc.dram_tensor("expert_tokens", [NT * MT, 2 * D], F16)
        ys_dram = nc.dram_tensor("expert_outputs", [NT * MT, D], F32)

        s_var, s_sqrt = sem("var_ready"), sem("sqrt_ready")
        s_whv, s_wha = sem("sizes_vector"), sem("sizes_scalar")
        s_tg = sem("tanh_ready")
        s_x, s_c, s_cs, s_cw = sem("x_loaded"), sem("consts_loaded"), sem("sizes_loaded"), sem("boxes_loaded")
        s_w, s_whi = [sem(f"{n}_weight_staged") for n in "qkv"], sem("weight_split_hi")
        s_wlo = sem("weight_split_lo")
        s_o = sem("out_weights_loaded")
        s_pv, s_pp = sem("prefix_vector"), sem("prefix_pool")
        s_fd, s_fv, s_fa, s_fhi, s_flo = (sem("gate_" + n) for n in ("difference", "vector", "scalar", "high", "low"))
        s_xn, s_xt, s_xh, s_xl = sem("xn_ready"), sem("xn_turned"), sem("xn_high"), sem("xn_low")
        s_cf, s_ch, s_cl = [sem("ctx_loaded_even"), sem("ctx_loaded_odd")], sem("ctx_high"), sem("ctx_low")
        s_qf, s_qe, s_qh, s_ql = sem("qkv_full"), sem("qkv_taken"), sem("qk_high"), sem("qk_low")
        s_sm, s_red = sem("row_scores"), sem("row_max")
        s_st, s_exp = sem("scores_full"), sem("exp_done")
        s_gf, s_pm, s_ph, s_pl = sem("gate_full"), sem("probs_ready"), sem("probs_high"), sem("probs_low")
        s_vh, s_vl = sem("values_high"), sem("values_low")
        s_of, s_rd, s_oe = sem("pv_full"), sem("den_inverse"), sem("pv_taken")
        s_ot, s_oc = sem("o_turned"), sem("o_turned_taken")
        s_op, s_opt, s_xu, s_bs, s_bn = sem("proj_full"), sem("proj_taken"), sem("x_updated"), sem("bn_stats_done"), sem("stats_ready")
        s_out = sem("stored")
        f_ld, f_m, f_lp, f_low, f_tp, f_hi, f_lo = (sem("ffn_" + n) for n in (
            "weights_loaded", "small_copied", "low_rank_full", "low_rank_added", "weights_turned",
            "weights_high", "weights_low"))
        f_mp = sem("ffn_small_full")
        f_xn, f_xt, f_xh, f_xl = (sem("ffn_" + n) for n in ("xn_ready", "xn_turned", "xn_high", "xn_low"))
        f_h, f_r, f_sq, f_h2, f_l = (sem("ffn_" + n) for n in ("hidden_full", "relu_done", "square_high", "square_done", "square_low"))
        m_ld, m_zf = sem("router_loaded"), sem("slots_zeroed")
        m_xn, m_xt, m_xc, m_xh, m_xl = (sem("router_" + n) for n in ("xn_ready", "xn_turned", "xn_copied", "xn_high", "xn_low"))
        m_lg, m_ex, m_er, m_pr, m_sl, m_c = (sem("route_" + n) for n in (
            "logits_full", "exponents_then_onehot_ready", "exp_done", "counts_full", "slots_ready", "constants_ready"))
        m_v = sem("route_vector")
        m_sc = sem("tokens_scattered")
        m_w = [sem("expert_weights_even"), sem("expert_weights_odd")]
        m_x = [sem("expert_tokens_even"), sem("expert_tokens_odd")]
        m_wd = [sem("expert_down_even"), sem("expert_down_odd")]
        w_ld = [sem("half_expert_loaded_even"), sem("half_expert_loaded_odd")]
        w_hi, w_lo = sem("half_expert_high"), sem("half_expert_low")
        w_st = [sem("half_expert_stored_even"), sem("half_expert_stored_odd")]
        m_tt, m_tc = sem("expert_tokens_turned"), sem("expert_tokens_copied")
        m_h, m_g, m_u, m_hh, m_hl = (sem("expert_" + n) for n in ("hidden_full", "gelu_done", "product_done", "hidden_high", "hidden_low"))
        m_o, m_y = sem("expert_out_full"), sem("expert_out_taken")
        m_ys = [sem("expert_stored_even"), sem("expert_stored_odd")]
        m_gk = [sem(f"gathered_{i}") for i in range(4)]
        m_f = sem("x_final")
        a_ld, a_w, a_wl = (sem("l1_" + n) for n in ("weights_loaded", "weights_high", "weights_low"))
        a_xn, a_xt, a_xh, a_xl = (sem("l1_" + n) for n in ("xn_ready", "xn_turned", "xn_high", "xn_low"))
        a_cf = [sem("l1_ctx_loaded_even"), sem("l1_ctx_loaded_odd")]
        a_ch, a_cl = sem("l1_ctx_high"), sem("l1_ctx_low")
        a_qf, a_kf, a_raw, a_red, a_v = (sem("l1_" + n) for n in ("q_full", "kv_full", "raw_copied", "squares_summed", "v_copied"))
        a_ms, a_sq = sem("l1_mean_ready"), sem("l1_root_ready")
        a_qn, a_gn, a_sh, a_sl = (sem("l1_" + n) for n in ("qk_scaled", "k_gamma_done", "segments_high", "segments_low"))
        a_tq, a_tk, a_cq, a_ck = (sem("l1_" + n) for n in ("q_turned", "k_turned", "q_copied", "k_copied"))
        a_sm, a_mx, a_st, a_ex, a_ph, a_pl = (sem("l1_" + n) for n in ("row_scores", "row_max", "scores_full", "exp_done", "probs_high", "probs_low"))
        a_pv, a_rd, a_o, a_ot, a_oc, a_op, a_xu = (sem("l1_" + n) for n in (
            "pv_full", "den_inverse", "pv_taken", "o_turned", "o_turned_taken", "proj_full", "x_updated"))
        f_o, f_ot, f_xu = sem("ffn_out_full"), sem("ffn_out_taken"), sem("ffn_x_updated")

        block = ctx.enter_context(nc.Block())

        @block.sync
        def _(sp):
            def load_ctx(b, par):
                sp.dma_start(ctxf[:, par, :, :], a["ctxT"][:, bass.ds(b * N, N)].rearrange("(k p) n -> p k n", p=P)).then_inc(s_cf[par], 16)

            sp.dma_start(cst[:, :], a["cst"]).then_inc(s_cs, 16)
            sp.dma_start(whc[:, :, :, :], a["whc"]).then_inc(s_cs, 16)
            sp.dma_start(AB[:, :, :], a["AB"]).then_inc(s_cs, 16)
            sp.dma_start(mask[:, :], a["mask"]).then_inc(s_cs, 16)
            sp.dma_start(We[:, :], a["We"]).then_inc(s_cs, 16)
            for j in range(3):
                sp.dma_start(wst[j], a["wqkv"][j].rearrange("(k p) f -> p k f", p=P)).then_inc(s_w[j], 16)
                if j == 1:
                    load_ctx(0, 0)
                    load_ctx(1, 1)
            sp.dma_start(boxn[:, :, :], a["boxn"]).then_inc(s_cw, 16)
            for xy in range(2):
                for e in range(2):
                    sp.dma_start((cm, rows)[e][64 * xy:64 * xy + 64, :], a["boxm"][xy, e, :].partition_broadcast(64)).then_inc(s_cw, 16)
            sp.dma_start(bqk[:, :, :], a["bqk"]).then_inc(s_o, 16)
            sp.dma_start(bv[:, :], a["bv"].partition_broadcast(P)).then_inc(s_o, 16)
            sp.dma_start(bo[:, :], a["bo"].partition_broadcast(P)).then_inc(s_o, 16)
            sp.dma_start(WoT[:, :, :], a["woT"].rearrange("(c p) f -> p c f", p=P)).then_inc(s_o, 16)
            with sp.Fori(0, B // 2 - 1) as i:
                for par in range(2):
                    b = i * 2 + par
                    sp.wait_ge(s_ch, b + 1)
                    sp.wait_ge(s_cl, b + 1)
                    load_ctx(b + 2, par)
            sp.wait_ge(s_qf, 6 * B)
            sp.wait_ge(s_fd, B)
            sp.dma_start(wfc, a["w_fc"].rearrange("(c p) d -> p c d", p=P)).then_inc(f_ld, 16)
            sp.dma_start(wpj, a["w_proj"].rearrange("(c p) f -> p c f", p=P)).then_inc(f_ld, 16)
            sp.dma_start(lowr, a["low"]).then_inc(f_ld, 16)
            sp.dma_start(fgate[:, :], a["fgate"].partition_broadcast(P)).then_inc(f_ld, 16)
            sp.wait_ge(s_op, B)
            sp.wait_ge(s_xu, B)
            sp.wait_ge(s_oc, 2 * B)
            sp.wait_ge(s_ql, 4 * B)
            sp.wait_ge(s_cl, B)
            sp.dma_start(wst1[:, :, 0:D], a["wq1"].rearrange("(k p) f -> p k f", p=P)).then_inc(a_ld, 16)
            sp.dma_start(wst1[:, :, D:], a["wkv1"].rearrange("(k p) f -> p k f", p=P)).then_inc(a_ld, 16)
            sp.dma_start(wpr[:, :, :], a["wpr1"].rearrange("(k p) f -> p k f", p=P)).then_inc(a_ld, 16)
            sp.dma_start(gam[:, 0, :], a["gq"].partition_broadcast(P)).then_inc(a_ld, 16)
            sp.dma_start(gam[:, 1, :], a["gk"].partition_broadcast(P)).then_inc(a_ld, 16)
            sp.wait_ge(f_xu, B)

            def load_ctx1(b, par):
                sp.dma_start(c1f[:, par, :, :], a["ctxT"][:, bass.ds(b * N, N)].rearrange("(k p) n -> p k n", p=P)).then_inc(a_cf[par], 16)

            load_ctx1(0, 0)
            load_ctx1(1, 1)
            with sp.Fori(0, B // 2 - 1) as i:
                for par in range(2):
                    b = i * 2 + par
                    sp.wait_ge(a_ch, b + 1)
                    sp.wait_ge(a_cl, b + 1)
                    load_ctx1(b + 2, par)
            def store_half(e, half):
                sp.wait_ge(w_hi, (e * 2 + half) * NSP + NSP)
                sp.wait_ge(w_lo, (e * 2 + half) * NSP + NSP)
                sp.dma_start(w16_dram.ap()[bass.ds(e, 1), :, :, half * HC:(half + 1) * HC].rearrange("o p r c -> (o p) r c"), ws16[:, half, :, :]).then_inc(w_st[half], 16)

            def load_half(e, half):
                sp.dma_start(ws[:, half, :], a["wcat"][bass.ds(e, 1), :, half * HC:(half + 1) * HC].rearrange("o p c -> (o p) c")).then_inc(w_ld[half], 16)

            load_half(0, 0)
            load_half(0, 1)
            with sp.Fori(0, E - 1) as e:
                for half in range(2):
                    store_half(e, half)
                    load_half(e + 1, half)
            store_half(E - 1, 0)
            store_half(E - 1, 1)
            sp.wait_ge(a_xu, B)
            sp.wait_ge(a_op, B)
            sp.wait_ge(w_st[0], 16 * E)
            sp.wait_ge(w_st[1], 16 * E)
            sp.dma_start(rwt[:, :, :], a["rwt"].rearrange("(k p) e -> p k e", p=P)).then_inc(m_ld, 16)
            sp.wait_ge(m_sl, 2)

            def load_hidden(t, par, first):
                e = sp.value_load(eti[0:1, bass.ds(t, 1)], min_val=0, max_val=E - 1)
                new = sp.value_load(chg[0:1, bass.ds(t, 1)], min_val=0, max_val=1)
                if not first:
                    sp.wait_ge(m_u, FC * (t - 1))
                sp.dma_start(wm16[:, par, :, 0:2 * KD * FF], w16_dram.ap()[bass.ds(e, 1), :, :, 0:2 * KD * FF].rearrange("o p r c -> (o p) r c"),
                             cond=new).then_inc(m_w[par], 16)
                sp.dma_start(bms[:, par, :], a["wcat"][bass.ds(e, 1), :, WM:WB].rearrange("o p c -> (o p) c")).then_inc(m_w[par], 16)

            def load_down(t, par, first):
                e = sp.value_load(eti[0:1, bass.ds(t, 1)], min_val=0, max_val=E - 1)
                new = sp.value_load(chg[0:1, bass.ds(t, 1)], min_val=0, max_val=1)
                if not first:
                    sp.wait_ge(m_y, t - 1)
                sp.dma_start(wm16[:, par, :, 2 * KD * FF:], w16_dram.ap()[bass.ds(e, 1), :, :, 2 * KD * FF:].rearrange("o p r c -> (o p) r c"),
                             cond=new).then_inc(m_wd[par], 16)
                sp.dma_start(b2r[:, par, :], a["b2"][bass.ds(e, 1), :].rearrange("o c -> (o c)").partition_broadcast(P)).then_inc(m_wd[par], 16)

            def load_tokens(t, par, first):
                if not first:
                    sp.wait_ge(m_tt, t - 1)
                sp.dma_start(xin[:, par, :, :], xs_dram.ap()[bass.ds(t * MT, MT), :].rearrange("(h p) c -> p h c", p=P)).then_inc(m_x[par], 16)

            def store(t, par):
                sp.wait_ge(m_y, t + 1)
                sp.dma_start(ys_dram.ap()[bass.ds(t * MT, MT), :].rearrange("(h p) c -> p h c", p=P), ys[:, par, :, :]).then_inc(m_ys[par], 16)

            load_hidden(0, 0, True)
            load_down(0, 0, True)
            load_hidden(1, 1, True)
            load_down(1, 1, True)
            sp.wait_ge(m_sc, 16 * 2 * B)
            load_tokens(0, 0, True)
            load_tokens(1, 1, True)
            load_tokens(2, 0, False)
            load_hidden(2, 0, False)
            with sp.Fori(0, (NT - 3) // 2) as i:
                for par in (1, 0):
                    t = i * 2 + 2 - par
                    load_tokens(t + 2, par, False)
                    store(t - 1, 1 - par)
                    load_down(t + 1, 1 - par, False)
                    load_hidden(t + 2, par, False)
            store(NT - 3, 0)
            load_down(NT - 1, 0, False)
            store(NT - 2, 1)
            store(NT - 1, 0)
            for q in range(4):
                sp.wait_ge(m_f, 4 * q + 4)
                sp.dma_start(a["out"].rearrange("b n d -> n b d")[:, 4 * q:4 * q + 4, :], X[:, 4 * q:4 * q + 4, :]).then_inc(s_out, 16)
            sp.wait_ge(s_out, 64)

        @block.gpsimd
        def _(gp):
            pc = Count(s_pp)
            pc.up(nc.gpsimd.memset(ident[:, :], 0.0))
            gp.wait_ge(s_pp, 1)
            n = pc.up(nc.gpsimd.affine_select(out=ident[:, :], in_=ident[:, :], compare_op=ALU.not_equal, fill=1.0,
                                              base=0, pattern=[[-1, P]], channel_multiplier=1))
            gp.wait_ge(s_pp, n)
            pc.up(nc.gpsimd.tensor_copy(ident16[:, :], ident[:, :]))
            nc.gpsimd.memset(zero[:, :], 0.0).then_inc(m_c, 1)

            def split_ctx(b, par):
                gp.wait_ge(s_ch, b + 1)
                nc.gpsimd.tensor_tensor(ctx16[:, par, 1, :, :], ctxf[:, par, :, :], ctx16[:, par, 0, :, :], ALU.subtract).then_inc(s_cl, 1)

            def separable(g, j, base):
                for r in range(2):
                    nc.gpsimd.tensor_tensor(Lp[:, r, :, :], AB[:, r, :].unsqueeze(2).to_broadcast([P, H, NN]),
                                            wht[:, r, g:g + 1, bass.ds(j * NN, NN)].to_broadcast([P, H, NN]), ALU.mult).then_inc(s_pp, 1)
                gp.wait_ge(s_pp, base + 2)
                high = Lw16[:, g, 0, bass.ds(j, 1), :].rearrange("p o (h n) -> p (o h) n", h=H)
                low = Lw16[:, g, 1, bass.ds(j, 1), :].rearrange("p o (h n) -> p (o h) n", h=H)
                nc.gpsimd.tensor_tensor(high, Lp[:, 0, :, :], Lp[:, 1, :, :], ALU.add).then_inc(s_pp, 1)
                gp.wait_ge(s_pp, base + 3)
                nc.gpsimd.tensor_tensor(Lp[:, 0, :, :], Lp[:, 0, :, :], Lp[:, 1, :, :], ALU.add).then_inc(s_pp, 1)
                gp.wait_ge(s_pp, base + 4)
                nc.gpsimd.tensor_tensor(low, Lp[:, 0, :, :], high, ALU.subtract).then_inc(s_pp, 1)
                gp.wait_ge(s_pp, base + 5)

            gp.wait_ge(s_wha, 2)
            gp.wait_ge(s_cs, 16 * 5)
            for j in range(NJ):
                separable(0, j, pc.n + 5 * j)
                if j == 3:
                    split_ctx(0, 0)
                    split_ctx(1, 1)

            def split_qk(b, par):
                for r in range(4):
                    w, g = r // 2, r % 2
                    hi = q16[:, par, w, 0, HS * g:HS * g + HS, :]
                    gp.wait_ge(s_qh, 4 * b + r + 1)
                    nc.gpsimd.tensor_tensor(q16[:, par, w, 1, HS * g:HS * g + HS, :], qt[:, r, :, :], hi, ALU.subtract).then_inc(s_ql, 1)

            def split_v(b, par):
                for r in range(2):
                    gp.wait_ge(s_vh, 2 * b + r + 1)
                    nc.gpsimd.tensor_tensor(vv16[:, par, 1, 8 * r:8 * r + 8, 0:DK], vf[:, r, :, :], vv16[:, par, 0, 8 * r:8 * r + 8, 0:DK], ALU.subtract).then_inc(s_vl, 1)

            def feature_low(n, par):
                gp.wait_ge(s_fhi, n + 1)
                nc.gpsimd.tensor_tensor(F16s[:, par, 1, :], fs, F16s[:, par, 0, :], ALU.subtract).then_inc(s_flo, 1)

            def probs_low(c):
                for g in range(4):
                    gp.wait_ge(s_ph, 4 * c + g + 1)
                    nc.gpsimd.tensor_tensor(PT16[:, 1, HS * g:HS * g + HS, :], PT[:, HS * g:HS * g + HS, :],
                                            PT16[:, 0, HS * g:HS * g + HS, :], ALU.subtract).then_inc(s_pl, 1)

            split_qk(0, 0)
            split_v(0, 0)
            feature_low(0, 0)

            def iteration(b, par, c, has_q, has_x, has_s=False):
                if c:
                    probs_low(b - 1)
                    feature_low(b, par)
                if has_q:
                    split_qk(b + 1, 1 - par)
                    split_v(b + 1, 1 - par)
                if has_x:
                    split_ctx(b + 2, par)
                if has_s:
                    separable(1, b, b * 5 + (pc.n + 5 * NJ))

            iteration(0, 0, 0, True, True, True)
            gp.wait_ge(m_c, 1)
            gp.dma_start(xs_dram.ap().rearrange("(a p) c -> p a c", p=P), zero[:, :].unsqueeze(1).to_broadcast([P, NT * MT // P, 2 * D])).then_inc(m_zf, 16)
            iteration(1, 1, 1, True, True, True)
            with gp.Fori(1, NJ // 2) as i:
                for par in range(2):
                    iteration(i * 2 + par, par, 2, True, True, True)
            with gp.Fori(NJ // 2, B // 2 - 1) as i:
                for par in range(2):
                    iteration(i * 2 + par, par, 2, True, True)
            iteration(B - 2, 0, 2, True, False)
            iteration(B - 1, 1, 2, False, False)
            probs_low(B - 1)

            for g in range(NG):
                for c in range(FC):
                    n = g * FC + c
                    gp.wait_ge(f_sq, n + 1)
                    gp.wait_ge(f_h2, n + 1)
                    if g > 1:
                        gp.wait_ge(f_o, GT * (g - 1))
                    nc.gpsimd.tensor_tensor(h216[:, g % 2, 1, c, :], h2[:, n % 2, :], h216[:, g % 2, 0, c, :], ALU.subtract).then_inc(f_l, 1)

            def split_ctx1(b, par):
                gp.wait_ge(a_ch, b + 1)
                nc.gpsimd.tensor_tensor(c116[:, par, 1, :, :], c1f[:, par, :, :], c116[:, par, 0, :, :], ALU.subtract).then_inc(a_cl, 1)

            split_ctx1(0, 0)
            split_ctx1(1, 1)
            with gp.Fori(1, B // 2) as i:
                for par in range(2):
                    split_ctx1(i * 2 + par, par)

            def lows1(h, par, weights=True):
                for g in range(NHG):
                    gp.wait_ge(a_ph, h * NHG + g + 1)
                    nc.gpsimd.tensor_tensor(P116[:, 1, HS * g:HS * g + HS, :], P1[:, HS * g:HS * g + HS, :],
                                            P116[:, 0, HS * g:HS * g + HS, :], ALU.subtract).then_inc(a_pl, 1)
                for q in range(NSP if weights else 0):
                    c0, c1 = q * HC // NSP, (q + 1) * HC // NSP
                    gp.wait_ge(w_hi, h * NSP + q + 1)
                    nc.gpsimd.tensor_tensor(ws16[:, par, 1, c0:c1], ws[:, par, c0:c1], ws16[:, par, 0, c0:c1], ALU.subtract).then_inc(w_lo, 1)

            with gp.Fori(0, B // 2 - 1) as i:
                for par in range(2):
                    lows1(i * 2 + par, par)
            lows1(B - 2, 0)
            lows1(B - 1, 1, False)
            gp.wait_ge(a_xu, B)
            gp.wait_ge(a_op, B)
            gp.wait_ge(w_st[0], 16 * E)
            gp.wait_ge(w_st[1], 16 * E)
            nc.gpsimd.memset(one16[:, :], 1.0).then_inc(m_c, 1)
            nc.gpsimd.memset(one[:, :], 1.0).then_inc(m_c, 1)
            gp.wait_ge(m_c, 3)
            nc.gpsimd.affine_select(out=tri[:, :], in_=one16[:, :], compare_op=ALU.is_gt, fill=0.0, base=0,
                                    pattern=[[1, P]], channel_multiplier=-1).then_inc(m_c, 1)
            nc.gpsimd.iota(ioe[:, :], pattern=[[1, E]], base=0, channel_multiplier=0, allow_small_or_imprecise_dtypes=True).then_inc(m_c, 1)
            nc.gpsimd.iota(iot[:, :], pattern=[[1, NT]], base=0, channel_multiplier=0, allow_small_or_imprecise_dtypes=True).then_inc(m_c, 1)

            with gp.Fori(0, B // 2) as i:
                for par in range(2):
                    b = i * 2 + par
                    gp.wait_ge(m_xh, b + 1)
                    nc.gpsimd.tensor_tensor(xm16[:, bass.ds(b, 1), 1, :], xnm[:, par:par + 1, :], xm16[:, bass.ds(b, 1), 0, :], ALU.subtract).then_inc(m_xl, 1)
            gp.wait_ge(m_xl, B)
            gp.wait_ge(m_zf, 16)
            gp.wait_ge(m_sl, 1)
            for b in range(B):
                for k in range(2):
                    nc.gpsimd.indirect_dma_start(out=xs_dram.ap(), out_offset=bass.IndirectOffsetOnAxis(ap=slot[:, 2 * b + k:2 * b + k + 1], axis=0),
                                                 in_=xm16[:, b, :, :].rearrange("p h d -> p (h d)"), in_offset=None).then_inc(m_sc, 16)

            gp.wait_ge(m_ys[0], 16 * ((NT + 1) // 2))
            gp.wait_ge(m_ys[1], 16 * (NT // 2))
            for b in range(B):
                for k in range(2):
                    n = 2 * b + k
                    if b > 3 and k == 0:
                        gp.wait_ge(m_f, b - 3)
                    nc.gpsimd.indirect_dma_start(out=yk[:, b % 4, k, :], out_offset=None, in_=ys_dram.ap(),
                                                 in_offset=bass.IndirectOffsetOnAxis(ap=slot[:, n:n + 1], axis=0)).then_inc(m_gk[b % 4], 16)

        @block.vector
        def _(dv):
            v = nc.vector
            vc = Count(s_pv)

            def step(ins):
                dv.wait_ge(s_pv, vc.up(ins))

            dv.wait_ge(s_cs, 16 * 5)
            step(v.tensor_tensor(wha[:, :, :], whc[:, :, 1, :], whc[:, :, 0, :], ALU.subtract))
            v.tensor_scalar(wha[:, :, :], wha[:, :, :], 1.0, None, ALU.add).then_inc(s_whv, 1)
            step(v.tensor_scalar(We[:, :], We[:, :], GSC, None, ALU.mult))
            step(v.tensor_scalar(AB[:, :, :], AB[:, :, :], GSC, None, ALU.mult))
            step(v.tensor_copy(We16[:, 0, :], We[:, :]))
            step(v.tensor_tensor(We16[:, 1, :], We[:, :], We16[:, 0, :], ALU.subtract))
            dv.wait_ge(s_wha, 1)
            for r in range(3):
                ins = v.tensor_scalar(wht[:, r, :, :], wha[:, :, :], cst[:, 2:3], cst[:, 3 + r:4 + r], ALU.mult, ALU.add)
            step(ins)
            step(v.tensor_scalar(whk[:, :, :, :], wht[:, :, :, :], ROUND, ROUND, ALU.add, ALU.subtract))
            v.tensor_tensor(wht[:, :, :, :], wht[:, :, :, :], whk[:, :, :, :], ALU.subtract).then_inc(s_whv, 1)
            dv.wait_ge(s_x, 16)
            stats = [1]

            def tile_stats():
                for b in range(B):
                    ins = v.bn_stats(bst[:, b, :], X[:, b, :])
                ins.then_inc(s_bs, 1)
                aggregate()

            def aggregate():
                k = stats[0]
                dv.wait_ge(s_bs, k)
                for b in range(B):
                    ins = v.bn_aggr(mv[:, b, :], bst[:, b, :])
                ins.then_inc(s_bn, 1)

            tile_stats()

            def make_rstd():
                k = stats[0]
                dv.wait_ge(s_bn, k)
                v.tensor_scalar(rstd_t[:, 0, :], mv[:, :, 1], 1e-5, None, ALU.add).then_inc(s_var, 1)
                dv.wait_ge(s_sqrt, k)
                step(v.reciprocal(rstd_t[:, 2, :], rstd_t[:, 1, :]))
                step(v.tensor_tensor(rstd_t[:, 1, :], rstd_t[:, 2, :], rstd_t[:, 2, :], ALU.mult))
                step(v.tensor_tensor(rstd_t[:, 1, :], rstd_t[:, 1, :], rstd_t[:, 0, :], ALU.mult))
                step(v.tensor_scalar(rstd_t[:, 1, :], rstd_t[:, 1, :], -0.5, 1.5, ALU.mult, ALU.add))
                step(v.tensor_tensor(rstd[:, :], rstd_t[:, 1, :], rstd_t[:, 2, :], ALU.mult))
                stats[0] += 1

            make_rstd()

            def separable(b0, b1):
                dv.wait_ge(s_wha, 2)
                for b in range(b0, b1):
                    ins = v.tensor_scalar(Rm16[:, b, 0, :], wht[:, 2, b // 8, :], mask[:, b % 8:b % 8 + 1], None, ALU.mult)
                step(ins)
                for b in range(b0, b1):
                    ins = v.scalar_tensor_tensor(Rm16[:, b, 1, :], wht[:, 2, b // 8, :], mask[:, b % 8:b % 8 + 1],
                                                 Rm16[:, b, 0, :], ALU.mult, ALU.subtract)
                ins.then_inc(s_whv, 1)

            def weight_low(j):
                dv.wait_ge(s_whi, j + 1)
                v.scalar_tensor_tensor(wqkv16[:, j, 1, :, :], wst[j], WSC, wqkv16[:, j, 0, :, :], ALU.mult, ALU.subtract).then_inc(s_wlo, 1)

            for par in range(2):
                v.memset(vv16[:, par, 0, :, DK:DK + 1], 1.0)
                ins = v.memset(vv16[:, par, 1, :, DK:DK + 1], 0.0)
            step(ins)

            def key_centres(b0, b1):
                step(v.tensor_tensor(cm[:, b0 * N:b1 * N], cm[:, b0 * N:b1 * N], rows[:, b0 * N:b1 * N], ALU.add))

            def feature_distance(n, par):
                for j in range(NJ):
                    ins = v.tensor_scalar(fu[:, par, j * N:(j + 1) * N], cm[:, bass.ds(n * N, N)],
                                          cn[:, bass.ds(n * NJ + j, 1)], rw[:, bass.ds(n * NJ + j, 1)],
                                          ALU.subtract, ALU.mult)
                ins.then_inc(s_fd, 1)

            def feature_floor(n, par):
                dv.wait_ge(s_fa, 3 * n + 1)
                v.tensor_scalar(fu[:, par, :], fu[:, par, :], 1e-3, None, ALU.max).then_inc(s_fv, 1)

            def feature_turns(n, par):
                dv.wait_ge(s_fa, 3 * n + 2)
                v.tensor_scalar(fu[:, par, :], fu[:, par, :], cst[:, 0:1], cst[:, 1:2], ALU.mult, ALU.add).then_inc(s_fv, 1)
                dv.wait_ge(s_fv, 4 * n + 2)
                v.tensor_scalar(fk, fu[:, par, :], ROUND, ROUND, ALU.add, ALU.subtract).then_inc(s_fv, 1)
                dv.wait_ge(s_fv, 4 * n + 3)
                v.tensor_tensor(fu[:, par, :], fu[:, par, :], fk, ALU.subtract).then_inc(s_fv, 1)

            def norm(b, wait):
                if wait is not None:
                    dv.wait_ge(s_xt, wait)
                v.tensor_scalar(xn[:, :], X[:, bass.ds(b, 1), :], mv[:, bass.ds(b, 1), 0:1], rstd[:, bass.ds(b, 1)],
                                ALU.subtract, ALU.mult).then_inc(s_xn, 1)

            def xn_low(b, par):
                dv.wait_ge(s_xh, b + 1)
                v.tensor_tensor(xn16[:, par, 1, :, :], bank[6][:, 0:KD * N].rearrange("p (k n) -> p k n", k=KD),
                                xn16[:, par, 0, :, :], ALU.subtract).then_inc(s_xl, 1)

            def row_max(b, gs):
                for g in gs:
                    dv.wait_ge(s_sm, 4 * b + g + 1)
                    v.tensor_reduce(nmx[:, HS * g:HS * g + HS], bank[g % 2][:, :].rearrange("p (h n) -> p h n", h=HS),
                                    AX.X, ALU.max, negate=True).then_inc(s_red, 1)

            def take_pv(c, first=False):
                for f in range(4):
                    ps = bank[6 + f % 2][:, 0:HS * (DK + 1)].rearrange("p (h d) -> p h d", h=HS)
                    dv.wait_ge(s_of, 4 * c + f + 1)
                    if f > 1 or not first:
                        dv.wait_ge(s_oe, 4 * c + f - 1)
                    v.reciprocal(rden[:, f % 2, :].unsqueeze(2), ps[:, :, DK:DK + 1]).then_inc(s_rd, 1)
                    dv.wait_ge(s_rd, 4 * c + f + 1)
                    if f == 0 and not first:
                        dv.wait_ge(s_ot, 2 * c)
                    v.tensor_tensor(O[:, f * HS * DK:(f + 1) * HS * DK].rearrange("p (h d) -> p h d", h=HS), ps[:, :, 0:DK],
                                    rden[:, f % 2, :].unsqueeze(2).to_broadcast([P, HS, DK]), ALU.mult).then_inc(s_oe, 1)

            def take_qk(b, rs, first=False):
                for r in rs:
                    dv.wait_ge(s_qf, 6 * b + r + 1)
                    if not first:
                        dv.wait_ge(s_ql, 4 * b + r - 3)
                    v.scalar_tensor_tensor(qt[:, r, :, :], bank[2 + r][:, :].rearrange("p (c n) -> p c n", c=HS), 1.0 / WSC,
                                           bqk[:, r // 2, HS * (r % 2):HS * (r % 2) + HS].unsqueeze(2).to_broadcast([P, HS, N]),
                                           ALU.mult, ALU.add).then_inc(s_qe, 1)

            def take_v(b, first=False):
                for r in range(2):
                    dv.wait_ge(s_qf, 6 * b + 4 + r + 1)
                    if not first:
                        dv.wait_ge(s_vl, 2 * b + r - 1)
                    v.scalar_tensor_tensor(vf[:, r, :, :], bank[2 + r][:, :].rearrange("p (h d) -> p h d", h=8), 1.0 / WSC,
                                           bv[:, 512 * r:512 * r + 512].rearrange("p (h d) -> p h d", h=8),
                                           ALU.mult, ALU.add).then_inc(s_qe, 1)

            def residual(c):
                dv.wait_ge(s_op, c + 1)
                v.tensor_tensor(otmp[:, :], bank[7][:, 0:D], bo[:, :], ALU.add).then_inc(s_opt, 1)
                dv.wait_ge(s_opt, c + 1)
                xb = X[:, bass.ds(c, 1), :]
                v.scalar_tensor_tensor(xb, otmp[:, :].unsqueeze(1), tg[:, 0:1], xb, ALU.mult, ALU.add).then_inc(s_xu, 1)

            def probs(b, first):
                for g in range(4):
                    dv.wait_ge(s_gf, 4 * b + g + 1)
                    if g == 0:
                        dv.wait_ge(s_exp, 4 * b + 4)
                        if not first:
                            dv.wait_ge(s_pl, 4 * b)
                    for jj in range(2):
                        j = 2 * g + jj
                        v.scalar_tensor_tensor(PT[:, :, j * NN:(j + 1) * NN],
                                               bank[2 + g][:, jj * 256:(jj + 1) * 256].rearrange("p (h n) -> p h n", h=H), 1e-6 * GSC,
                                               EX[:, :, j * NN:(j + 1) * NN], ALU.max, ALU.mult).then_inc(s_pm, 1)

            norm(0, None)
            weight_low(0)
            weight_low(1)
            norm(1, 1)
            xn_low(0, 0)
            xn_low(1, 1)
            dv.wait_ge(s_cw, 16 * 5)
            step(v.tensor_tensor(cn[:, :], boxn[:, :, 0], boxn[:, :, 1], ALU.add))
            step(v.tensor_tensor(rw[:, :], boxn[:, :, 1], boxn[:, :, 0], ALU.subtract))
            step(v.tensor_scalar(rw[:, :], rw[:, :], 1.0, None, ALU.add))
            step(v.reciprocal(rw[:, :], rw[:, :]))
            step(v.tensor_scalar(rw[:, :], rw[:, :], 0.5, None, ALU.mult))
            key_centres(0, 2)
            feature_distance(0, 0)
            weight_low(2)
            dv.wait_ge(s_o, 64)
            take_qk(0, (0,), True)
            feature_floor(0, 0)
            take_qk(0, (1, 2, 3), True)
            feature_turns(0, 0)
            take_v(0, True)
            feature_distance(1, 1)
            dv.wait_ge(s_tg, 1)

            def ternary_scale():
                dv.wait_ge(f_ld, 64)
                step(v.tensor_reduce(thr[:, 0, 0:FC], wfc, AX.X, ALU.add, apply_absolute_value=True))
                step(v.tensor_reduce(thr[:, 0, FC:], wpj, AX.X, ALU.add, apply_absolute_value=True))
                step(v.tensor_scalar(thr[:, 0, 0:FC], thr[:, 0, 0:FC], 1.0 / D, 1e-5, ALU.mult, ALU.max))
                step(v.tensor_scalar(thr[:, 0, FC:], thr[:, 0, FC:], 1.0 / FF, 1e-5, ALU.mult, ALU.max))
                for r, k in ((1, 0.5), (2, -0.5), (3, -1.0)):
                    ins = v.tensor_scalar(thr[:, r, :], thr[:, 0, :], k, None, ALU.mult)
                step(ins)

            def ternary_hidden():
                dv.wait_ge(s_fa, 3 * B)
                for c in range(FC):
                    v.tensor_scalar(wfa[:, c, :], wfc[:, c, :], thr[:, 1, c:c + 1], thr[:, 0, c:c + 1], ALU.is_gt, ALU.mult)
                    ins = v.tensor_scalar(wfb[:, c, :], wfc[:, c, :], thr[:, 2, c:c + 1], thr[:, 3, c:c + 1], ALU.is_lt, ALU.mult)
                step(ins)
                step(v.tensor_tensor(wfa, wfa, wfb, ALU.add))

            def ternary_out():
                dv.wait_ge(s_flo, B)
                for c in range(KD):
                    ins = v.tensor_scalar(wpa[:, c, :], wpj[:, c, :], thr[:, 2, FC + c:FC + c + 1], -1.0, ALU.is_lt, ALU.mult)
                step(ins)
                for c in range(KD):
                    ins = v.scalar_tensor_tensor(wpa[:, c, :], wpj[:, c, :], thr[:, 1, FC + c:FC + c + 1], wpa[:, c, :], ALU.is_gt, ALU.add)
                step(ins)

            def iteration(b, par, has_c, has_q, has_x, first=False):
                if has_x:
                    norm(b + 2, b + 2)
                row_max(b, (0, 1))
                if has_q:
                    take_qk(b + 1, (0, 1))
                row_max(b, (2, 3))
                if has_q:
                    take_qk(b + 1, (2, 3))
                if has_c:
                    take_pv(b - 1, first)
                if not has_c:
                    key_centres(2, B)
                if has_q:
                    feature_floor(b + 1, 1 - par)
                    take_v(b + 1)
                    feature_turns(b + 1, 1 - par)
                if has_x:
                    xn_low(b + 2, par)
                if has_c:
                    residual(b - 1)
                    dv.wait_ge(s_xu, b)
                else:
                    separable(0, 2)
                if not has_q:
                    ternary_scale()
                if has_x:
                    dv.wait_ge(s_fa, 3 * b + 3)
                    feature_distance(b + 2, par)
                if not has_c:
                    separable(2, B)
                    dv.wait_ge(s_whv, 4)
                probs(b, not has_c)
                if has_c:
                    v.bn_stats(bst[:, bass.ds(b - 1, 1), :].rearrange("p o c -> p (o c)"), X[:, bass.ds(b - 1, 1), :].rearrange("p o d -> p (o d)"))

            iteration(0, 0, False, True, True)
            iteration(1, 1, True, True, True, True)
            with dv.Fori(0, B // 2 - 2) as i:
                for par in range(2):
                    iteration(i * 2 + 2 + par, par, True, True, True)
            iteration(B - 2, 0, True, True, False)
            iteration(B - 1, 1, True, False, False)
            ternary_hidden()
            take_pv(B - 1)
            residual(B - 1)

            dv.wait_ge(s_xu, B)
            v.bn_stats(bst[:, B - 1, :], X[:, B - 1, :]).then_inc(s_bs, 1)
            ternary_out()
            aggregate()
            make_rstd()
            dv.wait_ge(f_mp, 1)
            v.tensor_copy(lowm, bank[4][0:RANK, 0:D]).then_inc(f_m, 1)
            for r in range(FC // 2):
                dv.wait_ge(f_lp, r + 1)
                v.scalar_tensor_tensor(wfa[:, 2 * r:2 * r + 2, :], bank[r][:, :].rearrange("p (c d) -> p c d", c=2), fgate[:, 0:1],
                                       wfa[:, 2 * r:2 * r + 2, :], ALU.mult, ALU.add).then_inc(f_low, 1)
            for r in range(4):
                dv.wait_ge(f_hi, r + 1)
                kk, fh = r // 2, r % 2
                v.scalar_tensor_tensor(W1T16[:, 1, kk, 512 * fh:512 * fh + 512], bank[r][:, :], WSC,
                                       W1T16[:, 0, kk, 512 * fh:512 * fh + 512], ALU.mult, ALU.subtract).then_inc(f_lo, 1)
            dv.wait_ge(f_mp, 2)
            v.tensor_copy(w2row[:, :], bank[4][:, 0:D]).then_inc(f_m, 1)

            def ffn_norm(g, i):
                t = g * GT + i
                v.tensor_scalar(xng[:, g % 2, i, :], X[:, t, :], mv[:, t, 0:1], rstd[:, t:t + 1], ALU.subtract, ALU.mult).then_inc(f_xn, 1)

            def ffn_low(g):
                for kk in range(KD):
                    dv.wait_ge(f_xh, 2 * g + kk + 1)
                    v.tensor_tensor(xg16[:, g % 2, 1, kk, :], bank[4 + kk][:, :], xg16[:, g % 2, 0, kk, :], ALU.subtract).then_inc(f_xl, 1)

            def ffn_square(g):
                for c in range(FC):
                    n = g * FC + c
                    dv.wait_ge(f_r, n + 1)
                    if n > 1:
                        dv.wait_ge(f_l, n - 1)
                    v.tensor_tensor(h2[:, n % 2, :], hr[:, n % 2, :], hr[:, n % 2, :], ALU.mult).then_inc(f_h2, 1)
                    if c < GT and g + 2 < NG:
                        ffn_norm(g + 2, c)

            def ffn_residual(g):
                for i in range(GT):
                    t = g * GT + i
                    dv.wait_ge(f_o, t + 1)
                    if t > 1:
                        dv.wait_ge(f_xu, t - 1)
                    v.tensor_tensor(ftmp[:, t % 2, :], bank[6 + t % 2][:, 0:D], w2row[:, :], ALU.mult).then_inc(f_ot, 1)
                    dv.wait_ge(f_ot, t + 1)
                    v.scalar_tensor_tensor(X[:, t, :], ftmp[:, t % 2, :], tg[:, 2:3], X[:, t, :], ALU.mult, ALU.add).then_inc(f_xu, 1)
                    dv.wait_ge(f_xu, t + 1)
                    ins = v.bn_stats(bst[:, t, :], X[:, t, :])
                if g == NG - 1:
                    ins.then_inc(s_bs, 1)

            for i in range(2 * GT):
                ffn_norm(i // GT, i % GT)
            ffn_low(0)
            for g in range(NG):
                if g == 2:
                    dv.wait_ge(a_w, 1)
                    v.scalar_tensor_tensor(w1_16[:, 1, :, :], wst1[:, :, :], WSC, w1_16[:, 0, :, :], ALU.mult, ALU.subtract).then_inc(a_wl, 1)
                    step(v.tensor_tensor(gam[:, 0, :], gam[:, 0, :], gam[:, 1, :], ALU.mult))
                    for i in range(B):
                        v.memset(v1[:, i, 0, :, HD:HD + 1], 1.0)
                        ins = v.memset(v1[:, i, 1, :, HD:HD + 1], 0.0)
                    step(ins)
                ffn_square(g)
                if g + 1 < NG:
                    ffn_low(g + 1)
                if g:
                    ffn_residual(g - 1)
            ffn_residual(NG - 1)

            aggregate()
            make_rstd()
            step(v.memset(seg[:, :, :, :, 3:4, :].rearrange("a r q h s d -> a (r q h) (s d)"), 0.0))

            def norm1(b, par, first):
                if not first:
                    dv.wait_ge(a_xt, b - 1)
                v.tensor_scalar(xn1[:, par, :], X[:, bass.ds(b, 1), :], mv[:, bass.ds(b, 1), 0:1], rstd[:, bass.ds(b, 1)],
                                ALU.subtract, ALU.mult).then_inc(a_xn, 1)

            def low1(b, par):
                dv.wait_ge(a_xh, b + 1)
                v.tensor_tensor(x116[:, par, 1, :, :], bank[par][:, 0:KD * N].rearrange("p (k n) -> p k n", k=KD),
                                x116[:, par, 0, :, :], ALU.subtract).then_inc(a_xl, 1)

            def sums(b, par):
                dv.wait_ge(a_kf, b + 1)
                full = bank[4 + par][:, D:].rearrange("p (o h d) -> p o h d", o=1, h=H)
                high = v1[:, bass.ds(b, 1), 0, :, 0:HD]
                v.tensor_scalar(high, full, 1.0 / WSC, None, ALU.mult).then_inc(a_v, 1)
                dv.wait_ge(a_v, 2 * b + 1)
                v.scalar_tensor_tensor(v1[:, bass.ds(b, 1), 1, :, 0:HD], full, 1.0 / WSC, high, ALU.mult, ALU.subtract).then_inc(a_v, 1)
                dv.wait_ge(a_raw, b + 1)
                v.tensor_reduce(ms[:, 0, bass.ds(b, 1), :], sq[:, par:par + 1, :, :].rearrange("p o q (h d) -> p o (q h) d", h=H),
                                AX.X, ALU.add).then_inc(a_red, 1)

            norm1(0, 0, True)
            norm1(1, 1, True)
            low1(0, 0)

            def stage1(b, par, has_next):
                if has_next > 1:
                    norm1(b + 2, par, False)
                if has_next:
                    low1(b + 1, 1 - par)
                sums(b, par)

            with dv.Fori(0, B // 2 - 1) as i:
                for par in range(2):
                    stage1(i * 2 + par, par, 2)
            stage1(B - 2, 0, 1)
            stage1(B - 1, 1, 0)
            dv.wait_ge(a_red, B)
            v.tensor_scalar(ms[:, 0, :, :], ms[:, 0, :, :], 1.0 / HD, 1e-6, ALU.mult, ALU.add).then_inc(a_ms, 1)
            dv.wait_ge(a_sq, 1)

            def inverse_norms(b0, b1):
                mean, root, inv, out = (ms[:, k, b0:b1, :] for k in range(4))
                step(v.reciprocal(inv, root))
                step(v.tensor_tensor(root, inv, inv, ALU.mult))
                step(v.tensor_tensor(root, root, mean, ALU.mult))
                step(v.tensor_scalar(root, root, -0.5, 1.5, ALU.mult, ALU.add))
                step(v.tensor_tensor(out, root, inv, ALU.mult))

            inverse_norms(0, 2)

            def scale1(b, par, first):
                if not first:
                    dv.wait_ge(a_sh, b - 1)
                    dv.wait_ge(a_sl, b - 1)
                v.tensor_tensor(qn[:, par, :, :].rearrange("p q (h d) -> p (q h) d", h=H),
                                raw[:, bass.ds(b, 1), :, :].rearrange("p o q (h d) -> p (o q h) d", h=H),
                                ms[:, 3, bass.ds(b, 1), :].rearrange("p o h -> p (o h)").unsqueeze(2).to_broadcast([P, 2 * H, HD]), ALU.mult).then_inc(a_qn, 1)
                dv.wait_ge(a_qn, b + 1)
                v.tensor_tensor(qn[:, par, 1, :], qn[:, par, 1, :], gam[:, 0, :], ALU.mult).then_inc(a_gn, 1)

            def seg_low(b, par):
                dv.wait_ge(a_sh, b + 1)
                for w, sg in ((0, 2), (1, 1)):
                    ins = v.tensor_tensor(seg[:, par, w, :, sg, :], qn[:, par, w, :].rearrange("p (h d) -> p h d", h=H),
                                          seg[:, par, w, :, 0, :], ALU.subtract)
                ins.then_inc(a_sl, 1)

            def copy_k(b, par):
                dv.wait_ge(a_tk, b + 1)
                v.tensor_copy(qT1[:, par, 1, :, :].rearrange("p c n -> p (c n)"), bank[3][:, :].bitcast(F16)).then_inc(a_ck, 1)

            def row_max1(b, gs):
                for g in gs:
                    dv.wait_ge(a_sm, 4 * b + g + 1)
                    v.tensor_reduce(nmx1[:, HS * g:HS * g + HS], bank[g % 2][:, :].rearrange("p (h n) -> p h n", h=HS),
                                    AX.X, ALU.max, negate=True).then_inc(a_mx, 1)

            def take_pv1(c, first):
                ps = bank[6][:, 0:H * (HD + 1)].rearrange("p (h d) -> p h d", h=H)
                dv.wait_ge(a_pv, c + 1)
                if not first:
                    dv.wait_ge(a_o, c)
                v.reciprocal(rden1[:, :].unsqueeze(2), ps[:, :, HD:HD + 1]).then_inc(a_rd, 1)
                dv.wait_ge(a_rd, c + 1)
                if not first:
                    dv.wait_ge(a_ot, c)
                v.tensor_tensor(O1[:, :].rearrange("p (h d) -> p h d", h=H), ps[:, :, 0:HD],
                                rden1[:, :].unsqueeze(2).to_broadcast([P, H, HD]), ALU.mult).then_inc(a_o, 1)

            def residual1(c):
                dv.wait_ge(a_op, c + 1)
                xb = X[:, bass.ds(c, 1), :]
                v.scalar_tensor_tensor(xb, bank[5][:, 0:D].unsqueeze(1), tg[:, 1:2], xb, ALU.mult, ALU.add).then_inc(a_xu, 1)

            scale1(0, 0, True)
            scale1(1, 1, True)
            seg_low(0, 0)
            seg_low(1, 1)
            copy_k(0, 0)

            def values1(b, par, first):
                if not first:
                    dv.wait_ge(a_pv, b - 1)
                v.tensor_copy(vb1[:, par, :, :].rearrange("p r c -> p (r c)"),
                              v1[:, bass.ds(b, 1), :, :, :].rearrange("p o r h d -> p (o r h d)")).then_inc(a_v, 1)

            def iteration1(b, par, c, has_q, has_x):
                row_max1(b, (0, 1))
                if c and has_q:
                    seg_low(b + 1, 1 - par)
                row_max1(b, (2, 3))
                if has_q:
                    copy_k(b + 1, 1 - par)
                if not c:
                    inverse_norms(2, B)
                if has_x:
                    scale1(b + 2, par, False)
                if c > 1:
                    residual1(b - 2)
                    dv.wait_ge(a_xu, b - 1)
                values1(b, par, c < 2)
                if c > 1:
                    v.bn_stats(bst[:, bass.ds(b - 2, 1), :].rearrange("p o c -> p (o c)"), X[:, bass.ds(b - 2, 1), :].rearrange("p o d -> p (o d)"))
                if c:
                    take_pv1(b - 1, c == 1)

            iteration1(0, 0, 0, True, True)
            iteration1(1, 1, 1, True, True)
            iteration1(2, 0, 2, True, True)
            iteration1(3, 1, 3, True, True)
            with dv.Fori(2, B // 2 - 1) as i:
                for par in range(2):
                    iteration1(i * 2 + par, par, 3, True, True)
            iteration1(B - 2, 0, 3, True, False)
            iteration1(B - 1, 1, 3, False, False)
            dv.wait_ge(w_lo, NSP * (B - 1))
            for q in range(NSP):
                c0, c1 = q * HC // NSP, (q + 1) * HC // NSP
                dv.wait_ge(w_hi, (B - 1) * NSP + q + 1)
                v.tensor_tensor(ws16[:, 1, 1, c0:c1], ws[:, 1, c0:c1], ws16[:, 1, 0, c0:c1], ALU.subtract).then_inc(w_lo, 1)
            residual1(B - 2)
            take_pv1(B - 1, False)
            residual1(B - 1)

            dv.wait_ge(a_xu, B)
            for b in (B - 2, B - 1):
                ins = v.bn_stats(bst[:, b, :], X[:, b, :])
            ins.then_inc(s_bs, 1)
            aggregate()
            make_rstd()
            v4 = Count(m_v)

            def then(ins):
                dv.wait_ge(m_v, v4.up(ins))

            def norm_m(b, par, first):
                if not first:
                    dv.wait_ge(m_xt, b - 1)
                    dv.wait_ge(m_xl, b - 1)
                v.tensor_scalar(xnm[:, par, :], X[:, bass.ds(b, 1), :], mv[:, bass.ds(b, 1), 0:1], rstd[:, bass.ds(b, 1)],
                                ALU.subtract, ALU.mult).then_inc(m_xn, 1)

            dv.wait_ge(a_op, B)
            dv.wait_ge(w_st[0], 16 * E)
            dv.wait_ge(w_st[1], 16 * E)
            norm_m(0, 0, True)
            norm_m(1, 1, True)
            with dv.Fori(1, B // 2) as i:
                for par in range(2):
                    norm_m(i * 2 + par, par, False)
            dv.wait_ge(m_lg, B)
            then(v.tensor_copy(lg[:, :, :], bank[7][:, 0:B * E].rearrange("p (b e) -> p b e", e=E)))
            for b in range(B):
                ins = v.max(top[:, b, :], lg[:, b, :])
            then(ins)
            for b in range(B):
                v.max_index(topi[:, b, :], top[:, b, :], lg[:, b, :])
            v.tensor_tensor(ex[:, :, 0:E], lg[:, :, :], top[:, :, 0:1].to_broadcast([P, B, E]), ALU.subtract)
            then(v.tensor_tensor(ex[:, :, E], top[:, :, 1], top[:, :, 0], ALU.subtract))
            v.engine_nop().then_inc(m_ex, 1)
            then(v.tensor_copy(idf[:, :, :], topi[:, :, 0:2]))
            dv.wait_ge(m_c, 6)
            then(v.tensor_tensor(oh[:, :, :], idf[:, :, :].rearrange("p b k -> p (b k)").unsqueeze(1).to_broadcast([P, E, B * 2]),
                                 ioe[:, :].unsqueeze(2).to_broadcast([P, E, B * 2]), ALU.is_equal))
            v.tensor_copy(oh16[:, :], oh[:, :, :].rearrange("p e n -> p (e n)")).then_inc(m_ex, 1)
            dv.wait_ge(m_er, 1)
            then(v.tensor_reduce(den[:, 0, :], ex[:, :, 0:E], AX.X, ALU.add))
            then(v.reciprocal(den[:, 1, :], den[:, 0, :]))
            then(v.tensor_scalar(wk[:, 0, :], den[:, 1, :], tg[:, 3:4], None, ALU.mult))
            then(v.tensor_tensor(wk[:, 1, :], wk[:, 0, :], ex[:, :, E], ALU.mult))
            dv.wait_ge(m_pr, 1)
            then(v.tensor_copy(tot[:, :], bank[6][:, 256:512]))
            v.tensor_tensor_scan(cum[:, :], one[:, :], tot[:, :], 0.0, ALU.mult, ALU.add)
            then(v.tensor_reduce(cnt[:, 0, :], tot[:, :].rearrange("p (e n) -> p e n", e=E), AX.X, ALU.add))
            then(v.tensor_tensor_scan(cnt[:, 1, :], one[:, 0:E], cnt[:, 0, :], 0.0, ALU.mult, ALU.add))
            then(v.tensor_scalar(cnt[:, 2, :], cnt[:, 0, :], 1.0 / MT, (MT - 1.0) / MT - 0.5 + 0.5 / MT, ALU.mult, ALU.add))
            then(v.tensor_scalar(cnt[:, 2, :], cnt[:, 2, :], ROUND, ROUND, ALU.add, ALU.subtract))
            then(v.tensor_tensor_scan(cnt[:, 3, :], one[:, 0:E], cnt[:, 2, :], 0.0, ALU.mult, ALU.add))
            then(v.tensor_tensor(cnt[:, 4, :], cnt[:, 3, :], cnt[:, 2, :], ALU.subtract))
            then(v.tensor_tensor(cnt[:, 5, :], cnt[:, 1, :], cnt[:, 0, :], ALU.subtract))
            then(v.scalar_tensor_tensor(cnt[:, 4, :], cnt[:, 4, :], float(MT), cnt[:, 5, :], ALU.mult, ALU.subtract))
            then(v.tensor_tensor(pos[:, :, :].rearrange("p e n -> p (e n)"), cum[:, :], tot[:, :], ALU.subtract))
            then(v.tensor_tensor(pos[:, :, :].rearrange("p e n -> p (e n)"), pos[:, :, :].rearrange("p e n -> p (e n)"), bank[6][:, 0:256], ALU.add))
            then(v.tensor_tensor(pos[:, :, :], pos[:, :, :], cnt[:, 4, :].unsqueeze(2).to_broadcast([P, E, B * 2]), ALU.add))
            then(v.tensor_tensor(pos[:, :, :], pos[:, :, :], oh[:, :, :], ALU.mult))
            then(v.tensor_reduce(slotf[:, :], pos[:, :, :].rearrange("p e n -> p n e"), AX.X, ALU.add))
            v.tensor_copy(slot[:, :], slotf[:, :]).then_inc(m_sl, 1)
            then(v.tensor_tensor(cmp[:, :, :], cnt[:, 3, :].unsqueeze(1).to_broadcast([P, NT, E]),
                                 iot[:, :].unsqueeze(2).to_broadcast([P, NT, E]), ALU.is_le))
            then(v.tensor_reduce(etf[:, :], cmp[:, :, :], AX.X, ALU.add))
            then(v.tensor_scalar(etf[:, :], etf[:, :], float(E - 1), None, ALU.min))
            then(v.memset(chg[:, 0:2], 1))
            then(v.tensor_tensor(chg[:, 2:], etf[:, 2:], etf[:, 0:NT - 2], ALU.not_equal))
            v.tensor_copy(eti[:, :], etf[:, :]).then_inc(m_sl, 1)

            def products(t, par, c0, c1, first):
                for c in range(c0, c1):
                    dv.wait_ge(m_g, FC * t + c + 1)
                    if c % 2 == 0 and not (first and c < 4):
                        dv.wait_ge(m_hh, 4 * t + c // 2 - 1)
                        dv.wait_ge(m_hl, 4 * t + c // 2 - 1)
                    v.scalar_tensor_tensor(hf[:, (c // 2) % 2, c % 2, :], bank[c % 4][:, MT:2 * MT], bms[:, par, FC + c:FC + c + 1],
                                           yg[:, c % 4, :], ALU.add, ALU.mult).then_inc(m_u, 1)
                    if c % 2:
                        q = c // 2
                        dv.wait_ge(m_hh, 4 * t + q + 1)
                        v.tensor_tensor(hm16[:, par, 1, c - 1:c + 1, :], hf[:, q % 2, :, :], hm16[:, par, 0, c - 1:c + 1, :], ALU.subtract).then_inc(m_hl, 1)

            def copy_tokens(t, par):
                dv.wait_ge(m_tt, t + 1)
                v.tensor_copy(xT16[:, par, :, :].rearrange("p a n -> p (a n)"), bank[4][:, :].bitcast(F16)).then_inc(m_tc, 1)

            def take_out(t, par, first):
                dv.wait_ge(m_o, t + 1)
                if not first:
                    dv.wait_ge(m_ys[par], (t - par) * 8)
                v.scalar_tensor_tensor(ys[:, par, :, :], bank[5 + par][:, :].rearrange("p (h d) -> p h d", h=2), 1.0,
                                       b2r[:, par, :].unsqueeze(1).to_broadcast([P, MT // P, D]), ALU.mult, ALU.add).then_inc(m_y, 1)

            def expert_v(t, par, prev, nxt, first=False):
                products(t, par, 0, 4, first)
                if prev:
                    take_out(t - 1, 1 - par, prev == 1)
                if nxt:
                    copy_tokens(t + 1, 1 - par)
                products(t, par, 4, 8, False)

            copy_tokens(0, 0)
            expert_v(0, 0, 0, True, True)
            expert_v(1, 1, 1, True)
            expert_v(2, 0, 1, True)
            with dv.Fori(0, (NT - 5) // 2) as i:
                for q in range(2):
                    expert_v(i * 2 + 3 + q, 1 - q, 2, True)
            expert_v(NT - 2, 1, 2, True)
            expert_v(NT - 1, 0, 2, False)
            take_out(NT - 1, 0, False)
            for b in range(B):
                for k in range(2):
                    if k == 0:
                        dv.wait_ge(m_gk[b % 4], 32 * (b // 4 + 1))
                    ins = v.scalar_tensor_tensor(X[:, b, :], yk[:, b % 4, k, :], wk[:, k, b:b + 1], X[:, b, :], ALU.mult, ALU.add)
                    if k == 0:
                        then(ins)
                ins.then_inc(m_f, 1)

        @block.scalar
        def _(ac):
            s = nc.scalar
            ac.dma_start(X[:, :, :], a["x"].rearrange("b n d -> n b d")).then_inc(s_x, 16)
            ac.dma_start(gates[:, 0:2], a["g_xattn"].partition_broadcast(P)).then_inc(s_c, 16)
            ac.dma_start(gates[:, 2:4], a["g_ffn"].partition_broadcast(P)).then_inc(s_c, 16)
            ac.wait_ge(s_c, 32)
            s.activation(tg[:, :], gates[:, :], ACT.Tanh).then_inc(s_tg, 1)
            ac.wait_ge(s_whv, 1)
            s.activation(wha[:, :, :], wha[:, :, :], ACT.Ln).then_inc(s_wha, 1)
            ac.wait_ge(s_whv, 2)
            s.activation(wht[:, :, :, :], wht[:, :, :, :], ACT.Sin, scale=TWO_PI).then_inc(s_wha, 1)
            ac.wait_ge(s_var, 1)
            s.activation(rstd_t[:, 1, :], rstd_t[:, 0, :], ACT.Sqrt).then_inc(s_sqrt, 1)
            def weight_high(j):
                ac.wait_ge(s_w[j], 16)
                s.activation(wqkv16[:, j, 0, :, :], wst[j], ACT.Copy, scale=WSC).then_inc(s_whi, 1)

            def feature_abs(n, par):
                ac.wait_ge(s_fd, n + 1)
                s.activation(fu[:, par, :], fu[:, par, :], ACT.Abs).then_inc(s_fa, 1)

            def feature_log(n, par):
                ac.wait_ge(s_fv, 4 * n + 1)
                s.activation(fu[:, par, :], fu[:, par, :], ACT.Ln).then_inc(s_fa, 1)

            def feature_sine(n, par, first):
                ac.wait_ge(s_fv, 4 * n + 4)
                if first:
                    ac.wait_ge(s_flo, n)
                s.activation(fs, fu[:, par, :], ACT.Sin, scale=TWO_PI).then_inc(s_fa, 1)
                ac.wait_ge(s_fa, 3 * n + 3)
                if first > 1:
                    ac.wait_ge(s_gf, 4 * n - 4)
                s.activation(F16s[:, par, 0, :], fs, ACT.Copy).then_inc(s_fhi, 1)

            def xn_high(b, par):
                ac.wait_ge(s_xt, b + 1)
                s.activation(xn16[:, par, 0, :, :], bank[6][:, 0:KD * N].rearrange("p (k n) -> p k n", k=KD), ACT.Copy).then_inc(s_xh, 1)

            def take_o(c, first):
                for r in range(2):
                    ac.wait_ge(s_ot, 2 * c + r + 1)
                    if r == 0 and not first:
                        ac.wait_ge(s_op, c)
                    s.activation(OT[:, 4 * r:4 * r + 4, :], bank[6 + r][:, :].rearrange("p (c n) -> p c n", c=4), ACT.Copy).then_inc(s_oc, 1)

            def exps(b, first):
                for g in range(4):
                    ac.wait_ge(s_st, 4 * b + g + 1)
                    if g == 0 and not first:
                        ac.wait_ge(s_pm, 8 * b)
                    s.activation(EX[:, HS * g:HS * g + HS, :], bank[g % 2][:, :].rearrange("p (h n) -> p h n", h=HS), ACT.Exp,
                                 scale=DK ** -0.5).then_inc(s_exp, 1)

            def ctx_high(b, par, first):
                ac.wait_ge(s_cf[par], (b - par) * 8 + 16)
                if not first:
                    ac.wait_ge(s_qf, 6 * b - 6)
                s.activation(ctx16[:, par, 0, :, :], ctxf[:, par, :, :], ACT.Copy).then_inc(s_ch, 1)

            def qk_high(b, par, rs, first=False):
                for r in rs:
                    w, g = r // 2, r % 2
                    ac.wait_ge(s_qe, 6 * b + r + 1)
                    s.activation(q16[:, par, w, 0, HS * g:HS * g + HS, :], qt[:, r, :, :], ACT.Copy).then_inc(s_qh, 1)

            def v_high(b, par, rs):
                for r in rs:
                    ac.wait_ge(s_qe, 6 * b + 4 + r + 1)
                    s.activation(vv16[:, par, 0, 8 * r:8 * r + 8, 0:DK], vf[:, r, :, :], ACT.Copy).then_inc(s_vh, 1)

            def probs_high(c, first):
                for g in range(4):
                    if g == 0:
                        ac.wait_ge(s_pm, 8 * c + 8)
                        if not first:
                            ac.wait_ge(s_of, 4 * c)
                    s.activation(PT16[:, 0, HS * g:HS * g + HS, :], PT[:, HS * g:HS * g + HS, :], ACT.Copy).then_inc(s_ph, 1)

            weight_high(0)
            weight_high(1)
            xn_high(0, 0)
            xn_high(1, 1)
            ctx_high(0, 0, True)
            ctx_high(1, 1, True)
            weight_high(2)
            feature_abs(0, 0)
            feature_log(0, 0)
            qk_high(0, 0, range(4))
            feature_sine(0, 0, 0)
            v_high(0, 0, (0, 1))

            def iteration(b, par, c, has_x, has_q=True):
                if c:
                    probs_high(b - 1, c == 1)
                if has_x:
                    ctx_high(b + 2, par, False)
                if has_q:
                    qk_high(b + 1, 1 - par, range(4))
                    feature_abs(b + 1, 1 - par)
                    feature_log(b + 1, 1 - par)
                    v_high(b + 1, 1 - par, (0,))
                if c:
                    take_o(b - 1, c == 1)
                if has_q:
                    v_high(b + 1, 1 - par, (1,))
                if has_x:
                    xn_high(b + 2, par)
                if has_q:
                    s.activation(warm[:, :], nmx[:, 0:1], ACT.Exp, scale=0.0)
                exps(b, c == 0)
                if has_q:
                    feature_sine(b + 1, 1 - par, min(c + 1, 2))

            iteration(0, 0, 0, True)
            iteration(1, 1, 1, True)
            with ac.Fori(0, B // 2 - 2) as i:
                for par in range(2):
                    iteration(i * 2 + 2 + par, par, 2, True)
            iteration(B - 2, 0, 2, False)
            iteration(B - 1, 1, 2, False, False)
            probs_high(B - 1, False)
            take_o(B - 1, False)

            ac.wait_ge(s_var, 2)
            s.activation(rstd_t[:, 1, :], rstd_t[:, 0, :], ACT.Sqrt).then_inc(s_sqrt, 1)
            for r in range(4):
                ac.wait_ge(f_tp, r + 1)
                kk, fh = r // 2, r % 2
                s.activation(W1T16[:, 0, kk, 512 * fh:512 * fh + 512], bank[r][:, :], ACT.Copy, scale=WSC).then_inc(f_hi, 1)
            for r in range(4):
                ac.wait_ge(f_tp, r + 5)
                s.activation(W2T16[:, 2 * r:2 * r + 2, :], bank[r][:, :].rearrange("p (f d) -> p f d", f=2), ACT.Copy).then_inc(f_hi, 1)

            def ffn_high(g):
                for kk in range(KD):
                    ac.wait_ge(f_xt, 2 * g + kk + 1)
                    s.activation(xg16[:, g % 2, 0, kk, :], bank[4 + kk][:, :], ACT.Copy).then_inc(f_xh, 1)

            def ffn_relu(g):
                for c in range(FC):
                    n = g * FC + c
                    ac.wait_ge(f_h, n + 1)
                    if n > 1:
                        ac.wait_ge(f_sq, n - 1)
                        ac.wait_ge(f_h2, n - 1)
                    s.activation(hr[:, n % 2, :], bank[n % 4][:, :], ACT.Relu, scale=1.0 / WSC).then_inc(f_r, 1)
                    ac.wait_ge(f_r, n + 1)
                    if c == 0 and g > 1:
                        ac.wait_ge(f_o, GT * (g - 1))
                    s.activation(h216[:, g % 2, 0, c, :], hr[:, n % 2, :], ACT.Square).then_inc(f_sq, 1)

            ffn_high(0)
            for g in range(NG):
                if g == 2:
                    ac.wait_ge(a_ld, 80)
                    s.activation(w1_16[:, 0, :, :], wst1[:, :, :], ACT.Copy, scale=WSC).then_inc(a_w, 1)
                if g + 1 < NG:
                    ffn_high(g + 1)
                ffn_relu(g)

            ac.wait_ge(s_var, 3)
            s.activation(rstd_t[:, 1, :], rstd_t[:, 0, :], ACT.Sqrt).then_inc(s_sqrt, 1)

            def high1(b, par):
                ac.wait_ge(a_xt, b + 1)
                s.activation(x116[:, par, 0, :, :], bank[par][:, 0:KD * N].rearrange("p (k n) -> p k n", k=KD), ACT.Copy).then_inc(a_xh, 1)

            def copy_raw(b, par, first):
                ac.wait_ge(a_qf, b + 1)
                ac.wait_ge(a_kf, b + 1)
                if not first:
                    ac.wait_ge(a_red, b - 1)
                for w, ps in ((0, bank[2 + par][:, 0:D]), (1, bank[4 + par][:, 0:D])):
                    if w:
                        ac.wait_ge(a_v, 2 * b + 2)
                    s.activation(sq[:, par, w, :], ps, ACT.Square, scale=1.0 / WSC)
                    ins = s.activation(raw[:, bass.ds(b, 1), w, :], ps.unsqueeze(1), ACT.Copy, scale=1.0 / WSC)
                ins.then_inc(a_raw, 1)

            def ctx_high1(b, par, first):
                ac.wait_ge(a_cf[par], (b - par) * 8 + 16)
                if not first:
                    ac.wait_ge(a_kf, b - 1)
                s.activation(c116[:, par, 0, :, :], c1f[:, par, :, :], ACT.Copy).then_inc(a_ch, 1)

            def stage1(b, par, first=False, has_next=True):
                if has_next:
                    ctx_high1(b + 1, 1 - par, first)
                    high1(b + 1, 1 - par)
                copy_raw(b, par, first or has_next == 2)

            ctx_high1(0, 0, True)
            high1(0, 0)
            stage1(0, 0, True)
            stage1(1, 1, False, 2)
            with ac.Fori(1, B // 2 - 1) as i:
                for par in range(2):
                    stage1(i * 2 + par, par)
            stage1(B - 2, 0)
            stage1(B - 1, 1, False, False)
            ac.wait_ge(a_ms, 1)
            s.activation(ms[:, 1, :, :], ms[:, 0, :, :], ACT.Sqrt).then_inc(a_sq, 1)

            def seg_high(b, par, first):
                ac.wait_ge(a_gn, b + 1)
                if not first:
                    ac.wait_ge(a_tq, b - 1)
                    ac.wait_ge(a_tk, b - 1)
                for w in range(2):
                    src = qn[:, par, w, :].rearrange("p (h d) -> p h d", h=H)
                    dst = seg[:, par, w, :, 0:2, :] if w == 0 else seg[:, par, w, :, 0:3:2, :]
                    ins = s.activation(dst, src.unsqueeze(2).to_broadcast([P, H, 2, HD]), ACT.Copy)
                ins.then_inc(a_sh, 1)

            def copy_q(b, par):
                ac.wait_ge(a_tq, b + 1)
                s.activation(qT1[:, par, 0, :, :].rearrange("p c n -> p (c n)"), bank[2][:, :].bitcast(F16), ACT.Copy).then_inc(a_cq, 1)

            def take_o1(c, first):
                ac.wait_ge(a_ot, c + 1)
                if not first:
                    ac.wait_ge(a_op, c)
                s.activation(OT1[:, :, :], bank[4][:, 0:KD * N].rearrange("p (k n) -> p k n", k=KD), ACT.Copy).then_inc(a_oc, 1)

            def exps1(b, first):
                for g in range(NHG):
                    ac.wait_ge(a_st, 4 * b + g + 1)
                    if not first:
                        ac.wait_ge(a_pl, 4 * b - 3 + g)
                    s.activation(P1[:, HS * g:HS * g + HS, :], bank[g % 2][:, :].rearrange("p (h n) -> p h n", h=HS), ACT.Exp,
                                 scale=HD ** -0.5).then_inc(a_ex, 1)

            seg_high(0, 0, True)
            seg_high(1, 1, True)
            copy_q(0, 0)

            def probs_high1(b, first):
                for g in range(NHG):
                    ac.wait_ge(a_ex, 4 * b + g + 1)
                    if g == 0 and not first:
                        ac.wait_ge(a_pv, b)
                    s.activation(P116[:, 0, HS * g:HS * g + HS, :], P1[:, HS * g:HS * g + HS, :], ACT.Copy).then_inc(a_ph, 1)

            def weights_high(h, par, q, first=False):
                if q == 0:
                    ac.wait_ge(w_ld[par], (h - par) * 8 + 16)
                    if not first:
                        ac.wait_ge(w_st[par], (h - par) * 8)
                c0, c1 = q * HC // NSP, (q + 1) * HC // NSP
                s.activation(ws16[:, par, 0, c0:c1], ws[:, par, c0:c1], ACT.Copy).then_inc(w_hi, 1)

            def iteration1(b, par, c, has_q, has_x):
                if c > 1:
                    take_o1(b - 2, c == 2)
                if has_q:
                    copy_q(b + 1, 1 - par)
                exps1(b, c == 0)
                if has_x:
                    seg_high(b + 2, par, False)
                probs_high1(b, c == 0)
                if not has_q:
                    take_o1(b - 1, False)
                for q in range(NSP):
                    weights_high(b, par, q, c < 2)

            iteration1(0, 0, 0, True, True)
            iteration1(1, 1, 1, True, True)
            iteration1(2, 0, 2, True, True)
            iteration1(3, 1, 3, True, True)
            with ac.Fori(2, B // 2 - 1) as i:
                for par in range(2):
                    iteration1(i * 2 + par, par, 3, True, True)
            iteration1(B - 2, 0, 3, True, False)
            iteration1(B - 1, 1, 3, False, False)
            take_o1(B - 1, False)

            ac.wait_ge(s_var, 4)
            s.activation(rstd_t[:, 1, :], rstd_t[:, 0, :], ACT.Sqrt).then_inc(s_sqrt, 1)

            def turned_m(b, par, first):
                ac.wait_ge(m_xn, b + 1)
                s.activation(xm16[:, bass.ds(b, 1), 0, :], xnm[:, par:par + 1, :], ACT.Copy).then_inc(m_xh, 1)
                ac.wait_ge(m_xt, b + 1)
                if not first:
                    ac.wait_ge(m_lg, b - 1)
                s.activation(xTm[:, par, :, :], bank[par][:, 0:KD * N].rearrange("p (k n) -> p k n", k=KD), ACT.Copy).then_inc(m_xc, 1)

            turned_m(0, 0, True)
            turned_m(1, 1, True)
            with ac.Fori(1, B // 2) as i:
                for par in range(2):
                    turned_m(i * 2 + par, par, False)
            ac.wait_ge(m_ex, 1)
            s.activation(ex[:, :, :], ex[:, :, :], ACT.Exp).then_inc(m_er, 1)
            ac.wait_ge(m_er, 1)
            s.activation(early_gelu[:, :], ex[:, 0, 0:1], ACT.Gelu)

            def expert_a(t, par, first):
                ac.wait_ge(m_w[par], (t - par) * 16 + 32)
                for c in range(FC):
                    ac.wait_ge(m_h, FC * t + c + 1)
                    if not (first and c < 4):
                        ac.wait_ge(m_u, FC * t + c - 3)
                    s.activation(yg[:, c % 4, :], bank[c % 4][:, 0:MT], ACT.Gelu, bias=bms[:, par, c:c + 1]).then_inc(m_g, 1)
                    if c % 2 == 0 and c:
                        hidden_high(t, par, c // 2 - 1)
                hidden_high(t, par, 3)

            def hidden_high(t, par, q):
                ac.wait_ge(m_u, FC * t + 2 * q + 2)
                s.activation(hm16[:, par, 0, 2 * q:2 * q + 2, :], hf[:, q % 2, :, :], ACT.Copy).then_inc(m_hh, 1)

            expert_a(0, 0, True)
            expert_a(1, 1, False)
            expert_a(2, 0, False)
            with ac.Fori(0, (NT - 5) // 2) as i:
                for q in range(2):
                    expert_a(i * 2 + 3 + q, 1 - q, False)
            expert_a(NT - 2, 1, False)
            expert_a(NT - 1, 0, False)

        @block.tensor
        def _(pe):
            t = nc.tensor

            def turn_xn(b, c):
                pe.wait_ge(s_xn, b + 1)
                if c is None:
                    if b:
                        pe.wait_ge(s_xh, b)
                        pe.wait_ge(s_xl, b)
                else:
                    pe.wait_ge(s_oc, c)
                for kk in range(KD):
                    ins = t.transpose(bank[6][:, kk * N:(kk + 1) * N], xn[:, kk * P:(kk + 1) * P], ident[:, :])
                ins.then_inc(s_xt, 1)

            PAIRS = [(0, 0), (0, 1), (1, 0)]

            def project_qk(b, par, rs, first=False):
                pe.wait_ge(s_xh, b + 1)
                pe.wait_ge(s_xl, b + 1)
                for r in rs:
                    w = r // 2
                    src = (xn16, ctx16)[w]
                    if r == 2:
                        pe.wait_ge(s_ch, b + 1)
                        pe.wait_ge(s_cl, b + 1)
                    if first and b:
                        pe.wait_ge(s_qe, 6 * (b - 1) + r + 1 + (4 if r < 2 else 0))
                    elif not first:
                        pe.wait_ge(s_pm, 8 * b + 2 * r - 14)
                    for c in range(HS):
                        col = (HS * (r % 2) + c) * P
                        n = 0
                        for (wp, xp) in PAIRS:
                            for kk in range(KD):
                                ins = t.matmul(bank[2 + r][:, c * N:(c + 1) * N], wqkv16[:, w, wp, kk, col:col + P],
                                               src[:, par, xp, kk, :], start=(n == 0), stop=(n == 5))
                                n += 1
                    ins.then_inc(s_qf, 1)

            def project_v(b, par, rs):
                for r in rs:
                    pe.wait_ge(s_qe, 6 * b + r + 1)
                    n = 0
                    for (wp, xp) in PAIRS:
                        for kk in range(KD):
                            ins = t.matmul(bank[2 + r][:, :], ctx16[:, par, xp, kk, :], wqkv16[:, 2, wp, kk, 512 * r:512 * r + 512],
                                           start=(n == 0), stop=(n == 5))
                            n += 1
                    ins.then_inc(s_qf, 1)

            def row_scores(b, par, gs, first):
                pe.wait_ge(s_qh, 4 * b + 4)
                for g in gs:
                    if g < 2:
                        if not first:
                            pe.wait_ge(s_exp, 4 * b - 4 + 3 + g)
                    else:
                        pe.wait_ge(s_red, 4 * b + g - 1)
                    half = 64 * (g % 2)
                    for i in range(HS):
                        ch = HS * (g // 2) + i
                        ins = t.matmul(bank[g % 2][:, i * N:(i + 1) * N], q16[half:half + 64, par, 0, 0, ch, :],
                                       q16[half:half + 64, par, 1, 0, ch, :], start=True, stop=True)
                    ins.then_inc(s_sm, 1)

            def scores(b, par, g):
                if g < 2:
                    pe.wait_ge(s_red, 4 * b + 3 + g)
                else:
                    pe.wait_ge(s_exp, 4 * b + g - 1)
                if g == 0:
                    pe.wait_ge(s_red, 4 * b + 4)
                    pe.wait_ge(s_ql, 4 * b + 4)
                half = 64 * (g % 2)
                for i in range(HS):
                    ch = HS * (g // 2) + i
                    o = bank[g % 2][:, i * N:(i + 1) * N]
                    sl = HS * g + i
                    t.matmul(o, nmx[:, sl:sl + 1].to_broadcast([P, N]), ident16[:, :], start=True, stop=False)
                    for n, (qp, kp) in enumerate(PAIRS):
                        ins = t.matmul(o, q16[half:half + 64, par, 1, kp, ch, :], q16[half:half + 64, par, 0, qp, ch, :],
                                       start=False, stop=(n == 2))
                ins.then_inc(s_st, 1)

            def gate(b, par, g, first, grp, has_q):
                if g == 0:
                    pe.wait_ge(s_flo, b + 1)
                    if first:
                        pe.wait_ge(s_whv, 3)
                        pe.wait_ge(s_pp, 3 + 5 * NJ)
                n = b + 1 if has_q else b
                pe.wait_ge(s_qe, 6 * n + g + 1 + (4 if g < 2 else 0))
                if not first:
                    pe.wait_ge(s_pm, 8 * b - 8 + 2 * g + 2)
                bk = bank[2 + g]
                for n, (lp, rp) in enumerate(PAIRS):
                    t.matmul(bk[:, :], Rm16[:, bass.ds(b, 1), rp, :], Lw16[:, grp, lp, 2 * g:2 * g + 2, :], start=(n == 0), stop=(n == 2))
                for jj in range(2):
                    j = 2 * g + jj
                    for n, (wp, fp) in enumerate(PAIRS):
                        ins = t.matmul(bk[:, jj * 256:(jj + 1) * 256], F16s[:, par, fp, j * N:(j + 1) * N], We16[:, wp, :], start=False,
                                       stop=(n == 2), skip_group_check=True)
                ins.then_inc(s_gf, 1)

            def pv(c, par, first):
                pe.wait_ge(s_pl, 4 * c + 4)
                pe.wait_ge(s_vl, 2 * c + 2)
                for f in range(4):
                    if f == 0:
                        pe.wait_ge(s_xh, xl_of(c))
                        pe.wait_ge(s_xl, xl_of(c))
                    elif f == 1:
                        if not first:
                            pe.wait_ge(s_opt, c)
                    else:
                        pe.wait_ge(s_oe, 4 * c + f - 1)
                    for i in range(HS):
                        sl = HS * f + i
                        for n, (pp, vp) in enumerate(PAIRS):
                            ins = t.matmul(bank[6 + f % 2][:, i * (DK + 1):(i + 1) * (DK + 1)], PT16[:, pp, sl, :], vv16[:, par, vp, sl, :],
                                           start=(n == 0), stop=(n == 2))
                    ins.then_inc(s_of, 1)

            def xl_of(c):
                return xl_cap[0] if xl_cap[0] else c + 3

            xl_cap = [0]

            def turn_o(c):
                for r in range(2):
                    pe.wait_ge(s_oe, 4 * c + 3 + r)
                    for i in range(4):
                        ch = 4 * r + i
                        ins = t.transpose(bank[6 + r][:, i * N:(i + 1) * N], O[:, ch * P:(ch + 1) * P], ident[:, :])
                    ins.then_inc(s_ot, 1)

            def project_o(c):
                pe.wait_ge(s_oc, 2 * c + 2)
                for ch in range(CH):
                    ins = t.matmul(bank[7][:, 0:D], OT[:, ch, :], WoT[:, ch, :], start=(ch == 0), stop=(ch == CH - 1))
                ins.then_inc(s_op, 1)

            pe.wait_ge(s_pp, 3)
            turn_xn(0, None)
            turn_xn(1, None)
            pe.wait_ge(s_wlo, 2)
            project_qk(0, 0, range(4), True)
            pe.wait_ge(s_wlo, 3)
            project_v(0, 0, (0, 1))

            def iteration(b, par, c, has_q, has_x, grp):
                row_scores(b, par, (0, 1), c == 0)
                if has_q:
                    project_qk(b + 1, 1 - par, (0, 1), c == 0)
                row_scores(b, par, (2, 3), c == 0)
                if has_q:
                    project_qk(b + 1, 1 - par, (2, 3), c == 0)
                if c:
                    pv(b - 1, 1 - par, c == 1)
                if has_q:
                    project_v(b + 1, 1 - par, (0,))
                if c:
                    turn_o(b - 1)
                if has_q:
                    project_v(b + 1, 1 - par, (1,))
                if has_x:
                    turn_xn(b + 2, (None if c == 0 else 2 * b - 1))
                if c:
                    project_o(b - 1)
                for g in range(4):
                    scores(b, par, g)
                    if g < 2:
                        gate(b, par, g, c == 0, grp, has_q)
                gate(b, par, 2, c == 0, grp, has_q)
                gate(b, par, 3, c == 0, grp, has_q)

            iteration(0, 0, 0, True, True, 0)
            iteration(1, 1, 1, True, True, 0)
            pe.wait_ge(s_whv, 4)
            with pe.Fori(0, 3) as i:
                for par in range(2):
                    iteration(i * 2 + 2 + par, par, 2, True, True, 0)
            pe.wait_ge(s_pp, 3 + 2 * 5 * NJ)
            with pe.Fori(0, 3) as i:
                for par in range(2):
                    iteration(i * 2 + 8 + par, par, 2, True, True, 1)
            iteration(B - 2, 0, 2, True, False, 1)
            xl_cap[0] = B
            iteration(B - 1, 1, 2, False, False, 1)
            pv(B - 1, 1, False)
            turn_o(B - 1)
            project_o(B - 1)

            pe.wait_ge(f_ld, 64)
            pe.wait_ge(s_qe, 6 * B)
            pe.wait_ge(s_opt, B)
            t.matmul(bank[4][0:RANK, 0:D], lowr[:, FF:FF + RANK], lowr[:, FF + RANK:], start=True, stop=True).then_inc(f_mp, 1)
            pe.wait_ge(f_m, 1)
            for r in range(FC // 2):
                for i in range(2):
                    c = 2 * r + i
                    ins = t.matmul(bank[r][:, i * D:(i + 1) * D], lowr[:, c * P:(c + 1) * P], lowm, start=True, stop=True)
                ins.then_inc(f_lp, 1)
            for r in range(4):
                kk, fh = r // 2, r % 2
                pe.wait_ge(f_low, FC // 2)
                for i in range(4):
                    c = 4 * fh + i
                    ins = t.transpose(bank[r][:, i * P:(i + 1) * P], wfa[:, c, kk * P:(kk + 1) * P], ident[:, :])
                ins.then_inc(f_tp, 1)
            for r in range(4):
                pe.wait_ge(f_lo, r + 1)
                for i in range(4):
                    c, kk = 2 * r + i // 2, i % 2
                    ins = t.transpose(bank[r][:, i * P:(i + 1) * P], wpa[:, kk, c * P:(c + 1) * P], ident[:, :])
                ins.then_inc(f_tp, 1)
            for kk in range(KD):
                ins = t.matmul(bank[4][:, kk * P:(kk + 1) * P], thr[:, 0, FC + kk:FC + kk + 1].to_broadcast([P, P]), ident[:, :],
                               start=True, stop=True)
            ins.then_inc(f_mp, 1)
            pe.wait_ge(f_m, 2)
            pe.wait_ge(f_hi, 8)

            def ffn_turn(g):
                pe.wait_ge(f_xn, GT * (g + 1))
                for kk in range(KD):
                    if g:
                        pe.wait_ge(f_xl, 2 * g - 1 + kk)
                    for i in range(GT):
                        ins = t.transpose(bank[4 + kk][:, i * N:(i + 1) * N], xng[:, g % 2, i, kk * P:(kk + 1) * P], ident[:, :])
                    ins.then_inc(f_xt, 1)

            def ffn_hidden(g):
                pe.wait_ge(f_xh, 2 * g + 2)
                pe.wait_ge(f_xl, 2 * g + 2)
                for c in range(FC):
                    n = g * FC + c
                    if n > 3:
                        pe.wait_ge(f_r, n - 3)
                    m = 0
                    for (wp, xp) in PAIRS:
                        for kk in range(KD):
                            ins = t.matmul(bank[n % 4][:, :], W1T16[:, wp, kk, c * P:(c + 1) * P], xg16[:, g % 2, xp, kk, :],
                                           start=(m == 0), stop=(m == 5))
                            m += 1
                    ins.then_inc(f_h, 1)

            def ffn_out(g):
                pe.wait_ge(f_l, FC * (g + 1))
                for i in range(GT):
                    n = g * GT + i
                    if n > 1:
                        pe.wait_ge(f_ot, n - 1)
                    for m in range(2 * FC):
                        ins = t.matmul(bank[6 + n % 2][:, 0:D], h216[:, g % 2, m // FC, m % FC, i * N:(i + 1) * N], W2T16[:, m % FC, :],
                                       start=(m == 0), stop=(m == 2 * FC - 1))
                    ins.then_inc(f_o, 1)

            ffn_turn(0)
            for g in range(NG):
                if g + 1 < NG:
                    ffn_turn(g + 1)
                ffn_hidden(g)
                if g:
                    ffn_out(g - 1)
            ffn_out(NG - 1)

            pe.wait_ge(a_w, 1)
            pe.wait_ge(a_wl, 1)

            def turn1(b, par, first):
                pe.wait_ge(a_xn, b + 1)
                if not first:
                    pe.wait_ge(a_xh, b - 1)
                    pe.wait_ge(a_xl, b - 1)
                for kk in range(KD):
                    ins = t.transpose(bank[par][:, kk * N:(kk + 1) * N], xn1[:, par, kk * P:(kk + 1) * P], ident[:, :])
                ins.then_inc(a_xt, 1)

            def project1(b, par, first):
                pe.wait_ge(a_xh, b + 1)
                pe.wait_ge(a_xl, b + 1)
                if not first:
                    pe.wait_ge(a_raw, b - 1)
                    pe.wait_ge(a_v, 2 * b - 2)
                for src, bk, c0, c1, done in ((x116, bank[2 + par], 0, D, a_qf), (c116, bank[4 + par], D, 3 * D, a_kf)):
                    if done is a_kf:
                        pe.wait_ge(a_ch, b + 1)
                        pe.wait_ge(a_cl, b + 1)
                    n = 0
                    for (wp, xp) in PAIRS:
                        for kk in range(KD):
                            ins = t.matmul(bk[:, 0:c1 - c0], src[:, par, xp, kk, :], w1_16[:, wp, kk, c0:c1], start=(n == 0), stop=(n == 5))
                            n += 1
                    ins.then_inc(done, 1)

            turn1(0, 0, True)
            turn1(1, 1, True)
            project1(0, 0, True)
            turn1(2, 0, False)
            project1(1, 1, True)
            turn1(3, 1, False)
            with pe.Fori(1, B // 2 - 1) as i:
                for par in range(2):
                    project1(i * 2 + par, par, False)
                    turn1(i * 2 + 2 + par, par, False)
            project1(B - 2, 0, False)
            project1(B - 1, 1, False)

            def turn_qk1(b, par, first):
                for w, ready, done in ((0, a_cq, a_tq), (1, a_ck, a_tk)):
                    if w == 0:
                        pe.wait_ge(a_sh, b + 1)
                        pe.wait_ge(a_sl, b + 1)
                    if not first:
                        pe.wait_ge(ready, b)
                    bk = bank[2 + w][:, :].bitcast(F16)
                    for c in range(CH):
                        ins = t.transpose(bk[:, c * N:(c + 1) * N], seg[:, par, w, 2 * c:2 * c + 2, :, :].rearrange("p h s d -> p (h s d)"), ident16[:, :])
                    ins.then_inc(done, 1)

            def row_scores1(b, par, first):
                pe.wait_ge(a_cq, b + 1)
                pe.wait_ge(a_ck, b + 1)
                for g in range(NHG):
                    if g < 2:
                        if not first:
                            pe.wait_ge(a_ex, 4 * b - 1 + g)
                    else:
                        pe.wait_ge(a_mx, 4 * b + g - 1)
                    half = 64 * (g % 2)
                    for i in range(HS):
                        ch = HS * (g // 2) + i
                        ins = t.matmul(bank[g % 2][:, i * N:(i + 1) * N], qT1[half:half + 64, par, 0, ch, :],
                                       qT1[half:half + 64, par, 1, ch, :], start=True, stop=True)
                    ins.then_inc(a_sm, 1)

            def scores1(b, par):
                for g in range(NHG):
                    if g < 2:
                        pe.wait_ge(a_mx, 4 * b + 3 + g)
                    else:
                        pe.wait_ge(a_ex, 4 * b + g - 1)
                    half = 64 * (g % 2)
                    for i in range(HS):
                        ch = HS * (g // 2) + i
                        sl = HS * g + i
                        o = bank[g % 2][:, i * N:(i + 1) * N]
                        t.matmul(o, nmx1[:, sl:sl + 1].to_broadcast([P, N]), ident16[:, :], start=True, stop=False)
                        ins = t.matmul(o, qT1[half:half + 64, par, 1, ch, :], qT1[half:half + 64, par, 0, ch, :], start=False, stop=True)
                    ins.then_inc(a_st, 1)

            def pv1(c, par, first):
                pe.wait_ge(a_v, 2 * B + c + 1)
                pe.wait_ge(a_ph, 4 * c + 4)
                pe.wait_ge(a_pl, 4 * c + 4)
                if not first:
                    pe.wait_ge(a_o, c)
                for sl in range(H):
                    h = HEAD_OF[sl]
                    for n, (pp, vp) in enumerate(PAIRS):
                        ins = t.matmul(bank[6][:, h * (HD + 1):(h + 1) * (HD + 1)], P116[:, pp, sl, :],
                                       vb1[:, par, vp, h * (HD + 1):(h + 1) * (HD + 1)], start=(n == 0), stop=(n == 2))
                ins.then_inc(a_pv, 1)

            def turn_o1(c, first):
                pe.wait_ge(a_o, c + 1)
                if not first:
                    pe.wait_ge(a_oc, c)
                for kk in range(KD):
                    ins = t.transpose(bank[4][:, kk * N:(kk + 1) * N], O1[:, kk * P:(kk + 1) * P], ident[:, :])
                ins.then_inc(a_ot, 1)

            def project_o1(c, first):
                pe.wait_ge(a_oc, c + 1)
                if not first:
                    pe.wait_ge(a_xu, c)
                for kk in range(KD):
                    ins = t.matmul(bank[5][:, 0:D], OT1[:, kk, :], wpr[:, kk, :], start=(kk == 0), stop=(kk == KD - 1))
                ins.then_inc(a_op, 1)

            pe.wait_ge(a_raw, B)
            pe.wait_ge(a_v, 2 * B)
            turn_qk1(0, 0, True)

            def iteration1(b, par, c, has_q):
                row_scores1(b, par, c == 0)
                if c > 1:
                    turn_o1(b - 2, c == 2)
                if has_q:
                    turn_qk1(b + 1, 1 - par, False)
                if c > 1:
                    project_o1(b - 2, c == 2)
                scores1(b, par)
                if c:
                    pv1(b - 1, 1 - par, c == 1)

            iteration1(0, 0, 0, True)
            iteration1(1, 1, 1, True)
            iteration1(2, 0, 2, True)
            iteration1(3, 1, 3, True)
            with pe.Fori(2, B // 2 - 1) as i:
                for par in range(2):
                    iteration1(i * 2 + par, par, 3, True)
            iteration1(B - 2, 0, 3, True)
            iteration1(B - 1, 1, 3, False)
            turn_o1(B - 2, False)
            project_o1(B - 2, False)
            pv1(B - 1, 1, False)
            turn_o1(B - 1, False)
            project_o1(B - 1, False)

            pe.wait_ge(m_ld, 16)

            def turn_m(b, par, first):
                pe.wait_ge(m_xn, b + 1)
                if not first:
                    pe.wait_ge(m_xc, b - 1)
                for kk in range(KD):
                    ins = t.transpose(bank[par][:, kk * N:(kk + 1) * N], xnm[:, par, kk * P:(kk + 1) * P], ident[:, :])
                ins.then_inc(m_xt, 1)

            def logits(b, par):
                pe.wait_ge(m_xc, b + 1)
                for kk in range(KD):
                    ins = t.matmul(bank[7][:, bass.ds(b * E, E)], xTm[:, par, kk, :], rwt[:, kk, :], start=(kk == 0), stop=(kk == KD - 1))
                ins.then_inc(m_lg, 1)

            turn_m(0, 0, True)
            turn_m(1, 1, True)
            with pe.Fori(0, B // 2 - 1) as i:
                for par in range(2):
                    logits(i * 2 + par, par)
                    turn_m(i * 2 + 2 + par, par, False)
            logits(B - 2, 0)
            logits(B - 1, 1)
            pe.wait_ge(m_ex, 2)
            pe.wait_ge(m_c, 6)
            t.matmul(bank[6][:, 0:256], tri[:, :], oh16[:, :], start=True, stop=True)
            t.matmul(bank[6][:, 256:512], one16[:, :], oh16[:, :], start=True, stop=True).then_inc(m_pr, 1)

            def turn_tokens(t_, par, first):
                pe.wait_ge(m_x[par], (t_ - par) * 8 + 16)
                if not first:
                    pe.wait_ge(m_tc, t_)
                bk = bank[4][:, :].bitcast(F16)
                for a4 in range(2 * KD):
                    for h in range(MT // P):
                        ins = t.transpose(bk[:, a4 * MT + h * P:a4 * MT + (h + 1) * P], xin[:, par, h, a4 * P:(a4 + 1) * P], ident16[:, :])
                ins.then_inc(m_tt, 1)

            def hidden(t_, par, c0, c1, first):
                for c in range(c0, c1):
                    if c == 0:
                        pe.wait_ge(m_tc, t_ + 1)
                        pe.wait_ge(m_w[par], (t_ - par) * 16 + 32)
                    if not (first and c < 4):
                        pe.wait_ge(m_u, FC * t_ + c - 3)
                    for w in range(2):
                        n = 0
                        for (wp, xp) in PAIRS:
                            for kk in range(KD):
                                col = (w * KD + kk) * FF + c * P
                                ins = t.matmul(bank[c % 4][:, w * MT:(w + 1) * MT], wm16[:, par, wp, col:col + P], xT16[:, par, xp * KD + kk, :],
                                               start=(n == 0), stop=(n == 5))
                                n += 1
                    ins.then_inc(m_h, 1)

            def expert_out(t_, par, first):
                pe.wait_ge(m_hl, 4 * t_ + 4)
                pe.wait_ge(m_wd[par], (t_ - par) * 16 + 32)
                if not first:
                    pe.wait_ge(m_y, t_ - 1)
                for h in range(MT // P):
                    n = 0
                    for (wp, xp) in PAIRS:
                        for c in range(FC):
                            col = 2 * KD * FF + c * D
                            ins = t.matmul(bank[5 + par][:, h * D:(h + 1) * D], hm16[:, par, xp, c, h * P:(h + 1) * P], wm16[:, par, wp, col:col + D],
                                           start=(n == 0), stop=(n == 3 * FC - 1))
                            n += 1
                ins.then_inc(m_o, 1)

            def expert_p(t_, par, prev, nxt, first=False):
                hidden(t_, par, 0, 2, first)
                if prev:
                    expert_out(t_ - 1, 1 - par, prev == 1)
                if nxt:
                    turn_tokens(t_ + 1, 1 - par, False)
                hidden(t_, par, 2, 8, first)

            turn_tokens(0, 0, True)
            expert_p(0, 0, 0, True, True)
            expert_p(1, 1, 1, True)
            expert_p(2, 0, 1, True)
            with pe.Fori(0, (NT - 5) // 2) as i:
                for q in range(2):
                    expert_p(i * 2 + 3 + q, 1 - q, 2, True)
            expert_p(NT - 2, 1, 2, True)
            expert_p(NT - 1, 0, 2, False)
            expert_out(NT - 1, 0, False)


def arrange(inputs):
    f = lambda n: np.asarray(inputs[n], np.float32)
    c = np.ascontiguousarray
    boxes = f("fside_BxSx4_0")
    heads = np.array(HEAD_OF)
    cols = (heads[:, None] * DK + np.arange(DK)[None, :]).reshape(-1)
    a = {"x": f("x"), "g_xattn": f("g_xattn"), "g_ffn": f("g_ffn")}
    a["ctxT"] = c(f("ctx_1024").reshape(T, D).T)
    lohi = boxes.reshape(B, NJ, NN, 2, 2)
    bn = lohi.transpose(4, 2, 0, 1, 3)
    a["boxn"] = c(np.broadcast_to(bn[:, None], (2, 4, NN, B, NJ, 2)).reshape(P, B * NJ, 2))
    a["boxm"] = c(boxes.reshape(T, 2, 2).transpose(2, 1, 0))
    delta = np.array([(s >> 1) & 1 if s < 8 else 0 for s in range(SLOTS)])
    wh = boxes.reshape(2, 8, N, 2, 2)[..., delta]
    a["whc"] = c(wh.transpose(1, 4, 0, 3, 2).reshape(P, 2, 2, N))
    Wg = f("L0_xattn_Wg")[heads]
    feat = lambda sc, dl, fr: Wg[:, sc * 8 + dl * 2 + fr]
    We = np.zeros((2, 2, 2, NN, H, NN), np.float32)
    for xy in range(2):
        for sc in range(2):
            for fr in range(2):
                for nn in range(NN):
                    We[xy, sc, fr, nn, :, nn] = feat(sc, xy, fr)
    a["We"] = We.reshape(P, H * NN)
    AB = np.zeros((SLOTS, 2, H), np.float32)
    for s in range(4):
        dl, fr = 2 + (s >> 1), s & 1
        AB[s, 0], AB[s, 1] = feat(1, dl, fr), feat(0, dl, fr)
        AB[4 + s, 0], AB[4 + s, 1] = feat(0, dl, fr), feat(1, dl, fr)
    AB[8, 1] = f("L0_xattn_bg")[heads]
    a["AB"] = c(np.broadcast_to(AB[None], (8, SLOTS, 2, H)).reshape(P, 2, H))
    turn = [100.0 / (1000.0 ** (fr / 2)) / (2 * np.pi) for fr in range(2)]
    cst = np.zeros((P, 8), np.float32)
    for p in range(P):
        sc, fr = (p >> 5) & 1, (p >> 4) & 1
        cst[p, 0], cst[p, 1] = turn[fr], 0.25 * sc
        s = p % SLOTS
        cst[p, 2] = turn[s & 1] if s < 8 else 0.0
        cst[p, 3], cst[p, 4], cst[p, 5] = 0.0, (-0.25 if s < 4 else 0.25), (0.0 if s < 4 else 0.25)
    a["cst"] = cst
    a["mask"] = c((np.arange(P)[:, None] // SLOTS == np.arange(8)[None, :]).astype(np.float32))
    a["wqkv"] = np.stack([f("L0_xattn_Wq").T, f("L0_xattn_Wk").T, f("L0_xattn_Wv")[cols].T])
    a["bqk"] = c(np.stack([f("L0_xattn_bq").reshape(CH, P).T, f("L0_xattn_bk").reshape(CH, P).T], 1))
    a["bv"] = c(f("L0_xattn_bv")[cols])
    a["woT"] = c(f("L0_xattn_Wo")[:, cols].T)
    a["bo"] = f("L0_xattn_bo")
    a["w_fc"], a["w_proj"] = f("L0_ffn_w_fc"), f("L0_ffn_w_proj")
    a["low"] = c(np.concatenate([f("L0_ffn_u").T, f("L0_ffn_fast_b").T, f("L0_ffn_v")], 1))
    a["wq1"], a["wkv1"], a["wpr1"] = f("L1_xattn_Wq"), f("L1_xattn_Wkv"), f("L1_xattn_Wproj")
    a["gq"], a["gk"] = np.tile(f("L1_xattn_q_gamma"), H), np.tile(f("L1_xattn_k_gamma"), H)
    a["rwt"] = c(f("L1_ffn_router_w").T)
    turned = lambda n: f(n).transpose(0, 2, 1).reshape(E, KD, P, FF).transpose(0, 2, 1, 3).reshape(E, P, KD * FF)
    down = f("L1_ffn_w2_w").transpose(0, 2, 1).reshape(E, FC, P, D).transpose(0, 2, 1, 3).reshape(E, P, FC * D)
    bias = lambda n: f(n).reshape(E, FC, P).transpose(0, 2, 1)
    a["wcat"] = c(np.concatenate([turned("L1_ffn_wg_w"), turned("L1_ffn_w1_w"), down, bias("L1_ffn_wg_b"), bias("L1_ffn_w1_b")], 2))
    a["b2"] = f("L1_ffn_w2_b")
    a["fgate"] = f("L0_ffn_gate").reshape(1)
    return a


def kernel(**inputs):
    import concourse.bacc as bacc
    from concourse.bass_utils import run_bass_kernel_spmd

    nc = bacc.Bacc("TRN2", target_bir_lowering=False, num_devices=1)
    arrays = {f"in_{n}": np.ascontiguousarray(v) for n, v in arrange(inputs).items()}
    aps = {n[3:]: nc.dram_tensor(n, v.shape, mybir.dt.from_np(v.dtype), kind="ExternalInput").ap() for n, v in arrays.items()}
    aps["out"] = nc.dram_tensor("out_x", (B, N, D), F32, kind="ExternalOutput").ap()
    build(nc, aps)
    r = run_bass_kernel_spmd(nc, [arrays], core_ids=[0])
    return r.results[0]["out_x"]
```
